# Optimizing a Trainium2 kernel written in Bass

```python
import numpy as np
import jax
import jax.numpy as jnp

def _softmax(x, axis=-1):
    return jax.nn.softmax(x, axis=axis)

def _gelu(x):
    return jax.nn.gelu(x, approximate=True)

def _silu(x):
    return jax.nn.silu(x)

def _sigmoid(x):
    return jax.nn.sigmoid(x)

def _layernorm(x, axis=-1, eps=1e-05):
    m = jnp.mean(x, axis=axis, keepdims=True)
    v = jnp.var(x, axis=axis, keepdims=True)
    return (x - m) / jnp.sqrt(v + eps)

def _scatter_add(tgt, idx, src, axis=0):
    return tgt.at[idx].add(src)

def _segment_sum(src, seg, n):
    return jax.ops.segment_sum(src, seg, n)
kernel_name = 'mk_gnn_ffn_d1_gnn_r32_9a3ad0'

def setup_inputs(seed: int=0):
    np.random.seed(seed)
    _w = jnp.asarray

    def _rec_inputs():
        import jax
        import jax.numpy as jnp
        _gk = jax.random.key(seed)
        x = -0.0002117 + 1 * jax.random.normal(jax.random.fold_in(_gk, 1), (10000, 512), jnp.float32)
        src = jax.random.randint(jax.random.fold_in(_gk, 2), (10000,), 0, 10000, jnp.int32)
        dst = jax.random.randint(jax.random.fold_in(_gk, 3), (10000,), 0, 10000, jnp.int32)
        _o = jnp.argsort(dst, stable=True)
        src = src[_o]
        dst = dst[_o]
        return (x, src, dst)
    x, src, dst = _rec_inputs()

    def _L0_gnn_setup():
        import jax, jax.numpy as jnp
        import numpy as np
        N, E, H, D_IN, D_PRIME = (50000, 25000, 8, 512, 64)

        def _segment_softmax(scores, seg, num_segments):
            smax = jax.ops.segment_max(scores, seg, num_segments=num_segments)
            ex = jnp.exp(scores - smax[seg])
            denom = jax.ops.segment_sum(ex, seg, num_segments=num_segments)
            return ex / denom[seg]
        key = jax.random.key(seed)
        ks = jax.random.split(key, 6)
        x = jax.random.normal(ks[0], (N, D_IN), dtype=jnp.float32)
        edge_index = jax.random.randint(ks[1], (2, E), 0, N)
        Ws = jax.random.normal(ks[2], (H, D_IN, D_PRIME), dtype=jnp.float32) * 0.05
        Wb = jax.random.normal(ks[3], (H, D_PRIME), dtype=jnp.float32) * 0.05
        a_w = jax.random.normal(ks[4], (H, 2 * D_PRIME), dtype=jnp.float32) * 0.05
        a_b = jax.random.normal(ks[5], (H,), dtype=jnp.float32) * 0.05
        return dict(x=x, edge_index=edge_index, Ws=Ws, Wb=Wb, a_w=a_w, a_b=a_b)
    _L0_gnn_all = _L0_gnn_setup()
    _L0_gnn_in = {k: v for k, v in _L0_gnn_all.items() if k in ('Ws', 'Wb', 'a_w', 'a_b')}
    del _L0_gnn_all

    def _L0_ffn_setup():
        import jax, jax.numpy as jnp
        import numpy as np
        EPS = 1e-05

        def _bitlinear(x, w):
            w_scale = jnp.clip(jnp.mean(jnp.abs(w)), EPS, None)
            w_q = jnp.clip(jnp.round(w / w_scale), -1.0, 1.0) * w_scale
            w_eff = w + jax.lax.stop_gradient(w_q - w)
            x_scale = 127.0 / jnp.clip(jnp.max(jnp.abs(x), axis=-1, keepdims=True), EPS, None)
            x_q = jnp.clip(jnp.round(x * x_scale), -128.0, 127.0) / x_scale
            x_eff = x + jax.lax.stop_gradient(x_q - x)
            return jnp.einsum('bsi,oi->bso', x_eff, w_eff)

        def _ste_round_clamp_int8(h):
            h_q = jnp.clip(jnp.round(h), -128.0, 127.0)
            return h + jax.lax.stop_gradient(h_q - h)
        key = jax.random.key(seed)
        k1, k2, k3 = jax.random.split(key, 3)
        B, S, D, F = (8, 256, 512, 64)
        x = jax.random.normal(k1, (B, S, D), dtype=jnp.float32)
        w_up = jax.random.normal(k2, (F, D), dtype=jnp.float32) * (1.0 / np.sqrt(D))
        w_down = jax.random.normal(k3, (D, F), dtype=jnp.float32) * (1.0 / np.sqrt(F))
        return {'x': x, 'w_up': w_up, 'w_down': w_down}
    _L0_ffn_all = _L0_ffn_setup()
    _L0_ffn_in = {k: v for k, v in _L0_ffn_all.items() if k in ('w_up', 'w_down')}
    del _L0_ffn_all
    return {'x': x, 'src': src, 'dst': dst, 'L0_gnn_Ws': _L0_gnn_in['Ws'], 'L0_gnn_Wb': _L0_gnn_in['Wb'], 'L0_gnn_a_w': _L0_gnn_in['a_w'], 'L0_gnn_a_b': _L0_gnn_in['a_b'], 'L0_ffn_w_up': _L0_ffn_in['w_up'], 'L0_ffn_w_down': _L0_ffn_in['w_down']}

def reference(x, src, dst, L0_gnn_Ws, L0_gnn_Wb, L0_gnn_a_w, L0_gnn_a_b, L0_ffn_w_up, L0_ffn_w_down):
    import jax
    import jax.numpy as jnp

    def _L0_gnn_ref(x, edge_index, Ws, Wb, a_w, a_b):
        import jax, jax.numpy as jnp
        import numpy as np
        N, E, H, D_IN, D_PRIME = (50000, 25000, 8, 512, 64)

        def _segment_softmax(scores, seg, num_segments):
            smax = jax.ops.segment_max(scores, seg, num_segments=num_segments)
            ex = jnp.exp(scores - smax[seg])
            denom = jax.ops.segment_sum(ex, seg, num_segments=num_segments)
            return ex / denom[seg]
        v_src, v_tgt = (edge_index[0], edge_index[1])
        n = x.shape[0]
        outs = []
        for h in range(Ws.shape[0]):
            Wx = x @ Ws[h] + Wb[h]
            d = Wx.shape[-1]
            s = Wx[v_tgt] @ a_w[h, :d] + Wx[v_src] @ a_w[h, d:] + a_b[h]
            s = jax.nn.leaky_relu(s, negative_slope=0.2)
            alpha = _segment_softmax(s, v_tgt, n)
            outs.append(jax.ops.segment_sum(alpha[:, None] * Wx[v_src], v_tgt, num_segments=n))
        return jnp.stack(outs, axis=1).reshape(n, -1)

    def _L0_ffn_ref(x, w_up, w_down):
        import jax, jax.numpy as jnp
        import numpy as np
        EPS = 1e-05

        def _bitlinear(x, w):
            w_scale = jnp.clip(jnp.mean(jnp.abs(w)), EPS, None)
            w_q = jnp.clip(jnp.round(w / w_scale), -1.0, 1.0) * w_scale
            w_eff = w + jax.lax.stop_gradient(w_q - w)
            x_scale = 127.0 / jnp.clip(jnp.max(jnp.abs(x), axis=-1, keepdims=True), EPS, None)
            x_q = jnp.clip(jnp.round(x * x_scale), -128.0, 127.0) / x_scale
            x_eff = x + jax.lax.stop_gradient(x_q - x)
            return jnp.einsum('bsi,oi->bso', x_eff, w_eff)

        def _ste_round_clamp_int8(h):
            h_q = jnp.clip(jnp.round(h), -128.0, 127.0)
            return h + jax.lax.stop_gradient(h_q - h)
        h = _bitlinear(x, w_up)
        h = jax.nn.relu(h)
        h = _ste_round_clamp_int8(h)
        return _bitlinear(h, w_down)
    edge_index = jnp.stack([src, dst])
    x = x + _L0_gnn_ref(_layernorm(x, axis=-1), edge_index, L0_gnn_Ws, L0_gnn_Wb, L0_gnn_a_w, L0_gnn_a_b)
    x = x + _L0_ffn_ref(_layernorm(x, axis=-1)[None], L0_ffn_w_up, L0_ffn_w_down)[0]
    return x

_drawn_inputs = setup_inputs


def setup_inputs(seed=0):
    import zlib

    import numpy as np

    out = dict(_drawn_inputs(seed))
    spreads = {}
    factors = {'L0_gnn_a_b': 5.637}
    for name, (base, spread) in spreads.items():
        noise = np.random.default_rng([zlib.crc32(name.encode()), seed]).standard_normal(out[name].shape)
        drawn = base * np.exp(spread * noise) if base else spread * noise
        out[name] = jnp.asarray(drawn.astype(out[name].dtype))
    for name, factor in factors.items():
        out[name] = (out[name] * factor).astype(out[name].dtype)
    return out
```

```python
from contextlib import ExitStack

import concourse.bass as bass
from concourse import mybir

ALU = mybir.AluOpType
ACT = mybir.ActivationFunctionType
AX = mybir.AxisListType
F32 = mybir.dt.float32
BF16 = mybir.dt.bfloat16
I32 = mybir.dt.int32

P = 128
BIG = 1.0e30
FAR = 20000
MAGIC = 1.5 * 2.0 ** 23
LN_EPS = 1e-5
Q_EPS = 1e-5
QMAX = 127.0


def wait(eng, sem, value):
    if isinstance(value, int) and value <= 0:
        return
    eng.wait_ge(sem, value)


class Chain:

    def __init__(self, eng, sem):
        self.eng, self.sem, self.base, self.n = eng, sem, 0, 0

    def mark(self, ins):
        ins.then_inc(self.sem, 1)
        self.n += 1

    def link(self, ins):
        self.mark(ins)
        self.join()

    def join(self):
        self.eng.wait_ge(self.sem, self.base + self.n)

    def enter(self, turn, per):
        self.start, self.per = self.base + self.n, per
        self.base, self.n = turn * per + self.start, 0

    def leave(self, turns):
        assert self.n == self.per, f"a turn of the loop marks {self.n} results, not {self.per}"
        self.base, self.n = self.start + turns * self.per, 0


def build(nc, x, src, dst, Ws, Wb, a_w, a_b, w_up, w_down, out):
    N, D = x.shape
    H, _, DH = Ws.shape
    F = w_up.shape[0]
    E = src.shape[0]
    C = D // P
    ET = 80
    EP = E // ET
    GR = 4
    NG = ET // GR
    FULL = N // P
    TAIL0 = N - P
    TN = N - FULL * P
    NT = FULL + 1
    RW = D + 2 * H
    SW = H + 2
    NB, SLOTS = 2, 3
    U = NB * SLOTS
    assert EP * ET == E and H * DH == D and FULL % U == 0 and C * P == D

    rows = nc.dram_tensor("edge_rows", (P * ET, RW), F32, kind="Internal").ap()
    dst_table = nc.dram_tensor("dst_table", (N, H), F32, kind="Internal").ap()
    src_table = nc.dram_tensor("src_table", (N, SW), F32, kind="Internal").ap()
    last_edge = nc.dram_tensor("last_edge", (N, 1), I32, kind="Internal").ap()

    with ExitStack() as ctx:
        def sb(name, shape, dt=F32):
            return ctx.enter_context(nc.sbuf_tensor(name, shape, dt))

        def sem(name):
            return ctx.enter_context(nc.semaphore(name))

        bank = [ctx.enter_context(nc.psum_tensor(f"bank{i}", [P, 512], F32)) for i in range(8)]
        xt_ps = bank[0:2]
        proj_ps = bank[2:4]
        sc_ps = bank[4:6]
        misc_ps = bank[6:8]

        identF = sb("identF", [P, P])
        identB = sb("identB", [P, P], BF16)
        shift = sb("shift", [P, P])
        before = sb("before", [P, P])
        inv_d = sb("inv_d", [P, P])
        epsT = sb("epsT", [P, 1])
        magicP = sb("magicP", [P, 1])
        magicN = sb("magicN", [P, 1])
        minus_half = sb("minus_half", [P, 1])
        onesB = sb("onesB", [P, P], BF16)

        Wsb = sb("Wsb", [P, C, H, DH])
        awb = sb("awb", [P, H, 2 * DH])
        wbb = sb("wbb", [P, D])
        abb = sb("abb", [P, H])
        prod = sb("prod", [P, C, H, DH])
        wts = sb("wts", [P, C, 2 * H])
        const_s = sb("const_s", [P, H])
        bpart = sb("bpart", [3, 3, D], BF16)
        brest = sb("brest", [3, D])
        brow = sb("brow", [3, D], BF16)

        dst_i = sb("dst_i", [P, ET], I32)
        nxt_i = sb("nxt_i", [P, ET], I32)
        prv_i = sb("prv_i", [P, 1], I32)
        src_i = sb("src_i", [P, ET], I32)
        dst_g = sb("dst_g", [P, ET], I32)
        dst_f = sb("dst_f", [P, ET])
        same_next = sb("same_next", [P, ET])
        edge_no = sb("edge_no", [P, ET], I32)
        scat = sb("scat", [P, ET, 2], I32)
        gcol = sb("gcol", [P, ET])
        gates = sb("gates", [P, NG, H, GR + 1])
        headeq = sb("headeq", [P, ET])
        headcnt = sb("headcnt", [P, 1])
        fx = sb("fx", [P, 8])
        fix_idx = sb("fix_idx", [P, 1], I32)
        far_i = sb("far_i", [P, FULL], I32)
        scat_ring = sb("scat_ring", [P, 2, GR, 2], I32)
        idx_ring = sb("idx_ring", [P, 2, 2, GR], I32)
        last_sb = sb("last_sb", [P, NT], I32)
        last_ring = sb("last_ring", [P, U], I32)

        x_in = sb("x_in", [P, U, D])
        xT = sb("xT", [P, 2, D])
        bn_all = sb("bn_all", [P, NT, 6])
        raw_s = sb("raw_s", [P, NT, 2 * H])
        meanT = sb("meanT", [P, NT])
        varT = sb("varT", [P, NT])
        difT = sb("difT", [P, NT])
        rstdT = sb("rstdT", [P, NT])
        dst_tab = sb("dst_tab", [P, NT, H])
        src_tab = sb("src_tab", [P, NT, SW])

        xg = sb("xg", [P, 2, GR, D])
        sdst = sb("sdst", [P, 2, GR, H])
        ssrc = sb("ssrc", [P, 2, GR, SW])
        xn = sb("xn", [P, 2, D])
        score = sb("score", [P, 2, H, GR + 1])
        mrun = sb("mrun", [P, 2, H, GR + 1])
        expin = sb("expin", [P, 2, 2, H, GR])
        wc = sb("wc", [P, 2, 2, H, GR + 1])
        den = sb("den", [P, 2, H, GR + 1])
        vbuf = sb("vbuf", [P, 2, D])
        row = sb("row", [P, 2, GR, RW])

        mB = sb("mB", [P, H, P])
        dB = sb("dB", [P, 2, P])
        egate = sb("egate", [P, P])
        cmask = sb("cmask", [P, P])
        gm = sb("gm", [P, H])
        wq_in = sb("wq_in", [P, H])
        wq = sb("wq", [P, H])
        tailrow = sb("tailrow", [P, D + H])
        fixrow = sb("fixrow", [P, RW])
        mtot = sb("mtot", [P, H])
        ab_in = sb("ab_in", [P, 2, H])
        ab = sb("ab", [P, 2, H])
        cden = sb("cden", [P, H])

        up_sb = sb("up_sb", [F, D])
        dn_sb = sb("dn_sb", [P, C, F])
        asum = sb("asum", [P, 2])
        wsc = sb("wsc", [P, 2])
        whalf = sb("whalf", [P, 2, 2])
        qsc = sb("qsc", [P, 2])
        tern = sb("tern", [P, D], BF16)
        up_t = sb("up_t", [F, D], BF16)
        dn_t = sb("dn_t", [P, C, F], BF16)
        upT = sb("upT", [P, C, F], BF16)
        dnT = sb("dnT", [F, D], BF16)

        rg = sb("rg", [P, U, RW])
        rden = sb("rden", [P, U, H])
        ybuf = sb("ybuf", [P, U, D])
        obuf = sb("obuf", [P, U, D])
        bn6 = sb("bn6", [P, U, 6])
        mv = sb("mv", [P, U, 2])
        negm = sb("negm", [P, U])
        std = sb("std", [P, U])
        yc = sb("yc", [P, 2, D])
        qm = sb("qm", [P, 2, D])
        qT = sb("qT", [P, 2, D], BF16)
        qs = sb("qs", [P, U, 8])
        hid = sb("hid", [P, 3, F])
        hq = sb("hq", [P, 2, P])
        hqT = sb("hqT", [F, 2, P], BF16)

        w_in = sem("w_in")
        ffw_in = sem("ffw_in")
        idx_in = sem("idx_in")
        pads_set = sem("pads_set")
        consts_set = sem("consts_set")
        far_out = sem("far_out")
        x_got1 = [sem(f"x_got1_{i}") for i in range(SLOTS)]
        tables_out = sem("tables_out")
        last_in = sem("last_in")
        dve_chain = sem("dve_chain")
        pool_chain = sem("pool_chain")
        pool_gate = sem("pool_gate")
        act_chain = sem("act_chain")
        scat_done = [sem(f"scat_done{i}") for i in range(2)]
        scat_ready = sem("scat_ready")
        wsum_ready = sem("wsum_ready")
        wmean_ready = sem("wmean_ready")
        wts_ready = sem("wts_ready")
        xt_ready = sem("xt_ready")
        xt_copied = sem("xt_copied")
        st_done = sem("st_done")
        st_copied = sem("st_copied")
        stats_done = sem("stats_done")
        var_ready = sem("var_ready")
        rstd_ready = sem("rstd_ready")
        tables_ready = sem("tables_ready")
        x_got2 = [sem(f"x_got2_{i}") for i in range(2)]
        small_got = [sem(f"small_got{i}") for i in range(2)]
        normed = sem("normed")
        scored = sem("scored")
        exped = sem("exped")
        mm_done = sem("mm_done")
        v_done = sem("v_done")
        group_done = sem("group_done")
        rows_out = [sem(f"rows_out{i}") for i in range(2)]
        aux_ready = sem("aux_ready")
        aux_done = sem("aux_done")
        cross_in = sem("cross_in")
        cross_exp = sem("cross_exp")
        fix_got = sem("fix_got")
        fix_ready = sem("fix_ready")
        fix_out = sem("fix_out")
        x_got4 = [sem(f"x_got4_{i}") for i in range(SLOTS)]
        rg_got = [sem(f"rg_got{i}") for i in range(U)]
        rden_ready = sem("rden_ready")
        agg_ready = sem("agg_ready")
        y_ready = sem("y_ready")
        yc_ready = sem("yc_ready")
        qs_ready = sem("qs_ready")
        qm_ready = sem("qm_ready")
        qt_ready = sem("qt_ready")
        qt_copied = sem("qt_copied")
        up_done = sem("up_done")
        h_ready = sem("h_ready")
        ht_ready = sem("ht_ready")
        ht_copied = sem("ht_copied")
        dn_done = sem("dn_done")
        o_ready = sem("o_ready")
        o_out = [sem(f"o_out{i}") for i in range(SLOTS)]
        tail_out = sem("tail_out")

        x_main = x[0:FULL * P, :].rearrange("(p j) d -> p j d", j=FULL)
        out_main = out[0:FULL * P, :].rearrange("(p j) d -> p j d", j=FULL)
        rows_v = rows.rearrange("(p t) w -> p t w", t=ET)
        block = ctx.enter_context(nc.Block())

        def heads(ap):
            return ap.rearrange("p (h d) -> p h d", h=H)

        def over(ap, n):
            return ap.unsqueeze(2).to_broadcast([P, H, n])

        @block.sync
        def _(sp):
            for c in range(C):
                sp.dma_start(Wsb[:, c, :, :], Ws[:, c * P:(c + 1) * P, :].rearrange("h k d -> k h d")).then_inc(w_in, 16)
            sp.dma_start(awb[:].rearrange("p h d -> p (h d)"), a_w.rearrange("h d -> (h d)").partition_broadcast(P)).then_inc(w_in, 16)
            sp.dma_start(wbb[:], Wb.rearrange("h d -> (h d)").partition_broadcast(P)).then_inc(w_in, 16)
            sp.dma_start(abb[:], a_b.partition_broadcast(P)).then_inc(w_in, 16)

            def load1(k, slot):
                sp.dma_start(x_in[:, NB * slot:NB * slot + NB, :], x_main[:, bass.ds(NB * k, NB), :]).then_inc(x_got1[slot], 16)

            for k in range(SLOTS):
                load1(k, k)
            with sp.Fori(1, FULL // U) as i:
                for slot in range(SLOTS):
                    k = SLOTS * i + slot
                    sp.wait_ge(xt_ready, NB * k - U + NB)
                    sp.wait_ge(stats_done, NB * k - U + NB)
                    load1(k, slot)
            sp.wait_ge(xt_ready, FULL - U + NB)
            sp.wait_ge(stats_done, FULL - U + NB)
            sp.dma_start(x_in[:, 0, :], x[TAIL0:N, :]).then_inc(x_got1[0], 16)

            sp.wait_ge(tables_ready, 1)
            for tab, sbt in ((dst_table, dst_tab), (src_table, src_tab)):
                sp.dma_start(tab[0:FULL * P, :].rearrange("(p j) w -> p j w", j=FULL), sbt[:, 0:FULL, :]).then_inc(tables_out, 16)
                sp.dma_start(tab[FULL * P:N, :], sbt[P - TN:P, FULL, :]).then_inc(tables_out, 16)
            for r in range(2):
                sp.wait_ge(scat_done[r], 16 * ET // 2)
            sp.dma_start(last_sb[:, 0:FULL], last_edge[0:FULL * P, :].rearrange("(p j) o -> p (j o)", j=FULL)).then_inc(last_in, 16)
            sp.dma_start(last_sb[:, FULL:NT], last_edge[TAIL0:N, :]).then_inc(last_in, 16)

            with sp.Fori(0, NG // 2) as i:
                for b in range(2):
                    sp.wait_ge(group_done, 2 * i + b + 1)
                    sp.dma_start(rows_v[:, bass.ds((2 * i + b) * GR, GR), :], row[:, b, :, :]).then_inc(rows_out[b], 16)

            def load4(k, slot):
                sp.dma_start(x_in[:, NB * slot:NB * slot + NB, :], x_main[:, bass.ds(NB * k, NB), :]).then_inc(x_got4[slot], 16)

            def store4(k, slot):
                sp.wait_ge(o_ready, NB * k + NB)
                sp.dma_start(out_main[:, bass.ds(NB * k, NB), :], obuf[:, NB * slot:NB * slot + NB, :]).then_inc(o_out[slot], 16)

            for k in range(SLOTS):
                load4(k, k)
            with sp.Fori(1, FULL // U) as i:
                for slot in range(SLOTS):
                    k = SLOTS * i + slot
                    sp.wait_ge(y_ready, NB * k - U + NB)
                    load4(k, slot)
                    store4(k - SLOTS, slot)
            sp.wait_ge(y_ready, FULL - U + NB)
            sp.dma_start(x_in[:, 0, :], x[TAIL0:N, :]).then_inc(x_got4[0], 16)
            for slot in range(SLOTS):
                store4(FULL // NB - SLOTS + slot, slot)
            sp.wait_ge(o_ready, NT)
            sp.dma_start(out[FULL * P:N, :], obuf[P - TN:P, 0, :]).then_inc(tail_out, 16)
            for slot in range(SLOTS):
                sp.wait_ge(o_out[slot], 16 * (FULL // U))
            sp.wait_ge(tail_out, 16)

        @block.gpsimd
        def _(gp):
            ch = Chain(gp, pool_chain)
            lim_nodes = gp.to_reg(N - 1)
            lim_rows = gp.to_reg(P * ET - 1)
            gp.memset(dst_i[:], FAR).then_inc(pads_set, 1)
            gp.memset(nxt_i[:], FAR + 1).then_inc(pads_set, 1)
            gp.memset(prv_i[:], -1).then_inc(pads_set, 1)
            gp.memset(src_i[:], 0).then_inc(pads_set, 1)
            gp.memset(far_i[:], FAR).then_inc(pads_set, 1)
            gp.iota(edge_no[:], [[1, ET]], base=0, channel_multiplier=ET).then_inc(consts_set, 1)
            ch.mark(gp.memset(identF[:], 0.0))
            ch.mark(gp.memset(shift[:], 0.0))
            ch.link(gp.memset(before[:], 1.0))
            gp.affine_select(out=identF[:], in_=identF[:], compare_op=ALU.not_equal, fill=1.0, base=0,
                             pattern=[[-1, P]], channel_multiplier=1).then_inc(consts_set, 1)
            gp.affine_select(out=shift[:], in_=shift[:], compare_op=ALU.not_equal, fill=1.0, base=-1,
                             pattern=[[1, P]], channel_multiplier=-1).then_inc(consts_set, 1)
            gp.affine_select(out=before[:], in_=before[:], compare_op=ALU.is_gt, fill=0.0, base=0,
                             pattern=[[1, P]], channel_multiplier=-1).then_inc(consts_set, 1)
            gp.memset(minus_half[:], -0.5).then_inc(consts_set, 1)

            gp.wait_ge(scat_ready, 1)
            gp.wait_ge(far_out, 32)
            def scatter_turn(i):
                for r in range(2):
                    if isinstance(i, int):
                        col = slice(i * 2 * GR + r * GR, i * 2 * GR + r * GR + GR)
                    else:
                        col = bass.ds(gp.snap(i * 2 * GR + r * GR), GR)
                    wait(gp, scat_done[r], i * (16 * GR))
                    ch.link(gp.tensor_copy(scat_ring[:, r, :, :], scat[:, col, :]))
                    gp.sem_inc(pool_gate, 1)
                    for k in range(GR):
                        gp.indirect_dma_start(last_edge, bass.IndirectOffsetOnAxis(ap=scat_ring[:, r, k, 0:1], axis=0),
                                              scat_ring[:, r, k, 1:2], None,
                                              bounds_check=lim_nodes, oob_is_err=False).then_inc(scat_done[r], 16)

            scatter_turn(0)
            with gp.Fori(1, ET // (2 * GR)) as i:
                ch.enter(i - 1, 2)
                scatter_turn(i)
            ch.leave(ET // (2 * GR) - 1)

            def take_indices(G, b):
                if isinstance(G, int):
                    col = slice(G * GR, G * GR + GR)
                else:
                    col = bass.ds(gp.snap(G * GR), GR)
                ch.mark(gp.tensor_copy(idx_ring[:, b, 0, :], dst_g[:, col]))
                ch.link(gp.tensor_copy(idx_ring[:, b, 1, :], src_i[:, col]))
                gp.sem_inc(pool_gate, 1)

            def gather_x(b):
                for r in range(GR):
                    gp.indirect_dma_start(xg[:, b, r, :], None, x, bass.IndirectOffsetOnAxis(ap=idx_ring[:, b, 1, r:r + 1], axis=0),
                                          bounds_check=lim_nodes, oob_is_err=False).then_inc(x_got2[b], 16)

            def gather_small(b):
                for r in range(GR):
                    gp.indirect_dma_start(sdst[:, b, r, :], None, dst_table, bass.IndirectOffsetOnAxis(ap=idx_ring[:, b, 0, r:r + 1], axis=0),
                                          bounds_check=lim_nodes, oob_is_err=False).then_inc(small_got[b], 16)
                    gp.indirect_dma_start(ssrc[:, b, r, :], None, src_table, bass.IndirectOffsetOnAxis(ap=idx_ring[:, b, 1, r:r + 1], axis=0),
                                          bounds_check=lim_nodes, oob_is_err=False).then_inc(small_got[b], 16)

            for b in range(2):
                take_indices(b, b)
                gather_x(b)
            gp.wait_ge(var_ready, 1)
            gp.tensor_tensor(rstdT[:], varT[:], minus_half[:].to_broadcast([P, NT]), ALU.pow).then_inc(rstd_ready, 1)
            gp.wait_ge(tables_out, 64)
            gp.sem_inc(pool_gate, 1)
            for b in range(2):
                gather_small(b)
            with gp.Fori(1, NG // 2) as i:
                ch.enter(i - 1, 4)
                for b in range(2):
                    G = 2 * i + b
                    gp.wait_ge(scored, G - 1)
                    gp.wait_ge(normed, (G - 1) * GR)
                    take_indices(G, b)
                    gather_small(b)
                    gather_x(b)
            ch.leave(NG // 2 - 1)

            ch.link(gp.memset(fixrow[:], 0.0))
            gp.wait_ge(rows_out[0], 16 * (NG // 2))
            gp.wait_ge(rows_out[1], 16 * (NG // 2))
            gp.sem_inc(pool_gate, 1)
            gp.indirect_dma_start(fixrow[:], None, rows, bass.IndirectOffsetOnAxis(ap=fix_idx[:], axis=0),
                                  bounds_check=lim_rows, oob_is_err=False).then_inc(fix_got, 16)
            gp.wait_ge(fix_ready, 1)
            gp.sem_inc(pool_gate, 1)
            gp.indirect_dma_start(rows, bass.IndirectOffsetOnAxis(ap=fix_idx[:], axis=0), fixrow[:], None,
                                  bounds_check=lim_rows, oob_is_err=False).then_inc(fix_out, 16)
            gp.wait_ge(last_in, 32)
            gp.wait_ge(fix_out, 16)

            def fetch(t, u):
                if isinstance(t, int):
                    col = slice(t, t + 1)
                else:
                    col = bass.ds(gp.snap(t), 1)
                wait(gp, y_ready, t - U + 1)
                ch.mark(gp.tensor_copy(last_ring[:, u:u + 1], last_sb[:, col]))
                ch.link(gp.memset(rg[:, u, :], 0.0))
                gp.sem_inc(pool_gate, 1)
                gp.indirect_dma_start(rg[:, u, :], None, rows, bass.IndirectOffsetOnAxis(ap=last_ring[:, u:u + 1], axis=0),
                                      bounds_check=lim_rows, oob_is_err=False).then_inc(rg_got[u], 16)

            def divide(t, u):
                wait(gp, rden_ready, t + 1)
                a = heads(rg[:, u, 0:D])
                gp.tensor_tensor(a, a, over(rden[:, u, :], DH), ALU.mult).then_inc(agg_ready, 1)

            AHEAD = 3
            for t in range(AHEAD):
                fetch(t, t)

            def step(s, m):
                if not isinstance(s, int) or s + AHEAD < NT:
                    fetch(s + AHEAD, (m + AHEAD) % U)
                if not isinstance(s, int) or s < NT:
                    divide(s, m)

            for s in range(U):
                step(s, s % U)
            with gp.Fori(1, FULL // U - 1) as i:
                ch.enter(i - 1, 2 * U)
                for m in range(U):
                    step(U * i + m, m)
            ch.leave(FULL // U - 2)
            for s in range(FULL - U, NT):
                step(s, s % U)

        @block.scalar
        def _(act):
            act.wait_ge(pads_set, 5)
            dst2 = dst.rearrange("(p t) -> p t", t=ET)
            act.dma_start(dst_i[0:EP, :], dst2).then_inc(idx_in, 16)
            act.dma_start(src_i[0:EP, :], src.rearrange("(p t) -> p t", t=ET)).then_inc(idx_in, 16)
            act.dma_start(nxt_i[0:EP - 1, :], dst[1:1 + (EP - 1) * ET].rearrange("(p t) -> p t", t=ET)).then_inc(idx_in, 16)
            act.dma_start(nxt_i[EP - 1:EP, 0:ET - 1], dst[1 + (EP - 1) * ET:E].rearrange("(p t) -> p t", p=1)).then_inc(idx_in, 16)
            act.dma_start(prv_i[1:EP, :], dst2[0:EP - 1, ET - 1:ET], allow_slow_non_contiguous=True).then_inc(idx_in, 16)
            act.dma_start(last_edge[0:FULL * P, :].rearrange("(p j) o -> p (j o)", j=FULL), far_i[:]).then_inc(far_out, 16)
            act.dma_start(last_edge[FULL * P:N, :], far_i[0:TN, 0:1]).then_inc(far_out, 16)
            act.dma_start(up_sb[:], w_up).then_inc(ffw_in, 16)
            act.dma_start(dn_sb[:], w_down.rearrange("(c k) f -> k c f", k=P)).then_inc(ffw_in, 16)
            act.sem_inc(xt_copied, 2)

            def copy1(t, u):
                act.wait_ge(xt_ready, t + 1)
                wait(act, st_done, t - 1)
                act.activation(xT[:, u, :], xt_ps[u][:], ACT.Copy).then_inc(xt_copied, 1)

            copy1(0, 0)
            copy1(1, 1)
            with act.Fori(1, FULL // 2) as i:
                copy1(2 * i, 0)
                copy1(2 * i + 1, 1)
            copy1(FULL, 0)

            def norm_tile(t, turn, b, r):
                act.wait_ge(x_got2[b], 16 * GR * turn + 16 * GR)
                act.wait_ge(small_got[b], 32 * GR * turn + 32 * GR)
                wait(act, xt_ready, NT + t - 1)
                act.activation(xn[:, r % 2, :], xg[:, b, r, :], ACT.Identity, bias=ssrc[:, b, r, H:H + 1],
                               scale=ssrc[:, b, r, H + 1:H + 2]).then_inc(normed, 1)

            def copy2(t, r):
                act.wait_ge(xt_ready, NT + t + 1)
                act.wait_ge(mm_done, t + 1)
                act.activation(xT[:, r % 2, :], xt_ps[r % 2][:], ACT.Copy).then_inc(xt_copied, 1)

            def exps(G, b):
                act.wait_ge(scored, G + 1)
                act.activation(wc[:, b, :, :, 1:GR + 1], expin[:, b, :, :, :], ACT.Exp).then_inc(exped, 1)

            act.wait_ge(st_done, NT)
            norm_tile(0, 0, 0, 0)
            exps(0, 0)

            def group(G, turn, b, last=False):
                for r in range(GR):
                    t = G * GR + r
                    copy2(t, r)
                    if r < GR - 1:
                        norm_tile(t + 1, turn, b, r + 1)
                    elif not last:
                        norm_tile(t + 1, turn + b, 1 - b, 0)
                    if r == 2 and not last:
                        exps(G + 1, 1 - b)

            with act.Fori(0, NG // 2 - 1) as i:
                group(2 * i, i, 0)
                group(2 * i + 1, i, 1)
            group(NG - 2, NG // 2 - 1, 0)
            group(NG - 1, NG // 2 - 1, 1, last=True)

            act.wait_ge(cross_in, 1)
            act.activation(wq[:], wq_in[:], ACT.Exp).then_inc(cross_exp, 1)
            act.wait_ge(cross_in, 2)
            act.activation(ab[:], ab_in[:], ACT.Exp).then_inc(cross_exp, 1)

            def step(s, m):
                def on(t):
                    return not isinstance(t, int) or 0 <= t < NT

                t, u = s - 5, (m - 5) % U
                if on(t):
                    act.wait_ge(ht_ready, t + 1)
                    wait(act, dn_done, t - 1)
                    act.activation(hqT[:, u % 2, :], misc_ps[u % 2][0:F, 0:P], ACT.Identity, bias=magicN[0:F, :]).then_inc(ht_copied, 1)
                t, u = s - 3, (m - 3) % U
                if on(t):
                    act.wait_ge(qt_ready, t + 1)
                    wait(act, up_done, t - 1)
                    act.activation(qT[:, u % 2, :], xt_ps[u % 2][:], ACT.Identity, bias=magicN[:]).then_inc(qt_copied, 1)
                t, u = s - 2, (m - 2) % U
                if on(t):
                    act.wait_ge(qs_ready, t + 1)
                    wait(act, qt_ready, t - 1)
                    act.activation(qm[:, u % 2, :], yc[:, u % 2, :], ACT.Identity, bias=magicP[:],
                                   scale=qs[:, u, 3:4]).then_inc(qm_ready, 1)
                t, u = s - 1, (m - 1) % U
                if on(t):
                    act.wait_ge(y_ready, t + 1)
                    act.activation(std[:, u:u + 1], mv[:, u, 1:2], ACT.Sqrt, bias=epsT[:])
                    wait(act, qm_ready, t - 1)
                    act.activation(yc[:, u % 2, :], ybuf[:, u, :], ACT.Identity, bias=negm[:, u:u + 1]).then_inc(yc_ready, 1)

            for s in range(2 * U):
                step(s, s % U)
            with act.Fori(2, FULL // U) as i:
                for m in range(U):
                    step(U * i + m, m)
            for s in range(FULL, NT + 5):
                step(s, s % U)

        @block.tensor
        def _(pe):
            pe.sem_inc(mm_done, 2)
            pe.wait_ge(wsum_ready, 1)
            for c in range(C):
                mm = pe.matmul(misc_ps[0][:, 0:2 * H], inv_d[:], wts[:, c, :], start=(c == 0), stop=(c == C - 1))
            mm.then_inc(wmean_ready, 1)
            pe.wait_ge(consts_set, 5)

            def turn1(t, u, slot_value):
                if slot_value is not None:
                    pe.wait_ge(x_got1[u // NB], slot_value)
                pe.wait_ge(xt_copied, t + 1)
                for c in range(C):
                    mm = pe.transpose(xt_ps[u % 2][:, c * P:(c + 1) * P], x_in[:, u, c * P:(c + 1) * P], identF[:])
                mm.then_inc(xt_ready, 1)

            def scores1(t, u):
                pe.wait_ge(xt_copied, t + 3)
                pe.wait_ge(st_copied, t + 1)
                for c in range(C):
                    mm = pe.matmul(sc_ps[u % 2][:, 0:2 * H], xT[:, u % 2, c * P:(c + 1) * P], wts[:, c, :],
                                   start=(c == 0), stop=(c == C - 1))
                mm.then_inc(st_done, 1)

            turn1(0, 0, 16)
            pe.wait_ge(wts_ready, 1)
            with pe.Fori(0, FULL // U) as i:
                for m in range(U):
                    t = U * i + m
                    nu = (m + 1) % U
                    turn1(t + 1, nu, (16 * i + 16 + (16 if nu == 0 else 0)) if nu % NB == 0 else None)
                    scores1(t, m)
            scores1(FULL, 0)

            pe.wait_ge(aux_ready, 1)
            for k in range(2):
                mm = pe.matmul(misc_ps[0][:, k * P:(k + 1) * P], dB[:, k, :], identF[:], start=True, stop=True)
            mm.then_inc(aux_done, 1)
            pe.matmul(misc_ps[1][:, 0:1], inv_d[0:F, :], asum[0:F, 0:1], start=True, stop=True)
            pe.matmul(misc_ps[1][:, 1:2], inv_d[:], asum[:, 1:2], start=True, stop=True).then_inc(aux_done, 1)

            def turn2(t, r):
                pe.wait_ge(normed, t + 1)
                pe.wait_ge(xt_copied, NT + t + 1)
                for c in range(C):
                    mm = pe.transpose(xt_ps[r % 2][:, c * P:(c + 1) * P], xn[:, r % 2, c * P:(c + 1) * P], identF[:])
                mm.then_inc(xt_ready, 1)

            def project(t, r):
                pe.wait_ge(xt_copied, NT + t + 3)
                pe.wait_ge(v_done, t + 1)
                ps = proj_ps[r % 2]
                for c in range(C):
                    pe.matmul(ps[:], xT[:, r % 2, c * P:(c + 1) * P], Wsb[:, c, :, :].rearrange("p h d -> p (h d)"),
                              start=(c == 0), stop=False)
                pe.matmul(ps[:], onesB[0:3, :], brow[:], start=False, stop=True).then_inc(mm_done, 1)

            turn2(0, 0)
            with pe.Fori(0, NG - 1) as i:
                for r in range(GR):
                    t = GR * i + r
                    turn2(t + 1, (r + 1) % GR)
                    project(t, r)
            for t in range(GR * (NG - 1), ET):
                if t + 1 < ET:
                    turn2(t + 1, (t + 1) % GR)
                project(t, t % GR)

            pe.wait_ge(aux_ready, 2)
            for c in range(C):
                pe.transpose(misc_ps[0][:].bitcast(BF16)[:, c * F:(c + 1) * F], up_t[:, c * P:(c + 1) * P], identB[0:F, 0:F])
            for c in range(C):
                mm = pe.transpose(misc_ps[1][:].bitcast(BF16)[0:F, c * P:(c + 1) * P], dn_t[:, c, :], identB[:])
            mm.then_inc(aux_done, 1)
            pe.wait_ge(aux_ready, 3)
            for h in range(H):
                mm = pe.matmul(proj_ps[h // 4][:, (h % 4) * P:(h % 4 + 1) * P], mB[:, h, :], identF[:], start=True, stop=True)
            mm.then_inc(aux_done, 1)
            pe.wait_ge(aux_ready, 4)
            pe.matmul(xt_ps[0][:], cmask[:], tailrow[:, 0:D], start=True, stop=True)
            pe.matmul(sc_ps[0][:, 0:H], cmask[:], tailrow[:, D:D + H], start=True, stop=True)
            pe.matmul(sc_ps[0][:, H:2 * H], shift[:], gm[:], start=True, stop=True).then_inc(aux_done, 1)
            pe.wait_ge(fix_ready, 1)

            def step(s, m):
                def on(t):
                    return not isinstance(t, int) or 0 <= t < NT

                t, u = s - 5, (m - 5) % U
                if on(t):
                    pe.wait_ge(ht_copied, t + 1)
                    wait(pe, o_ready, t - 1)
                    pe.matmul(proj_ps[u % 2][:], hqT[:, u % 2, :], dnT[:], start=True, stop=True).then_inc(dn_done, 1)
                t, u = s - 3, (m - 3) % U
                if on(t):
                    pe.wait_ge(qt_copied, t + 1)
                    wait(pe, h_ready, t - 1)
                    for c in range(C):
                        mm = pe.matmul(sc_ps[u % 2][:, 0:F], qT[:, u % 2, c * P:(c + 1) * P], upT[:, c, :],
                                       start=(c == 0), stop=(c == C - 1))
                    mm.then_inc(up_done, 1)
                t, u = s - 2, (m - 2) % U
                if on(t):
                    pe.wait_ge(qm_ready, t + 1)
                    wait(pe, qt_copied, t - 1)
                    for c in range(C):
                        mm = pe.transpose(xt_ps[u % 2][:, c * P:(c + 1) * P], qm[:, u % 2, c * P:(c + 1) * P], identF[:])
                    mm.then_inc(qt_ready, 1)
                t, u = s - 4, (m - 4) % U
                if on(t):
                    pe.wait_ge(h_ready, t + 1)
                    wait(pe, ht_copied, t - 1)
                    pe.transpose(misc_ps[u % 2][:, 0:P], hq[:, u % 2, :], identF[:]).then_inc(ht_ready, 1)

            for s in range(2 * U):
                step(s, s % U)
            with pe.Fori(2, FULL // U) as i:
                for m in range(U):
                    step(U * i + m, m)
            for s in range(FULL, NT + 5):
                step(s, s % U)

        @block.vector
        def _(ve):
            ch = Chain(ve, dve_chain)
            ve.sem_inc(v_done, 2)
            ve.sem_inc(st_copied, 2)
            ch.mark(ve.memset(inv_d[:], 1.0 / D))
            ve.memset(onesB[:], 1.0)
            ve.memset(epsT[:], LN_EPS)
            ve.memset(magicP[:], MAGIC)
            ve.memset(magicN[:], -MAGIC)
            ve.memset(mrun[:], 0.0)
            ve.memset(den[:], 0.0)
            ve.memset(wc[:], 0.0)
            ve.memset(hq[:], 0.0)
            ve.memset(row[:, 1, GR - 1, :], 0.0)
            ch.link(ve.memset(gates[:], -BIG))

            ve.wait_ge(idx_in, 16 * 5)
            ve.wait_ge(consts_set, 5)
            ch.mark(ve.tensor_copy(dst_f[:], dst_i[:]))
            ch.mark(ve.tensor_scalar(dst_g[:], dst_i[:], float(N - 1), None, ALU.min))
            ch.link(ve.tensor_tensor(same_next[:], dst_i[:], nxt_i[:], ALU.is_equal))
            ch.mark(ve.scalar_tensor_tensor(scat[:, :, 0], same_next[:], float(FAR), dst_f[:], ALU.mult, ALU.add))
            ve.tensor_copy(scat[:, :, 1], edge_no[:]).then_inc(scat_ready, 1)
            ch.mark(ve.tensor_copy(identB[:], identF[:]))

            ve.wait_ge(w_in, 16 * (C + 3))
            for half in range(2):
                a = awb[:, :, half * DH:(half + 1) * DH].unsqueeze(1).to_broadcast([P, C, H, DH])
                ch.link(ve.tensor_tensor(prod[:], Wsb[:], a, ALU.mult))
                ch.link(ve.tensor_reduce(wts[:, :, half * H:(half + 1) * H], prod[:], AX.X, ALU.add))
            ve.sem_inc(wsum_ready, 1)
            p0 = prod[:, 0, :, :]
            ch.link(ve.tensor_tensor(p0, awb[:, :, 0:DH], awb[:, :, DH:2 * DH], ALU.add))
            ch.link(ve.tensor_tensor(p0, p0, heads(wbb[:]), ALU.mult))
            ch.link(ve.tensor_reduce(const_s[:], p0, AX.X, ALU.add))
            ch.mark(ve.tensor_tensor(const_s[:], const_s[:], abb[:], ALU.add))
            ch.link(ve.tensor_copy(bpart[:, 0, :], wbb[0:3, :]))
            ch.link(ve.tensor_tensor(brest[:], wbb[0:3, :], bpart[:, 0, :], ALU.subtract))
            ch.link(ve.tensor_copy(bpart[:, 1, :], brest[:]))
            ch.link(ve.tensor_tensor(brest[:], brest[:], bpart[:, 1, :], ALU.subtract))
            ch.link(ve.tensor_copy(bpart[:, 2, :], brest[:]))
            ch.link(ve.tensor_scalar(brow[:], bpart[:, 0, :], identF[0:3, 0:1], None, ALU.mult))
            for k in (1, 2):
                ch.link(ve.scalar_tensor_tensor(brow[:], bpart[:, k, :], identF[0:3, k:k + 1], brow[:], ALU.mult, ALU.add))
            ve.wait_ge(wmean_ready, 1)
            ve.tensor_tensor(wts[:], wts[:], misc_ps[0][:, 0:2 * H].unsqueeze(1).to_broadcast([P, C, 2 * H]),
                             ALU.subtract).then_inc(wts_ready, 1)

            def stats1(t, u, slot_value):
                if slot_value is not None:
                    ve.wait_ge(x_got1[u // NB], slot_value)
                ve.bn_stats(bn_all[:, bass.ds(t, 1), :].rearrange("p o s -> p (o s)"), x_in[:, u, :]).then_inc(stats_done, 1)

            def keep1(t, u):
                ve.wait_ge(st_done, t + 1)
                ve.tensor_copy(raw_s[:, bass.ds(t, 1), :].rearrange("p o s -> p (o s)"), sc_ps[u % 2][:, 0:2 * H]).then_inc(st_copied, 1)

            stats1(0, 0, 16)
            with ve.Fori(0, FULL // U) as i:
                for m in range(U):
                    nu = (m + 1) % U
                    stats1(U * i + m + 1, nu, (16 * i + 16 + (16 if nu == 0 else 0)) if nu % NB == 0 else None)
                    keep1(U * i + m, m)
            keep1(FULL, 0)

            ve.wait_ge(stats_done, NT)
            ve.wait_ge(st_copied, NT + 2)
            ch.mark(ve.tensor_tensor(meanT[:], bn_all[:, :, 1], bn_all[:, :, 4], ALU.add))
            ch.mark(ve.tensor_tensor(difT[:], bn_all[:, :, 1], bn_all[:, :, 4], ALU.subtract))
            ch.link(ve.tensor_tensor(varT[:], bn_all[:, :, 2], bn_all[:, :, 5], ALU.add))
            ch.link(ve.scalar_tensor_tensor(difT[:], difT[:], 0.25, difT[:], ALU.mult, ALU.mult))
            ch.link(ve.scalar_tensor_tensor(varT[:], varT[:], 1.0 / D, difT[:], ALU.mult, ALU.add))
            ve.tensor_scalar(varT[:], varT[:], LN_EPS, None, ALU.add).then_inc(var_ready, 1)
            ve.wait_ge(rstd_ready, 1)
            rb = rstdT[:].unsqueeze(2).to_broadcast([P, NT, H])
            ch.mark(ve.scalar_tensor_tensor(src_tab[:, :, H], meanT[:], -0.5, rstdT[:], ALU.mult, ALU.mult))
            ch.mark(ve.tensor_copy(src_tab[:, :, H + 1], rstdT[:]))
            ch.mark(ve.tensor_tensor(src_tab[:, :, 0:H], raw_s[:, :, H:2 * H], rb, ALU.mult))
            ch.link(ve.tensor_tensor(dst_tab[:], raw_s[:, :, 0:H], rb, ALU.mult))
            ve.tensor_tensor(dst_tab[:], dst_tab[:], const_s[:].unsqueeze(1).to_broadcast([P, NT, H]),
                             ALU.add).then_inc(tables_ready, 1)

            ch.link(ve.memset(gcol[:, 0:1], -BIG))
            ch.link(ve.tensor_tensor(gcol[:, 1:ET], dst_f[:, 1:ET], dst_f[:, 0:ET - 1], ALU.is_equal))
            ch.link(ve.tensor_scalar(gcol[:, 1:ET], gcol[:, 1:ET], 1.0, BIG, ALU.subtract, ALU.mult))
            ch.link(ve.tensor_copy(gates[:, :, :, 1:GR + 1],
                                   gcol[:].rearrange("p (g s) -> p g s", s=GR).unsqueeze(2).to_broadcast([P, NG, H, GR])))
            first, last = dst_f[:, 0:1], dst_f[:, ET - 1:ET]
            ch.link(ve.tensor_scalar(headeq[:], dst_f[:], first, 0.0, ALU.is_equal, ALU.add, accum_out=headcnt[:]))
            ch.mark(ve.tensor_copy(fx[:, 0:1], edge_no[:, 0:1]))
            ch.mark(ve.tensor_tensor(fx[:, 1:2], prv_i[:], dst_i[:, 0:1], ALU.is_equal))
            ch.mark(ve.tensor_tensor(fx[:, 2:3], nxt_i[:, ET - 1:ET], dst_i[:, 0:1], ALU.not_equal))
            ch.link(ve.tensor_scalar(fx[:, 3:4], headcnt[:], ET - 0.5, None, ALU.is_lt))
            ch.link(ve.tensor_tensor(fx[:, 4:5], fx[:, 2:3], fx[:, 3:4], ALU.max))
            ch.link(ve.tensor_tensor(fx[:, 5:6], fx[:, 4:5], fx[:, 1:2], ALU.mult))
            ch.link(ve.tensor_scalar(fx[:, 5:6], fx[:, 5:6], 1.0, -float(FAR), ALU.subtract, ALU.mult))
            ch.link(ve.tensor_tensor(fx[:, 6:7], fx[:, 0:1], headcnt[:], ALU.add))
            ch.link(ve.scalar_tensor_tensor(fix_idx[:], fx[:, 6:7], 1.0, fx[:, 5:6], ALU.subtract, ALU.add))
            ch.mark(ve.tensor_copy(dB[:, 0, :], last.to_broadcast([P, P])))
            ch.mark(ve.tensor_copy(dB[:, 1, :], first.to_broadcast([P, P])))
            ve.wait_ge(ffw_in, 32)
            ch.mark(ve.tensor_reduce(asum[0:F, 0:1], up_sb[:], AX.X, ALU.add, apply_absolute_value=True))
            ch.link(ve.tensor_reduce(asum[:, 1:2], dn_sb[:].rearrange("p c f -> p (c f)"), AX.X, ALU.add, apply_absolute_value=True))
            ve.sem_inc(aux_ready, 1)
            ve.wait_ge(aux_done, 1)
            ch.link(ve.tensor_scalar(egate[:], misc_ps[0][:, 0:P], last, 1.0, ALU.is_equal, ALU.subtract))
            ch.mark(ve.tensor_scalar(egate[:], egate[:], BIG, None, ALU.mult))
            ch.mark(ve.scalar_tensor_tensor(cmask[:], misc_ps[0][:, P:2 * P], last, before[:], ALU.is_equal, ALU.mult))
            ve.wait_ge(aux_done, 2)
            ch.link(ve.tensor_scalar(wsc[:], misc_ps[1][:, 0:2], 1.0 / F, Q_EPS, ALU.mult, ALU.max))
            ch.mark(ve.tensor_scalar(whalf[:, 0, :], wsc[:], 0.5, None, ALU.mult))
            ch.mark(ve.tensor_scalar(qsc[:], wsc[:], 1.0 / QMAX, None, ALU.mult))
            ch.link(ve.tensor_scalar(whalf[:, 1, :], wsc[:], -0.5, None, ALU.mult))
            ch.link(ve.tensor_scalar(tern[0:F, :], up_sb[:], whalf[0:F, 1, 0:1], None, ALU.is_lt))
            ch.link(ve.scalar_tensor_tensor(up_t[:], up_sb[:], whalf[0:F, 0, 0:1], tern[0:F, :], ALU.is_gt, ALU.subtract))
            dn2, dt2 = dn_sb[:].rearrange("p c f -> p (c f)"), dn_t[:].rearrange("p c f -> p (c f)")
            ch.link(ve.tensor_scalar(tern[:, 0:C * F], dn2, whalf[:, 1, 1:2], None, ALU.is_lt))
            ch.link(ve.scalar_tensor_tensor(dt2, dn2, whalf[:, 0, 1:2], tern[:, 0:C * F], ALU.is_gt, ALU.subtract))
            ve.sem_inc(aux_ready, 1)

            def scores(G, turn, b):
                gate = gates[:, bass.ds(G, 1), :, :].rearrange("p o h s -> p (o h) s")
                s = score[:, b, :, 1:GR + 1]
                m = mrun[:, b, :, :]
                ve.wait_ge(small_got[b], 32 * GR * turn + 32 * GR)
                ch.mark(ve.tensor_copy(score[:, b, :, 0], mrun[:, 1 - b, :, GR]))
                ch.link(ve.tensor_tensor(s, sdst[:, b, :, :].rearrange("p s h -> p h s"),
                                         ssrc[:, b, :, 0:H].rearrange("p s h -> p h s"), ALU.add))
                ch.link(ve.scalar_tensor_tensor(s, s, 0.2, s, ALU.mult, ALU.max))
                ch.link(ve.tensor_tensor_scan(m.rearrange("p h s -> p (h s)"), gate.rearrange("p h s -> p (h s)"),
                                              score[:, b, :, :].rearrange("p h s -> p (h s)"), 0.0, ALU.add, ALU.max))
                ch.mark(ve.tensor_tensor(expin[:, b, 0, :, :], s, m[:, :, 1:GR + 1], ALU.subtract))
                ch.link(ve.tensor_tensor(expin[:, b, 1, :, :], m[:, :, 0:GR], gate[:, :, 1:GR + 1], ALU.add))
                ve.tensor_tensor(expin[:, b, 1, :, :], expin[:, b, 1, :, :], m[:, :, 1:GR + 1], ALU.subtract).then_inc(scored, 1)

            def weights(G, turn, b):
                w, c = wc[:, b, 0, :, :], wc[:, b, 1, :, :]
                ve.wait_ge(exped, G + 1)
                ch.link(ve.tensor_copy(w[:, :, 0], den[:, 1 - b, :, GR]))
                ch.link(ve.tensor_tensor_scan(den[:, b, :, :].rearrange("p h s -> p (h s)"), c.rearrange("p h s -> p (h s)"),
                                              w.rearrange("p h s -> p (h s)"), 0.0, ALU.mult, ALU.add))
                wait(ve, rows_out[b], 16 * turn)
                ch.mark(ve.tensor_copy(row[:, b, :, D:D + H].rearrange("p s h -> p h s"), den[:, b, :, 1:GR + 1]))
                ch.mark(ve.tensor_copy(row[:, b, :, D + H:RW].rearrange("p s h -> p h s"), mrun[:, b, :, 1:GR + 1]))

            def fold(t, b, r):
                ve.wait_ge(mm_done, t + 3)
                ve.tensor_tensor(heads(vbuf[:, r % 2, :]), heads(proj_ps[r % 2][:]), over(wc[:, b, 0, :, r + 1], DH), ALU.mult).then_inc(v_done, 1)
                ve.wait_ge(v_done, t + 3)
                prev = row[:, b, r - 1, :] if r > 0 else row[:, 1 - b, GR - 1, :]
                for h in range(H):
                    c = slice(h * DH, (h + 1) * DH)
                    ins = ve.scalar_tensor_tensor(row[:, b, r, c], prev[:, c], wc[:, b, 1, h, r + 1:r + 2], vbuf[:, r % 2, c],
                                                  ALU.mult, ALU.add)
                if r == GR - 1:
                    ins.then_inc(group_done, 1)
                else:
                    ch.mark(ins)

            def group(G, turn, b, last=False):
                for r in range(GR):
                    fold(G * GR + r, b, r)
                    if r == 1 and not last:
                        scores(G + 1, turn + b, 1 - b)
                    if r == 3 and not last:
                        weights(G + 1, turn + b, 1 - b)

            scores(0, 0, 0)
            weights(0, 0, 0)
            group(0, 0, 0)
            group(1, 0, 1)
            with ve.Fori(1, NG // 2 - 1) as i:
                ch.enter(i - 1, 26)
                group(2 * i, i, 0)
                group(2 * i + 1, i, 1)
            ch.leave(NG // 2 - 2)
            group(NG - 2, NG // 2 - 1, 0)
            group(NG - 1, NG // 2 - 1, 1, last=True)

            ve.wait_ge(group_done, NG)
            ch.join()
            mlast, dlast = mrun[:, 1, :, GR], den[:, 1, :, GR]
            ch.link(ve.tensor_copy(mB[:], over(mlast, P)))
            ve.sem_inc(aux_ready, 1)
            ve.wait_ge(aux_done, 3)
            ch.mark(ve.tensor_copy(upT[:].rearrange("p c f -> p (c f)"), misc_ps[0][:].bitcast(BF16)[:, 0:C * F]))
            ch.mark(ve.tensor_copy(dnT[:], misc_ps[1][:].bitcast(BF16)[0:F, 0:D]))
            ve.wait_ge(aux_done, 4)
            for k in range(2):
                v = mB[:, 4 * k:4 * k + 4, :]
                ch.link(ve.tensor_tensor(v, proj_ps[k][:].rearrange("p (h q) -> p h q", h=4),
                                         egate[:].unsqueeze(1).to_broadcast([P, 4, P]), ALU.add))
                ch.link(ve.tensor_reduce(gm[:, 4 * k:4 * k + 4], v, AX.X, ALU.max))
            ve.tensor_tensor(wq_in[:], mlast, gm[:], ALU.subtract).then_inc(cross_in, 1)
            ve.wait_ge(cross_exp, 1)
            ch.mark(ve.tensor_tensor(heads(tailrow[:, 0:D]), heads(row[:, 1, GR - 1, 0:D]), over(wq[:], DH), ALU.mult))
            ch.link(ve.tensor_tensor(tailrow[:, D:D + H], dlast, wq[:], ALU.mult))
            ve.sem_inc(aux_ready, 1)
            ve.wait_ge(aux_done, 5)
            ve.wait_ge(fix_got, 16)
            gmax = sc_ps[0][:, H:2 * H]
            ch.link(ve.tensor_tensor(mtot[:], fixrow[:, D + H:RW], gmax, ALU.max))
            ch.mark(ve.tensor_tensor(ab_in[:, 0, :], fixrow[:, D + H:RW], mtot[:], ALU.subtract))
            ve.tensor_tensor(ab_in[:, 1, :], gmax, mtot[:], ALU.subtract).then_inc(cross_in, 1)
            ve.wait_ge(cross_exp, 2)
            fa = heads(fixrow[:, 0:D])
            ch.mark(ve.tensor_tensor(fa, fa, over(ab[:, 0, :], DH), ALU.mult))
            ch.mark(ve.tensor_tensor(heads(vbuf[:, 0, :]), heads(xt_ps[0][:]), over(ab[:, 1, :], DH), ALU.mult))
            ch.mark(ve.tensor_tensor(fixrow[:, D:D + H], fixrow[:, D:D + H], ab[:, 0, :], ALU.mult))
            ch.link(ve.tensor_tensor(cden[:], sc_ps[0][:, 0:H], ab[:, 1, :], ALU.mult))
            ch.mark(ve.tensor_tensor(fixrow[:, D:D + H], fixrow[:, D:D + H], cden[:], ALU.add))
            ch.link(ve.tensor_tensor(fixrow[:, 0:D], fixrow[:, 0:D], vbuf[:, 0, :], ALU.add))
            ve.sem_inc(fix_ready, 1)

            def step(s, m):
                def on(t):
                    return not isinstance(t, int) or 0 <= t < NT

                t, u = s - 6, m % U
                if on(t):
                    ve.wait_ge(dn_done, t + 1)
                    if u % NB == 0:
                        wait(ve, o_out[u // NB], (16 * (t // U)) if isinstance(t, int) else t_turn[0] * 16 - 16)
                    ve.scalar_tensor_tensor(obuf[:, u, :], proj_ps[u % 2][:], qs[:, u, 7:8], ybuf[:, u, :],
                                            ALU.mult, ALU.add).then_inc(o_ready, 1)
                t, u = s - 4, (m - 4) % U
                if on(t):
                    ve.wait_ge(up_done, t + 1)
                    ch.link(ve.tensor_scalar(hid[:, 0, :], sc_ps[u % 2][:, 0:F], qs[:, u, 4:5], MAGIC, ALU.mult, ALU.add))
                    ch.link(ve.tensor_scalar(hid[:, 1, :], hid[:, 0, :], MAGIC, 0.0, ALU.subtract, ALU.max))
                    ch.link(ve.tensor_scalar(hid[:, 2, :], hid[:, 1, :], QMAX, Q_EPS, ALU.min, ALU.max, accum_out=qs[:, u, 5:6]))
                    ch.mark(ve.tensor_scalar(qs[:, u, 7:8], qs[:, u, 5:6], qsc[:, 1:2], None, ALU.mult))
                    ch.link(ve.reciprocal(qs[:, u, 6:7], qs[:, u, 5:6]))
                    ch.link(ve.tensor_scalar(qs[:, u, 6:7], qs[:, u, 6:7], QMAX, None, ALU.mult))
                    wait(ve, ht_ready, t - 1)
                    ve.tensor_scalar(hq[:, u % 2, 0:F], hid[:, 2, :], qs[:, u, 6:7], MAGIC, ALU.mult, ALU.add).then_inc(h_ready, 1)
                t, u = s - 2, (m - 2) % U
                if on(t):
                    ve.wait_ge(yc_ready, t + 1)
                    ch.mark(ve.tensor_reduce(qs[:, u, 0:1], yc[:, u % 2, :], AX.X, ALU.max, apply_absolute_value=True))
                    ch.link(ve.reciprocal(qs[:, u, 1:2], std[:, u:u + 1]))
                    ch.link(ve.tensor_scalar(qs[:, u, 2:3], qs[:, u, 0:1], qs[:, u, 1:2], Q_EPS, ALU.mult, ALU.max))
                    ch.mark(ve.tensor_scalar(qs[:, u, 4:5], qs[:, u, 2:3], qsc[:, 0:1], None, ALU.mult))
                    ch.link(ve.reciprocal(qs[:, u, 0:1], qs[:, u, 2:3]))
                    ve.tensor_scalar(qs[:, u, 3:4], qs[:, u, 0:1], qs[:, u, 1:2], QMAX, ALU.mult, ALU.mult).then_inc(qs_ready, 1)
                t, u = s - 1, (m - 1) % U
                if on(t):
                    ve.wait_ge(agg_ready, t + 1)
                    if u % NB == 0:
                        ve.wait_ge(x_got4[u // NB], 16 * (t // U) + 16 if isinstance(t, int) else t_turn[0] * 16 + 16)
                    ch.link(ve.tensor_tensor(ybuf[:, u, :], x_in[:, u, :], rg[:, u, 0:D], ALU.add))
                    ch.mark(ve.bn_stats(bn6[:, u, :], ybuf[:, u, :]))
                v = m
                if on(s):
                    ve.wait_ge(rg_got[v], 16 * (s // U) + 16 if isinstance(s, int) else t_turn[0] * 16 + 16)
                    ch.link(ve.tensor_scalar(rden[:, v, :], rg[:, v, D:D + H], 0.5, None, ALU.max))
                    ve.reciprocal(rden[:, v, :], rden[:, v, :]).then_inc(rden_ready, 1)
                elif on(t):
                    ch.join()
                if on(t):
                    ch.link(ve.bn_aggr(mv[:, u, :], bn6[:, u, :]))
                    ve.tensor_scalar(negm[:, u:u + 1], mv[:, u, 0:1], -1.0, None, ALU.mult).then_inc(y_ready, 1)

            t_turn = [None]
            for s in range(2 * U):
                step(s, s % U)
            with ve.Fori(2, FULL // U) as i:
                t_turn[0] = i
                ch.enter(i - 2, 15 * U)
                for m in range(U):
                    step(U * i + m, m)
            ch.leave(FULL // U - 2)
            for s in range(FULL, NT + 6):
                step(s, s % U)


_INS = ["x", "src", "dst", "L0_gnn_Ws", "L0_gnn_Wb", "L0_gnn_a_w", "L0_gnn_a_b", "L0_ffn_w_up", "L0_ffn_w_down"]


def kernel(**inputs):
    import numpy as np
    import concourse.bacc as bacc
    from concourse.bass_utils import run_bass_kernel_spmd

    nc = bacc.Bacc("TRN2", target_bir_lowering=False, num_devices=1)
    arrays, args = {}, []
    for name in _INS:
        a = np.ascontiguousarray(inputs[name])
        arrays[f"in_{name}"] = a
        args.append(nc.dram_tensor(f"in_{name}", a.shape, mybir.dt.from_np(a.dtype), kind="ExternalInput").ap())
    out = nc.dram_tensor("out", arrays["in_x"].shape, F32, kind="ExternalOutput").ap()
    build(nc, *args, out)
    return run_bass_kernel_spmd(nc, [arrays], core_ids=[0]).results[0]["out"]
```

```python
from contextlib import ExitStack

import concourse.bass as bass
from concourse import mybir

ALU = mybir.AluOpType
ACT = mybir.ActivationFunctionType
AX = mybir.AxisListType
F32 = mybir.dt.float32
F32R = mybir.dt.float32r
BF16 = mybir.dt.bfloat16
I32 = mybir.dt.int32

P = 128
BIG = 1.0e30
FAR = 20000
MAGIC = 1.5 * 2.0 ** 23
LN_EPS = 1e-5
Q_EPS = 1e-5
QMAX = 127.0


def wait(eng, sem, value):
    if isinstance(value, int) and value <= 0:
        return
    eng.wait_ge(sem, value)


class Chain:

    def __init__(self, eng, sem):
        self.eng, self.sem, self.base, self.n = eng, sem, 0, 0

    def mark(self, ins):
        ins.then_inc(self.sem, 1)
        self.n += 1
        return self.base + self.n

    def need(self, mark):
        self.eng.wait_ge(self.sem, mark)

    def link(self, ins):
        self.need(self.mark(ins))

    def enter(self, turn, per):
        self.start, self.per = self.base + self.n, per
        self.base, self.n = turn * per + self.start, 0

    def leave(self, turns):
        assert self.n == self.per, f"a turn of the loop marks {self.n} results, not {self.per}"
        self.base, self.n = self.start + turns * self.per, 0


def build(nc, x, src, dst, Ws, Wb, a_w, a_b, w_up, w_down, out):
    N, D = x.shape
    H, _, DH = Ws.shape
    F = w_up.shape[0]
    E = src.shape[0]
    C = D // P
    ET = 80
    EP = E // ET
    GR = 4
    NG = ET // GR
    FULL = N // P
    TAIL0 = N - P
    TN = N - FULL * P
    NT = 80
    RW = D + 2 * H
    SW = H + 2
    NQ = NT // 2
    QS = 4
    NG1 = NT // GR
    assert EP * ET == E and H * DH == D and C * P == D and FULL == NT - 2

    rows = nc.dram_tensor("edge_rows", (P * ET + P, RW), F32, kind="Internal").ap()
    dst_table = nc.dram_tensor("dst_table", (N, H), F32, kind="Internal").ap()
    src_table = nc.dram_tensor("src_table", (N, SW), F32, kind="Internal").ap()
    last_edge = nc.dram_tensor("last_edge", (N, 1), I32, kind="Internal").ap()

    with ExitStack() as ctx:
        def sb(name, shape, dt=F32):
            return ctx.enter_context(nc.sbuf_tensor(name, shape, dt))

        def sem(name):
            return ctx.enter_context(nc.semaphore(name))

        bank = [ctx.enter_context(nc.psum_tensor(f"bank{i}", [P, 512], F32)) for i in range(8)]
        xt_ps = bank[0:4]
        proj_ps = bank[2:4]
        sc_ps = bank[4:6]
        misc_ps = bank[6:8]

        identF = sb("identF", [P, P])
        identB = sb("identB", [P, P], BF16)
        shift = sb("shift", [P, P])
        before = sb("before", [P, P])
        inv_d = sb("inv_d", [P, P])
        epsT = sb("epsT", [P, 1])
        magicP = sb("magicP", [P, 1])
        magicN = sb("magicN", [P, 1])
        minus_half = sb("minus_half", [P, 1])
        onesB = sb("onesB", [P, P], BF16)

        Wsb = sb("Wsb", [P, C, H, DH])
        awb = sb("awb", [P, H, 2 * DH])
        wbb = sb("wbb", [P, D])
        abb = sb("abb", [P, H])
        prod = sb("prod", [P, C, H, DH])
        Whi = sb("Whi", [P, C, D], F32R)
        Wlo = sb("Wlo", [P, C, D], F32R)
        wts = sb("wts", [P, C, 2 * H])
        wparts = sb("wparts", [P, C, 4 * H], F32R)
        fold2 = sb("fold2", [4 * H, 2 * H])
        s_sb = sb("s_sb", [4 * H, 2, GR * P])
        zrow = sb("zrow", [P, RW])
        const_s = sb("const_s", [P, H])
        bpart = sb("bpart", [3, 3, D], BF16)
        brest = sb("brest", [3, D])
        brow = sb("brow", [3, D], BF16)

        dst_i = sb("dst_i", [P, ET], I32)
        nxt_i = sb("nxt_i", [P, ET], I32)
        prv_i = sb("prv_i", [P, 1], I32)
        src_i = sb("src_i", [P, ET], I32)
        dst_g = sb("dst_g", [P, ET], I32)
        dst_f = sb("dst_f", [P, ET])
        same_next = sb("same_next", [P, ET])
        edge_no = sb("edge_no", [P, ET], I32)
        scat = sb("scat", [P, ET, 2], I32)
        gcol = sb("gcol", [P, ET])
        gates = sb("gates", [P, NG, H, GR + 1])
        headeq = sb("headeq", [P, ET])
        headcnt = sb("headcnt", [P, 1])
        fx = sb("fx", [P, 8])
        fix_idx = sb("fix_idx", [P, 1], I32)
        zero_i = sb("zero_i", [P, FULL], I32)
        scat_ring = sb("scat_ring", [P, 2, GR, 2], I32)
        idx_ring = sb("idx_ring", [P, 2, 2, GR], I32)
        last_sb = sb("last_sb", [P, NT], I32)
        last_ring = sb("last_ring", [P, QS, 2], I32)

        x_in = sb("x_in", [P, QS, 2, D])
        xThi = sb("xThi", [P, 2, C, GR * P], F32R)
        xTlo = sb("xTlo", [P, 2, C, GR * P], F32R)
        bn_all = sb("bn_all", [P, NT, 6])
        raw_s = sb("raw_s", [P, NT, 2 * H])
        meanT = sb("meanT", [P, NT])
        varT = sb("varT", [P, NT])
        difT = sb("difT", [P, NT])
        rstdT = sb("rstdT", [P, NT])
        dst_tab = sb("dst_tab", [P, NT, H])
        src_tab = sb("src_tab", [P, NT, SW])

        xg = sb("xg", [P, 2, GR, D])
        sdst = sb("sdst", [P, 2, GR, H])
        ssrc = sb("ssrc", [P, 2, GR, SW])
        xn = sb("xn", [P, 2, D])
        score = sb("score", [P, 2, H, GR + 1])
        mrun = sb("mrun", [P, 2, H, GR + 1])
        expin = sb("expin", [P, 2, 2, H, GR])
        wc = sb("wc", [P, 2, 2, H, GR + 1])
        den = sb("den", [P, 2, H, GR + 1])
        vbuf = sb("vbuf", [P, 2, D])
        carry = sb("carry", [P, 2, D])
        row = sb("row", [P, 2, GR, RW])

        mB = sb("mB", [P, H, P])
        dB = sb("dB", [P, 2, P])
        egate = sb("egate", [P, P])
        cmask = sb("cmask", [P, P])
        gm = sb("gm", [P, H])
        wq_in = sb("wq_in", [P, H])
        wq = sb("wq", [P, H])
        tailrow = sb("tailrow", [P, D + H])
        fixrow = sb("fixrow", [P, RW])
        mtot = sb("mtot", [P, H])
        ab_in = sb("ab_in", [P, 2, H])
        ab = sb("ab", [P, 2, H])
        cden = sb("cden", [P, H])

        up_sb = sb("up_sb", [F, D])
        dn_sb = sb("dn_sb", [P, C, F])
        asum = sb("asum", [P, 2])
        wsc = sb("wsc", [P, 2])
        whalf = sb("whalf", [P, 2, 2])
        qsc = sb("qsc", [P, 2])
        tern = sb("tern", [P, D], BF16)
        up_t = sb("up_t", [F, D], BF16)
        dn_t = sb("dn_t", [P, C, F], BF16)
        upT = sb("upT", [P, C, F], BF16)
        dnT = sb("dnT", [F, D], BF16)

        f1 = wbb[:]
        rg = row
        ybuf = xg
        obuf = prod
        rden = sb("rden", [P, QS, 2, H])
        ysum = sb("ysum", [P, QS, 2])
        sqsum = sb("sqsum", [P, QS, 2])
        negm = sb("negm", [P, QS, 2])
        std = sb("std", [P, QS, 2])
        qT = sb("qT", [P, 2, D], BF16)
        qv = sb("qv", [P, QS, 8, 2])
        hid = sb("hid", [P, 2, 2, F])
        hid2 = sb("hid2", [P, 2, 2, F])
        hq = sb("hq", [P, 2, 2, P])
        hqT = sb("hqT", [F, 2, 2 * P], BF16)

        w_in = sem("w_in")
        ffw_in = sem("ffw_in")
        idx_in = sem("idx_in")
        pads_set = sem("pads_set")
        consts_set = sem("consts_set")
        fill_out = sem("fill_out")
        x_got1 = [sem(f"x_got1_{i}") for i in range(QS)]
        tables_out = sem("tables_out")
        last_in = sem("last_in")
        dve_chain = sem("dve_chain")
        pool_chain = sem("pool_chain")
        pool_gate = sem("pool_gate")
        act_chain = sem("act_chain")
        scat_done = [sem(f"scat_done{i}") for i in range(2)]
        scat_ready = sem("scat_ready")
        wsum_ready = sem("wsum_ready")
        wmean_ready = sem("wmean_ready")
        wts_ready = sem("wts_ready")
        t1_done = sem("t1_done")
        hi1_done = sem("hi1_done")
        lo1_done = sem("lo1_done")
        s1_done = sem("s1_done")
        s1_copied = sem("s1_copied")
        back_done = sem("back_done")
        kept = sem("kept")
        stats_done = sem("stats_done")
        var_ready = sem("var_ready")
        rstd_ready = sem("rstd_ready")
        tables_ready = sem("tables_ready")
        x_got2 = [sem(f"x_got2_{i}") for i in range(2)]
        small_got = [sem(f"small_got{i}") for i in range(2)]
        normed = sem("normed")
        scored = sem("scored")
        exped = sem("exped")
        t2_done = sem("t2_done")
        hi2_done = sem("hi2_done")
        lo2_done = sem("lo2_done")
        mm_done = sem("mm_done")
        v_done = sem("v_done")
        group_done = sem("group_done")
        rows_out = [sem(f"rows_out{i}") for i in range(2)]
        aux_ready = sem("aux_ready")
        aux_done = sem("aux_done")
        cross_in = sem("cross_in")
        cross_exp = sem("cross_exp")
        fix_got = sem("fix_got")
        fix_ready = sem("fix_ready")
        fix_out = sem("fix_out")
        x_got4 = [sem(f"x_got4_{i}") for i in range(QS)]
        rg_got = [sem(f"rg_got{i}") for i in range(QS)]
        rden_ready = sem("rden_ready")
        agg_ready = sem("agg_ready")
        y_ready = sem("y_ready")
        yc_ready = sem("yc_ready")
        sq_done = sem("sq_done")
        std_ready = sem("std_ready")
        qs_ready = sem("qs_ready")
        qm_ready = [sem(f"qm_ready{k}") for k in range(2)]
        qt_ready = sem("qt_ready")
        qt_copied = sem("qt_copied")
        up_done = sem("up_done")
        relu_ready = sem("relu_ready")
        h_ready = sem("h_ready")
        ht_ready = sem("ht_ready")
        ht_copied = sem("ht_copied")
        dn_done = sem("dn_done")
        f1_ready = sem("f1_ready")
        o_ready = [sem(f"o_ready{k}") for k in range(2)]
        o_out = [sem(f"o_out{i}") for i in range(2)]
        tail_out = sem("tail_out")

        x_main = x[0:FULL * P, :].rearrange("(p j) d -> p j d", j=FULL)
        out_main = out[0:FULL * P, :].rearrange("(p j) d -> p j d", j=FULL)
        rows_v = rows[0:P * ET, :].rearrange("(p t) w -> p t w", t=ET)
        block = ctx.enter_context(nc.Block())

        AMAX, RSTD, IA2, QSC, SUP, A3, X2, SDN = range(8)
        LAGS = 5

        def o_tile(b, k):
            return obuf[:, 2 * b + k, :, :].rearrange("p h d -> p (h d)")

        def o_pair(b):
            return obuf[:, 2 * b:2 * b + 2, :, :].rearrange("p k h d -> p k (h d)")

        def rg_pair(a):
            return rg[:, a // 2, 2 * (a % 2):2 * (a % 2) + 2, :]

        def y_pair(a):
            return ybuf[:, a // 2, 2 * (a % 2):2 * (a % 2) + 2, :]

        def yc_tile(b, k):
            return Wsb[:, 2 * b + k, :, :].rearrange("p h d -> p (h d)")

        def qm_tile(b, k):
            return (vbuf, carry)[b][:, k, :]

        def sq_tile(k):
            return xn[:, k, :]

        def heads(ap):
            return ap.rearrange("p (h d) -> p h d", h=H)

        def over(ap, n):
            return ap.unsqueeze(2).to_broadcast([P, H, n])

        @block.sync
        def _(sp):
            for c in range(C):
                sp.dma_start(Wsb[:, c, :, :], Ws[:, c * P:(c + 1) * P, :].rearrange("h k d -> k h d")).then_inc(w_in, 16)
            sp.dma_start(awb[:].rearrange("p h d -> p (h d)"), a_w.rearrange("h d -> (h d)").partition_broadcast(P)).then_inc(w_in, 16)
            sp.dma_start(wbb[:], Wb.rearrange("h d -> (h d)").partition_broadcast(P)).then_inc(w_in, 16)
            sp.dma_start(abb[:], a_b.partition_broadcast(P)).then_inc(w_in, 16)

            def load(q, slot, got):
                if isinstance(q, int) and q == NQ - 1:
                    sp.dma_start(x_in[:, slot, 0, :], x[TAIL0:N, :]).then_inc(got[slot], 16)
                else:
                    sp.dma_start(x_in[:, slot, :, :], x_main[:, bass.ds(2 * q, 2), :]).then_inc(got[slot], 16)

            def refill1(q, slot):
                sp.wait_ge(t1_done, 2 * q - 2 * QS + 2)
                sp.wait_ge(stats_done, 2 * q - 2 * QS + 2)
                load(q, slot, x_got1)

            for q in range(QS):
                load(q, q, x_got1)
            with sp.Fori(1, NQ // QS - 1) as i:
                for slot in range(QS):
                    refill1(QS * i + slot, slot)
            for slot in range(QS):
                refill1(NQ - QS + slot, slot)

            sp.wait_ge(tables_ready, 1)
            for tab, sbt in ((dst_table, dst_tab), (src_table, src_tab)):
                sp.dma_start(tab[0:FULL * P, :].rearrange("(p j) w -> p j w", j=FULL), sbt[:, 0:FULL, :]).then_inc(tables_out, 16)
                sp.dma_start(tab[FULL * P:N, :], sbt[P - TN:P, FULL, :]).then_inc(tables_out, 16)
            for r in range(2):
                sp.wait_ge(scat_done[r], 16 * ET // 2)
            sp.dma_start(last_sb[:, 0:FULL], last_edge[0:FULL * P, :].rearrange("(p j) o -> p (j o)", j=FULL)).then_inc(last_in, 16)
            sp.dma_start(last_sb[:, FULL:FULL + 1], last_edge[TAIL0:N, :]).then_inc(last_in, 16)

            with sp.Fori(0, NG // 2) as i:
                for b in range(2):
                    sp.wait_ge(group_done, 2 * i + b + 1)
                    sp.dma_start(rows_v[:, bass.ds((2 * i + b) * GR, GR), :], row[:, b, :, :]).then_inc(rows_out[b], 16)

            def store(q, b):
                sp.wait_ge(o_ready[0], q + 1)
                sp.wait_ge(o_ready[1], q + 1)
                sp.dma_start(out_main[:, bass.ds(2 * q, 2), :], o_pair(b)).then_inc(o_out[b], 16)

            def refill4(q, slot):
                sp.wait_ge(y_ready, q - QS + 1)
                load(q, slot, x_got4)

            for q in range(QS):
                load(q, q, x_got4)
            with sp.Fori(1, NQ // QS - 1) as i:
                for slot in range(QS):
                    refill4(QS * i + slot, slot)
                    store(QS * i + slot - QS, slot % 2)
            for slot in range(QS):
                refill4(NQ - QS + slot, slot)
                store(NQ - 2 * QS + slot, slot % 2)
            for q in range(NQ - QS, NQ - 1):
                store(q, q % 2)
            sp.wait_ge(o_ready[0], NQ)
            sp.dma_start(out[FULL * P:N, :], o_tile((NQ - 1) % 2, 0)[P - TN:P, :]).then_inc(tail_out, 16)
            sp.wait_ge(o_out[0], 16 * (NQ // 2))
            sp.wait_ge(o_out[1], 16 * (NQ // 2 - 1))
            sp.wait_ge(tail_out, 16)

        @block.gpsimd
        def _(gp):
            ch = Chain(gp, pool_chain)
            lim_nodes = gp.to_reg(N - 1)
            lim_rows = gp.to_reg(P * ET + P - 1)
            gp.memset(dst_i[:], FAR).then_inc(pads_set, 1)
            gp.memset(nxt_i[:], FAR + 1).then_inc(pads_set, 1)
            gp.memset(prv_i[:], -1).then_inc(pads_set, 1)
            gp.memset(src_i[:], 0).then_inc(pads_set, 1)
            gp.iota(zero_i[:], [[0, FULL]], base=P * ET, channel_multiplier=1).then_inc(pads_set, 1)
            gp.memset(zrow[:], 0.0).then_inc(pads_set, 1)
            gp.iota(edge_no[:], [[1, ET]], base=0, channel_multiplier=ET).then_inc(consts_set, 1)
            ch.mark(gp.memset(identF[:], 0.0))
            ch.mark(gp.memset(shift[:], 0.0))
            ch.link(gp.memset(before[:], 1.0))
            gp.affine_select(out=identF[:], in_=identF[:], compare_op=ALU.not_equal, fill=1.0, base=0,
                             pattern=[[-1, P]], channel_multiplier=1).then_inc(consts_set, 1)
            gp.affine_select(out=shift[:], in_=shift[:], compare_op=ALU.not_equal, fill=1.0, base=-1,
                             pattern=[[1, P]], channel_multiplier=-1).then_inc(consts_set, 1)
            gp.affine_select(out=before[:], in_=before[:], compare_op=ALU.is_gt, fill=0.0, base=0,
                             pattern=[[1, P]], channel_multiplier=-1).then_inc(consts_set, 1)
            gp.memset(minus_half[:], -0.5).then_inc(consts_set, 1)

            gp.wait_ge(scat_ready, 1)
            gp.wait_ge(fill_out, 48)
            def scatter_turn(i):
                for r in range(2):
                    if isinstance(i, int):
                        col = slice(i * 2 * GR + r * GR, i * 2 * GR + r * GR + GR)
                    else:
                        col = bass.ds(gp.snap(i * 2 * GR + r * GR), GR)
                    wait(gp, scat_done[r], i * (16 * GR))
                    ch.link(gp.tensor_copy(scat_ring[:, r, :, :], scat[:, col, :]))
                    gp.sem_inc(pool_gate, 1)
                    for k in range(GR):
                        gp.indirect_dma_start(last_edge, bass.IndirectOffsetOnAxis(ap=scat_ring[:, r, k, 0:1], axis=0),
                                              scat_ring[:, r, k, 1:2], None,
                                              bounds_check=lim_nodes, oob_is_err=False).then_inc(scat_done[r], 16)

            scatter_turn(0)
            with gp.Fori(1, ET // (2 * GR)) as i:
                ch.enter(i - 1, 2)
                scatter_turn(i)
            ch.leave(ET // (2 * GR) - 1)

            def take_indices(G, b):
                if isinstance(G, int):
                    col = slice(G * GR, G * GR + GR)
                else:
                    col = bass.ds(gp.snap(G * GR), GR)
                ch.mark(gp.tensor_copy(idx_ring[:, b, 0, :], dst_g[:, col]))
                ch.link(gp.tensor_copy(idx_ring[:, b, 1, :], src_i[:, col]))
                gp.sem_inc(pool_gate, 1)

            def gather_x(b):
                for r in range(GR):
                    gp.indirect_dma_start(xg[:, b, r, :], None, x, bass.IndirectOffsetOnAxis(ap=idx_ring[:, b, 1, r:r + 1], axis=0),
                                          bounds_check=lim_nodes, oob_is_err=False).then_inc(x_got2[b], 16)

            def gather_small(b):
                for r in range(GR):
                    gp.indirect_dma_start(sdst[:, b, r, :], None, dst_table, bass.IndirectOffsetOnAxis(ap=idx_ring[:, b, 0, r:r + 1], axis=0),
                                          bounds_check=lim_nodes, oob_is_err=False).then_inc(small_got[b], 16)
                    gp.indirect_dma_start(ssrc[:, b, r, :], None, src_table, bass.IndirectOffsetOnAxis(ap=idx_ring[:, b, 1, r:r + 1], axis=0),
                                          bounds_check=lim_nodes, oob_is_err=False).then_inc(small_got[b], 16)

            for b in range(2):
                take_indices(b, b)
                gather_x(b)
            gp.wait_ge(var_ready, 1)
            gp.tensor_tensor(rstdT[:], varT[:], minus_half[:].to_broadcast([P, NT]), ALU.pow).then_inc(rstd_ready, 1)
            gp.wait_ge(tables_out, 64)
            gp.sem_inc(pool_gate, 1)
            for b in range(2):
                gather_small(b)
            with gp.Fori(1, NG // 2) as i:
                ch.enter(i - 1, 4)
                for b in range(2):
                    G = 2 * i + b
                    gp.wait_ge(scored, G - 1)
                    gp.wait_ge(normed, (G - 1) * GR)
                    take_indices(G, b)
                    gather_small(b)
                    gather_x(b)
            ch.leave(NG // 2 - 1)

            ch.link(gp.memset(fixrow[:], 0.0))
            gp.wait_ge(rows_out[0], 16 * (NG // 2))
            gp.wait_ge(rows_out[1], 16 * (NG // 2))
            gp.sem_inc(pool_gate, 1)
            gp.indirect_dma_start(fixrow[:], None, rows, bass.IndirectOffsetOnAxis(ap=fix_idx[:], axis=0),
                                  bounds_check=lim_rows, oob_is_err=False).then_inc(fix_got, 16)
            gp.wait_ge(fix_ready, 1)
            gp.sem_inc(pool_gate, 1)
            gp.indirect_dma_start(rows, bass.IndirectOffsetOnAxis(ap=fix_idx[:], axis=0), fixrow[:], None,
                                  bounds_check=lim_rows, oob_is_err=False).then_inc(fix_out, 16)
            gp.wait_ge(last_in, 32)
            gp.wait_ge(fix_out, 16)

            def fetch(q, a):
                col = slice(2 * q, 2 * q + 2) if isinstance(q, int) else bass.ds(gp.snap(2 * q), 2)
                wait(gp, y_ready, q - QS + 1)
                ch.link(gp.tensor_copy(last_ring[:, a, :], last_sb[:, col]))
                gp.sem_inc(pool_gate, 1)
                for k in range(2):
                    gp.indirect_dma_start(rg_pair(a)[:, k, :], None, rows, bass.IndirectOffsetOnAxis(ap=last_ring[:, a, k:k + 1], axis=0),
                                          bounds_check=lim_rows, oob_is_err=False).then_inc(rg_got[a], 16)

            def divide(q, a):
                wait(gp, rden_ready, q + 1)
                v = rg_pair(a)[:, :, 0:D].rearrange("p k (h d) -> p k h d", h=H)
                gp.tensor_tensor(v, v, rden[:, a, :, :].unsqueeze(3).to_broadcast([P, 2, H, DH]), ALU.mult).then_inc(agg_ready, 1)

            def output(q, a, stores):
                gp.wait_ge(f1_ready, q + 1)
                b = a % 2
                wait(gp, o_out[b], stores)
                gp.tensor_tensor(o_tile(b, 1), f1, y_pair(a)[:, 1, :], ALU.add).then_inc(o_ready[1], 1)

            AHEAD = 2

            def step(s, m, i=None):
                if not isinstance(s, int) or s + AHEAD < NQ:
                    fetch(s + AHEAD, (m + AHEAD) % QS)
                if not isinstance(s, int) or 5 <= s:
                    output(s - 5, (m - 5) % QS, 16 * ((s - 5) // 2) if i is None else 32 * i + 16 * ((m - 5) // 2))
                if not isinstance(s, int) or s < NQ:
                    divide(s, m)

            for q in range(AHEAD):
                fetch(q, q)
            for s in range(2 * QS):
                step(s, s % QS)
            with gp.Fori(2, NQ // QS - 1) as i:
                ch.enter(i - 2, QS)
                for m in range(QS):
                    step(QS * i + m, m, i)
            ch.leave(NQ // QS - 3)
            for s in range(NQ - QS, NQ + LAGS):
                step(s, s % QS)

        @block.scalar
        def _(act):
            act.wait_ge(pads_set, 6)
            dst2 = dst.rearrange("(p t) -> p t", t=ET)
            act.dma_start(dst_i[0:EP, :], dst2).then_inc(idx_in, 16)
            act.dma_start(src_i[0:EP, :], src.rearrange("(p t) -> p t", t=ET)).then_inc(idx_in, 16)
            act.dma_start(nxt_i[0:EP - 1, :], dst[1:1 + (EP - 1) * ET].rearrange("(p t) -> p t", t=ET)).then_inc(idx_in, 16)
            act.dma_start(nxt_i[EP - 1:EP, 0:ET - 1], dst[1 + (EP - 1) * ET:E].rearrange("(p t) -> p t", p=1)).then_inc(idx_in, 16)
            act.dma_start(prv_i[1:EP, :], dst2[0:EP - 1, ET - 1:ET], allow_slow_non_contiguous=True).then_inc(idx_in, 16)
            act.dma_start(last_edge[0:FULL * P, :].rearrange("(p j) o -> p (j o)", j=FULL), zero_i[:]).then_inc(fill_out, 16)
            act.dma_start(last_edge[FULL * P:N, :], zero_i[0:TN, 0:1]).then_inc(fill_out, 16)
            act.dma_start(rows[P * ET:P * ET + P, :], zrow[:]).then_inc(fill_out, 16)
            act.dma_start(up_sb[:], w_up).then_inc(ffw_in, 16)
            act.dma_start(dn_sb[:], w_down.rearrange("(c k) f -> k c f", k=P)).then_inc(ffw_in, 16)

            def high1(t, b, r):
                act.wait_ge(t1_done, t + 1)
                act.activation(xThi[:, b, :, r * P:(r + 1) * P], xt_ps[r][:].rearrange("p (c n) -> p c n", c=C),
                               ACT.Copy).then_inc(hi1_done, 1)

            def scores1(g, b):
                act.wait_ge(s1_done, g + 1)
                wait(act, back_done, g - 1)
                act.activation(s_sb[:, b, :], sc_ps[b][0:4 * H, :], ACT.Copy).then_inc(s1_copied, 1)

            def group1(g, b):
                for r in range(GR):
                    if not isinstance(g, int) or g + 1 < NG1:
                        wait(act, s1_done, g)
                        high1(GR * (g + 1) + r, 1 - b, r)
                if not isinstance(g, int) or g >= 0:
                    scores1(g, b)

            group1(-1, 1)
            group1(0, 0)
            group1(1, 1)
            with act.Fori(1, NG1 // 2 - 1) as i:
                group1(2 * i, 0)
                group1(2 * i + 1, 1)
            group1(NG1 - 2, 0)
            group1(NG1 - 1, 1)

            def norm_tile(t, turn, b, r):
                act.wait_ge(x_got2[b], 16 * GR * turn + 16 * GR)
                act.wait_ge(small_got[b], 32 * GR * turn + 32 * GR)
                wait(act, t2_done, t - 1)
                act.activation(xn[:, r % 2, :], xg[:, b, r, :], ACT.Identity, bias=ssrc[:, b, r, H:H + 1],
                               scale=ssrc[:, b, r, H + 1:H + 2]).then_inc(normed, 1)

            def high2(t, r):
                act.wait_ge(t2_done, t + 1)
                wait(act, mm_done, t - 1)
                act.activation(xThi[:, r % 2, :, 0:P], xt_ps[r % 2][:].rearrange("p (c n) -> p c n", c=C),
                               ACT.Copy).then_inc(hi2_done, 1)

            def exps(G, b):
                act.wait_ge(scored, G + 1)
                act.activation(wc[:, b, :, :, 1:GR + 1], expin[:, b, :, :, :], ACT.Exp).then_inc(exped, 1)

            norm_tile(0, 0, 0, 0)
            exps(0, 0)

            def group(G, turn, b, last=False):
                for r in range(GR):
                    t = G * GR + r
                    high2(t, r)
                    if r < GR - 1:
                        norm_tile(t + 1, turn, b, r + 1)
                    elif not last:
                        norm_tile(t + 1, turn + b, 1 - b, 0)
                    if r == 3 and not last:
                        exps(G + 1, 1 - b)

            group(0, 0, 0)
            group(1, 0, 1)
            with act.Fori(1, NG // 2 - 1) as i:
                group(2 * i, i, 0)
                group(2 * i + 1, i, 1)
            group(NG - 2, NG // 2 - 1, 0)
            group(NG - 1, NG // 2 - 1, 1, last=True)

            act.wait_ge(cross_in, 1)
            act.activation(wq[:], wq_in[:], ACT.Exp).then_inc(cross_exp, 1)
            act.wait_ge(cross_in, 2)
            act.activation(ab[:], ab_in[:], ACT.Exp).then_inc(cross_exp, 1)

            def step(s, m):
                def on(q):
                    return not isinstance(q, int) or 0 <= q < NQ

                q3, a3, q2, a2, q4, a4 = s - 3, (m - 3) % QS, s - 2, (m - 2) % QS, s - 4, (m - 4) % QS

                def square(k):
                    ins = act.activation(sq_tile(k), y_pair(a2)[:, k, :], ACT.Square,
                                         bias=negm[:, a2, k:k + 1], accum_out=sqsum[:, a2, k:k + 1])
                    if k == 1:
                        ins.then_inc(sq_done, 1)

                if on(q3):
                    act.wait_ge(qs_ready, q3 + 1)
                    act.activation(qm_tile(a3 % 2, 0), yc_tile(a3 % 2, 0), ACT.Identity, bias=magicP[:],
                                   scale=qv[:, a3, QSC, 0:1]).then_inc(qm_ready[0], 1)
                if on(q2):
                    act.wait_ge(y_ready, q2 + 1)
                    for k in range(2):
                        act.activation(yc_tile(a2 % 2, k), y_pair(a2)[:, k, :], ACT.Identity,
                                       bias=negm[:, a2, k:k + 1]).then_inc(yc_ready, 1)
                q5, a5 = s - 5, (m - 5) % QS
                if on(q5):
                    act.wait_ge(dn_done, q5 + 1)
                    wait(act, o_ready[1], q5)
                    act.activation(f1, proj_ps[1][:], ACT.Copy, scale=qv[:, a5, SDN, 1:2]).then_inc(f1_ready, 1)
                if on(q3):
                    for k in range(2):
                        act.wait_ge(qt_ready, 2 * q3 + 1 + k)
                        wait(act, up_done, q3)
                        act.activation(qT[:, k, :], xt_ps[k][:], ACT.Identity, bias=magicN[:]).then_inc(qt_copied, 1)
                if on(q2):
                    square(0)
                    square(1)
                    act.wait_ge(sq_done, q2 + 1)
                    act.activation(std[:, a2, :], sqsum[:, a2, :], ACT.Sqrt, bias=epsT[:], scale=1.0 / D).then_inc(std_ready, 1)
                if on(q4):
                    act.wait_ge(ht_ready, q4 + 1)
                    wait(act, dn_done, q4 - 1)
                    act.activation(hqT[:, a4 % 2, :], misc_ps[a4 % 2][0:F, 0:2 * P], ACT.Identity,
                                   bias=magicN[0:F, :]).then_inc(ht_copied, 1)
                if on(q3):
                    act.wait_ge(up_done, q3 + 1)
                    wait(act, h_ready, q3 - 1)
                    for k in range(2):
                        ins = act.activation(hid[:, a3 % 2, k, :], sc_ps[a3 % 2][:, k * F:(k + 1) * F], ACT.Relu,
                                             scale=qv[:, a3, SUP, k:k + 1])
                    ins.then_inc(relu_ready, 1)

            for s in range(2 * QS):
                step(s, s % QS)
            with act.Fori(2, NQ // QS - 1) as i:
                for m in range(QS):
                    step(QS * i + m, m)
            for s in range(NQ - QS, NQ + LAGS):
                step(s, s % QS)

        @block.tensor
        def _(pe):
            pe.wait_ge(wsum_ready, 1)
            for c in range(C):
                mm = pe.matmul(misc_ps[0][:, 0:2 * H], inv_d[:], wts[:, c, :], start=(c == 0), stop=(c == C - 1))
            mm.then_inc(wmean_ready, 1)
            pe.wait_ge(consts_set, 5)

            def turn1(t, r, slot, loads):
                if r % 2 == 0:
                    pe.wait_ge(x_got1[slot], loads)
                wait(pe, lo1_done, t - GR + 1)
                for c in range(C):
                    mm = pe.transpose(xt_ps[r][:, c * P:(c + 1) * P], x_in[:, slot, r % 2, c * P:(c + 1) * P], identF[:])
                mm.then_inc(t1_done, 1)

            def group1(g, b, loads):
                for r in range(GR):
                    if not isinstance(g, int) or g + 1 < NG1:
                        turn1(GR * (g + 1) + r, r, 2 * (1 - b) + r // 2, loads)
                back = not isinstance(g, int) or 0 < g
                if back:
                    pe.wait_ge(s1_copied, g)
                    wait(pe, kept, g - 2)
                if not isinstance(g, int) or 0 <= g < NG1:
                    pe.wait_ge(hi1_done, GR * (g + 1))
                    pe.wait_ge(lo1_done, GR * (g + 1))
                    wait(pe, s1_copied, g - 1)
                    for k, part in enumerate((xThi, xTlo)):
                        for c in range(C):
                            mm = pe.matmul(sc_ps[b][0:4 * H, :], wparts[:, c, :], part[:, b, c, :],
                                           start=(k == 0 and c == 0), stop=(k == 1 and c == C - 1))
                    mm.then_inc(s1_done, 1)
                if back:
                    for r in range(GR):
                        mm = pe.matmul(misc_ps[1 - b][:, r * 2 * H:(r + 1) * 2 * H], s_sb[:, 1 - b, r * P:(r + 1) * P],
                                       fold2[:], start=True, stop=True)
                    mm.then_inc(back_done, 1)

            group1(-1, 1, 16)
            pe.wait_ge(wts_ready, 1)
            group1(0, 0, 16)
            group1(1, 1, 32)
            with pe.Fori(1, NG1 // 2 - 1) as i:
                group1(2 * i, 0, 16 * i + 16)
                group1(2 * i + 1, 1, 16 * i + 32)
            group1(NG1 - 2, 0, 16 * (NG1 // 2))
            group1(NG1 - 1, 1, None)
            group1(NG1, 0, None)

            pe.wait_ge(aux_ready, 1)
            for k in range(2):
                mm = pe.matmul(misc_ps[0][:, k * P:(k + 1) * P], dB[:, k, :], identF[:], start=True, stop=True)
            mm.then_inc(aux_done, 1)
            pe.matmul(misc_ps[1][:, 0:1], inv_d[0:F, :], asum[0:F, 0:1], start=True, stop=True)
            pe.matmul(misc_ps[1][:, 1:2], inv_d[:], asum[:, 1:2], start=True, stop=True).then_inc(aux_done, 1)

            def turn2(t, r):
                pe.wait_ge(normed, t + 1)
                wait(pe, lo2_done, t - 1)
                for c in range(C):
                    mm = pe.transpose(xt_ps[r % 2][:, c * P:(c + 1) * P], xn[:, r % 2, c * P:(c + 1) * P], identF[:])
                mm.then_inc(t2_done, 1)

            def project(t, r):
                pe.wait_ge(hi2_done, t + 1)
                wait(pe, v_done, t - 1)
                ps = proj_ps[r % 2]
                for c in range(C):
                    hi = xThi[:, r % 2, c, 0:P]
                    pe.matmul(ps[:], hi, Whi[:, c, :], start=(c == 0), stop=False)
                    pe.matmul(ps[:], hi, Wlo[:, c, :], start=False, stop=False)
                pe.wait_ge(lo2_done, t + 1)
                for c in range(C):
                    pe.matmul(ps[:], xTlo[:, r % 2, c, 0:P], Whi[:, c, :], start=False, stop=False)
                pe.matmul(ps[:], onesB[0:3, :], brow[:], start=False, stop=True).then_inc(mm_done, 1)

            turn2(0, 0)
            for t in range(GR):
                turn2(t + 1, (t + 1) % GR)
                project(t, t)
            with pe.Fori(1, NG - 1) as i:
                for r in range(GR):
                    t = GR * i + r
                    turn2(t + 1, (r + 1) % GR)
                    project(t, r)
            for t in range(GR * (NG - 1), ET):
                if t + 1 < ET:
                    turn2(t + 1, (t + 1) % GR)
                project(t, t % GR)

            pe.wait_ge(aux_ready, 2)
            for c in range(C):
                pe.transpose(misc_ps[0][:].bitcast(BF16)[:, c * F:(c + 1) * F], up_t[:, c * P:(c + 1) * P], identB[0:F, 0:F])
            for c in range(C):
                mm = pe.transpose(misc_ps[1][:].bitcast(BF16)[0:F, c * P:(c + 1) * P], dn_t[:, c, :], identB[:])
            mm.then_inc(aux_done, 1)
            pe.wait_ge(aux_ready, 3)
            for h in range(H):
                mm = pe.matmul(proj_ps[h // 4][:, (h % 4) * P:(h % 4 + 1) * P], mB[:, h, :], identF[:], start=True, stop=True)
            mm.then_inc(aux_done, 1)
            pe.wait_ge(aux_ready, 4)
            pe.matmul(xt_ps[0][:], cmask[:], tailrow[:, 0:D], start=True, stop=True)
            pe.matmul(sc_ps[0][:, 0:H], cmask[:], tailrow[:, D:D + H], start=True, stop=True)
            pe.matmul(sc_ps[0][:, H:2 * H], shift[:], gm[:], start=True, stop=True).then_inc(aux_done, 1)
            pe.wait_ge(fix_ready, 1)

            def step(s, m):
                def on(q):
                    return not isinstance(q, int) or 0 <= q < NQ

                q, a = s - 3, (m - 3) % QS
                if on(q):
                    for k in range(2):
                        pe.wait_ge(qm_ready[k], q + 1)
                        wait(pe, qt_copied, 2 * q - 1 + k)
                        for c in range(C):
                            mm = pe.transpose(xt_ps[k][:, c * P:(c + 1) * P], qm_tile(a % 2, k)[:, c * P:(c + 1) * P], identF[:])
                        mm.then_inc(qt_ready, 1)
                    wait(pe, relu_ready, q - 1)
                    for k in range(2):
                        pe.wait_ge(qt_copied, 2 * q + 1 + k)
                        for c in range(C):
                            mm = pe.matmul(sc_ps[a % 2][:, k * F:(k + 1) * F], qT[:, k, c * P:(c + 1) * P], upT[:, c, :],
                                           start=(c == 0), stop=(c == C - 1))
                    mm.then_inc(up_done, 1)
                q, a = s - 4, (m - 4) % QS
                if on(q):
                    pe.wait_ge(h_ready, q + 1)
                    wait(pe, ht_copied, q - 1)
                    for k in range(2):
                        mm = pe.transpose(misc_ps[a % 2][:, k * P:(k + 1) * P], hq[:, a % 2, k, :], identF[:])
                    mm.then_inc(ht_ready, 1)
                    pe.wait_ge(ht_copied, q + 1)
                    wait(pe, o_ready[0], q)
                    wait(pe, f1_ready, q)
                    for k in range(2):
                        mm = pe.matmul(proj_ps[k][:], hqT[:, a % 2, k * P:(k + 1) * P], dnT[:], start=True, stop=True)
                    mm.then_inc(dn_done, 1)

            for s in range(2 * QS):
                step(s, s % QS)
            with pe.Fori(2, NQ // QS - 1) as i:
                for m in range(QS):
                    step(QS * i + m, m)
            for s in range(NQ - QS, NQ + LAGS):
                step(s, s % QS)

        @block.vector
        def _(ve):
            ch = Chain(ve, dve_chain)
            ch.mark(ve.memset(inv_d[:], 1.0 / D))
            ve.memset(onesB[:], 1.0)
            ve.memset(epsT[:], LN_EPS)
            ve.memset(magicP[:], MAGIC)
            ve.memset(magicN[:], -MAGIC)
            ve.memset(mrun[:], 0.0)
            ve.memset(den[:], 0.0)
            ve.memset(wc[:], 0.0)
            ve.memset(hq[:], 0.0)
            ve.memset(row[:, 1, GR - 1, :], 0.0)
            ch.link(ve.memset(gates[:], -BIG))

            ve.wait_ge(idx_in, 16 * 5)
            ve.wait_ge(consts_set, 5)
            ch.mark(ve.tensor_copy(dst_f[:], dst_i[:]))
            ch.mark(ve.tensor_scalar(dst_g[:], dst_i[:], float(N - 1), None, ALU.min))
            ch.link(ve.tensor_tensor(same_next[:], dst_i[:], nxt_i[:], ALU.is_equal))
            ch.mark(ve.scalar_tensor_tensor(scat[:, :, 0], same_next[:], float(FAR), dst_f[:], ALU.mult, ALU.add))
            ve.tensor_copy(scat[:, :, 1], edge_no[:]).then_inc(scat_ready, 1)
            ch.mark(ve.tensor_copy(identB[:], identF[:]))
            ch.mark(ve.tensor_tensor(fold2[:], identF[0:4 * H, 0:2 * H], identF[0:4 * H, 2 * H:4 * H], ALU.add))
            ch.mark(ve.memset(last_sb[:, NT - 1:NT], P * ET))

            ve.wait_ge(w_in, 16 * (C + 3))
            for half in range(2):
                a = awb[:, :, half * DH:(half + 1) * DH].unsqueeze(1).to_broadcast([P, C, H, DH])
                ch.link(ve.tensor_tensor(prod[:], Wsb[:], a, ALU.mult))
                ch.link(ve.tensor_reduce(wts[:, :, half * H:(half + 1) * H], prod[:], AX.X, ALU.add))
            ve.sem_inc(wsum_ready, 1)
            ve.wait_ge(wmean_ready, 1)
            ch.link(ve.tensor_tensor(wts[:], wts[:], misc_ps[0][:, 0:2 * H].unsqueeze(1).to_broadcast([P, C, 2 * H]),
                                     ALU.subtract))
            ch.link(ve.tensor_copy(wparts[:, :, 0:2 * H], wts[:]))
            ve.tensor_tensor(wparts[:, :, 2 * H:4 * H], wts[:], wparts[:, :, 0:2 * H].bitcast(F32),
                             ALU.subtract).then_inc(wts_ready, 1)

            def tile1(t, b, r, slot, loads):
                if r % 2 == 0:
                    ve.wait_ge(x_got1[slot], loads)
                ve.bn_stats(bn_all[:, bass.ds(t, 1), :].rearrange("p o s -> p (o s)"), x_in[:, slot, r % 2, :]).then_inc(stats_done, 1)
                ve.wait_ge(hi1_done, t + 1)
                view = (slice(None), b, slice(None), slice(r * P, (r + 1) * P))
                ve.tensor_tensor(xTlo[view], xt_ps[r][:].rearrange("p (c n) -> p c n", c=C), xThi[view].bitcast(F32),
                                 ALU.subtract).then_inc(lo1_done, 1)

            def keep1(g, b):
                ve.wait_ge(back_done, g + 1)
                ve.tensor_copy(raw_s[:, bass.ds(GR * g, GR), :].rearrange("p t s -> p (t s)"),
                               misc_ps[b][:, 0:GR * 2 * H]).then_inc(kept, 1)

            def group1(g, b, loads):
                for r in range(GR):
                    if not isinstance(g, int) or g + 1 < NG1:
                        wait(ve, s1_done, g)
                        tile1(GR * (g + 1) + r, 1 - b, r, 2 * (1 - b) + r // 2, loads)
                if not isinstance(g, int) or 0 < g:
                    keep1(g - 1, 1 - b)

            group1(-1, 1, 16)
            group1(0, 0, 16)
            group1(1, 1, 32)
            with ve.Fori(1, NG1 // 2 - 1) as i:
                group1(2 * i, 0, 16 * i + 16)
                group1(2 * i + 1, 1, 16 * i + 32)
            group1(NG1 - 2, 0, 16 * (NG1 // 2))
            group1(NG1 - 1, 1, None)
            group1(NG1, 0, None)

            ve.wait_ge(stats_done, NT)
            ve.wait_ge(kept, NG1)
            ch.mark(ve.tensor_tensor(meanT[:], bn_all[:, :, 1], bn_all[:, :, 4], ALU.add))
            ch.mark(ve.tensor_tensor(difT[:], bn_all[:, :, 1], bn_all[:, :, 4], ALU.subtract))
            ch.link(ve.tensor_tensor(varT[:], bn_all[:, :, 2], bn_all[:, :, 5], ALU.add))
            ch.link(ve.scalar_tensor_tensor(difT[:], difT[:], 0.25, difT[:], ALU.mult, ALU.mult))
            ch.link(ve.scalar_tensor_tensor(varT[:], varT[:], 1.0 / D, difT[:], ALU.mult, ALU.add))
            ve.tensor_scalar(varT[:], varT[:], LN_EPS, None, ALU.add).then_inc(var_ready, 1)
            p0 = prod[:, 0, :, :]
            ch.link(ve.tensor_tensor(p0, awb[:, :, 0:DH], awb[:, :, DH:2 * DH], ALU.add))
            ch.link(ve.tensor_tensor(p0, p0, heads(wbb[:]), ALU.mult))
            ch.link(ve.tensor_reduce(const_s[:], p0, AX.X, ALU.add))
            ch.mark(ve.tensor_tensor(const_s[:], const_s[:], abb[:], ALU.add))
            ve.wait_ge(rstd_ready, 1)
            rb = rstdT[:].unsqueeze(2).to_broadcast([P, NT, H])
            ch.mark(ve.scalar_tensor_tensor(src_tab[:, :, H], meanT[:], -0.5, rstdT[:], ALU.mult, ALU.mult))
            ch.mark(ve.tensor_copy(src_tab[:, :, H + 1], rstdT[:]))
            ch.mark(ve.tensor_tensor(src_tab[:, :, 0:H], raw_s[:, :, H:2 * H], rb, ALU.mult))
            ch.link(ve.tensor_tensor(dst_tab[:], raw_s[:, :, 0:H], rb, ALU.mult))
            ve.tensor_tensor(dst_tab[:], dst_tab[:], const_s[:].unsqueeze(1).to_broadcast([P, NT, H]),
                             ALU.add).then_inc(tables_ready, 1)

            ch.link(ve.tensor_copy(Whi[:], Wsb[:].rearrange("p c h d -> p c (h d)")))
            ch.mark(ve.tensor_tensor(Wlo[:], Wsb[:].rearrange("p c h d -> p c (h d)"), Whi[:].bitcast(F32), ALU.subtract))
            ch.link(ve.tensor_copy(bpart[:, 0, :], wbb[0:3, :]))
            ch.link(ve.tensor_tensor(brest[:], wbb[0:3, :], bpart[:, 0, :], ALU.subtract))
            ch.link(ve.tensor_copy(bpart[:, 1, :], brest[:]))
            ch.link(ve.tensor_tensor(brest[:], brest[:], bpart[:, 1, :], ALU.subtract))
            ch.link(ve.tensor_copy(bpart[:, 2, :], brest[:]))
            ch.link(ve.tensor_scalar(brow[:], bpart[:, 0, :], identF[0:3, 0:1], None, ALU.mult))
            for k in (1, 2):
                ch.link(ve.scalar_tensor_tensor(brow[:], bpart[:, k, :], identF[0:3, k:k + 1], brow[:], ALU.mult, ALU.add))
            ch.link(ve.memset(gcol[:, 0:1], -BIG))
            ch.link(ve.tensor_tensor(gcol[:, 1:ET], dst_f[:, 1:ET], dst_f[:, 0:ET - 1], ALU.is_equal))
            ch.link(ve.tensor_scalar(gcol[:, 1:ET], gcol[:, 1:ET], 1.0, BIG, ALU.subtract, ALU.mult))
            ch.link(ve.tensor_copy(gates[:, :, :, 1:GR + 1],
                                   gcol[:].rearrange("p (g s) -> p g s", s=GR).unsqueeze(2).to_broadcast([P, NG, H, GR])))
            first, last = dst_f[:, 0:1], dst_f[:, ET - 1:ET]
            ch.link(ve.tensor_scalar(headeq[:], dst_f[:], first, 0.0, ALU.is_equal, ALU.add, accum_out=headcnt[:]))
            ch.mark(ve.tensor_copy(fx[:, 0:1], edge_no[:, 0:1]))
            ch.mark(ve.tensor_tensor(fx[:, 1:2], prv_i[:], dst_i[:, 0:1], ALU.is_equal))
            ch.mark(ve.tensor_tensor(fx[:, 2:3], nxt_i[:, ET - 1:ET], dst_i[:, 0:1], ALU.not_equal))
            ch.link(ve.tensor_scalar(fx[:, 3:4], headcnt[:], ET - 0.5, None, ALU.is_lt))
            ch.link(ve.tensor_tensor(fx[:, 4:5], fx[:, 2:3], fx[:, 3:4], ALU.max))
            ch.link(ve.tensor_tensor(fx[:, 5:6], fx[:, 4:5], fx[:, 1:2], ALU.mult))
            ch.link(ve.tensor_scalar(fx[:, 5:6], fx[:, 5:6], 1.0, -float(FAR), ALU.subtract, ALU.mult))
            ch.link(ve.tensor_tensor(fx[:, 6:7], fx[:, 0:1], headcnt[:], ALU.add))
            ch.link(ve.scalar_tensor_tensor(fix_idx[:], fx[:, 6:7], 1.0, fx[:, 5:6], ALU.subtract, ALU.add))
            ch.mark(ve.tensor_copy(dB[:, 0, :], last.to_broadcast([P, P])))
            ch.mark(ve.tensor_copy(dB[:, 1, :], first.to_broadcast([P, P])))
            ve.wait_ge(ffw_in, 32)
            ch.mark(ve.tensor_reduce(asum[0:F, 0:1], up_sb[:], AX.X, ALU.add, apply_absolute_value=True))
            ch.link(ve.tensor_reduce(asum[:, 1:2], dn_sb[:].rearrange("p c f -> p (c f)"), AX.X, ALU.add, apply_absolute_value=True))
            ve.sem_inc(aux_ready, 1)
            ve.wait_ge(aux_done, 1)
            ch.link(ve.tensor_scalar(egate[:], misc_ps[0][:, 0:P], last, 1.0, ALU.is_equal, ALU.subtract))
            ch.mark(ve.tensor_scalar(egate[:], egate[:], BIG, None, ALU.mult))
            ch.mark(ve.scalar_tensor_tensor(cmask[:], misc_ps[0][:, P:2 * P], last, before[:], ALU.is_equal, ALU.mult))
            ve.wait_ge(aux_done, 2)
            ch.link(ve.tensor_scalar(wsc[:], misc_ps[1][:, 0:2], 1.0 / F, Q_EPS, ALU.mult, ALU.max))
            ch.mark(ve.tensor_scalar(whalf[:, 0, :], wsc[:], 0.5, None, ALU.mult))
            ch.mark(ve.tensor_scalar(qsc[:], wsc[:], 1.0 / QMAX, None, ALU.mult))
            ch.link(ve.tensor_scalar(whalf[:, 1, :], wsc[:], -0.5, None, ALU.mult))
            ch.link(ve.tensor_scalar(tern[0:F, :], up_sb[:], whalf[0:F, 1, 0:1], None, ALU.is_lt))
            ch.link(ve.scalar_tensor_tensor(up_t[:], up_sb[:], whalf[0:F, 0, 0:1], tern[0:F, :], ALU.is_gt, ALU.subtract))
            dn2, dt2 = dn_sb[:].rearrange("p c f -> p (c f)"), dn_t[:].rearrange("p c f -> p (c f)")
            ch.link(ve.tensor_scalar(tern[:, 0:C * F], dn2, whalf[:, 1, 1:2], None, ALU.is_lt))
            ch.link(ve.scalar_tensor_tensor(dt2, dn2, whalf[:, 0, 1:2], tern[:, 0:C * F], ALU.is_gt, ALU.subtract))
            ve.sem_inc(aux_ready, 1)

            def low2(t, r):
                ve.wait_ge(hi2_done, t + 1)
                wait(ve, mm_done, t - 1)
                view = (slice(None), r % 2, slice(None), slice(0, P))
                ve.tensor_tensor(xTlo[view], xt_ps[r % 2][:].rearrange("p (c n) -> p c n", c=C), xThi[view].bitcast(F32),
                                 ALU.subtract).then_inc(lo2_done, 1)

            def scores(G, turn, b):
                gate = gates[:, bass.ds(G, 1), :, :].rearrange("p o h s -> p (o h) s")
                s = score[:, b, :, 1:GR + 1]
                m = mrun[:, b, :, :]
                ve.wait_ge(small_got[b], 32 * GR * turn + 32 * GR)
                ch.mark(ve.tensor_copy(score[:, b, :, 0], mrun[:, 1 - b, :, GR]))
                mark = ch.mark(ve.tensor_tensor(s, sdst[:, b, :, :].rearrange("p s h -> p h s"),
                                                ssrc[:, b, :, 0:H].rearrange("p s h -> p h s"), ALU.add))
                yield
                ch.need(mark)
                mark = ch.mark(ve.scalar_tensor_tensor(s, s, 0.2, s, ALU.mult, ALU.max))
                yield
                ch.need(mark)
                mark = ch.mark(ve.tensor_tensor_scan(m.rearrange("p h s -> p (h s)"), gate.rearrange("p h s -> p (h s)"),
                                                     score[:, b, :, :].rearrange("p h s -> p (h s)"), 0.0, ALU.add, ALU.max))
                yield
                ch.need(mark)
                ch.mark(ve.tensor_tensor(expin[:, b, 0, :, :], s, m[:, :, 1:GR + 1], ALU.subtract))
                mark = ch.mark(ve.tensor_tensor(expin[:, b, 1, :, :], m[:, :, 0:GR], gate[:, :, 1:GR + 1], ALU.add))
                yield
                ch.need(mark)
                ve.tensor_tensor(expin[:, b, 1, :, :], expin[:, b, 1, :, :], m[:, :, 1:GR + 1], ALU.subtract).then_inc(scored, 1)
                yield

            def weights(G, turn, b):
                w, c = wc[:, b, 0, :, :], wc[:, b, 1, :, :]
                ve.wait_ge(exped, G + 1)
                mark = ch.mark(ve.tensor_copy(w[:, :, 0], den[:, 1 - b, :, GR]))
                yield
                ch.need(mark)
                mark = ch.mark(ve.tensor_tensor_scan(den[:, b, :, :].rearrange("p h s -> p (h s)"), c.rearrange("p h s -> p (h s)"),
                                                     w.rearrange("p h s -> p (h s)"), 0.0, ALU.mult, ALU.add))
                yield
                wait(ve, rows_out[b], 16 * turn)
                ch.mark(ve.tensor_copy(row[:, b, :, D + H:RW].rearrange("p s h -> p h s"), mrun[:, b, :, 1:GR + 1]))
                ch.need(mark)
                ch.mark(ve.tensor_copy(row[:, b, :, D:D + H].rearrange("p s h -> p h s"), den[:, b, :, 1:GR + 1]))
                yield

            def fold(t, b, r, small, last):
                prev = row[:, b, r - 1, 0:D] if r > 0 else row[:, 1 - b, GR - 1, 0:D]
                if r > 0:
                    ch.need(fold.mark)
                ch.mark(ve.tensor_tensor(heads(carry[:, r % 2, :]), heads(prev), over(wc[:, b, 1, :, r + 1], DH), ALU.mult))
                next(small, None)
                ve.wait_ge(mm_done, t + 1)
                ve.tensor_tensor(heads(vbuf[:, r % 2, :]), heads(proj_ps[r % 2][:]), over(wc[:, b, 0, :, r + 1], DH), ALU.mult).then_inc(v_done, 1)
                if not last or r < GR - 2:
                    low2(t + 2, r)
                else:
                    next(small, None)
                next(small, None)
                ve.wait_ge(v_done, t + 1)
                ins = ve.tensor_tensor(row[:, b, r, 0:D], carry[:, r % 2, :], vbuf[:, r % 2, :], ALU.add)
                if r == GR - 1:
                    ins.then_inc(group_done, 1)
                else:
                    fold.mark = ch.mark(ins)
                    next(small, None)

            def group(G, turn, b, last=False):
                small = iter(()) if last else scores(G + 1, turn + b, 1 - b)
                for r in range(GR):
                    if r == 2:
                        for _ in small:
                            pass
                        small = iter(()) if last else weights(G + 1, turn + b, 1 - b)
                    if r == 0 and (not isinstance(G, int) or G > 0):
                        ve.wait_ge(group_done, G)
                    fold(G * GR + r, b, r, small if r != 2 else iter(()), last)
                for _ in small:
                    pass

            for part in (scores(0, 0, 0), weights(0, 0, 0)):
                for _ in part:
                    pass
            ch.need(ch.base + ch.n)
            low2(0, 0)
            low2(1, 1)
            group(0, 0, 0)
            group(1, 0, 1)
            with ve.Fori(1, NG // 2 - 1) as i:
                ch.enter(i - 1, 34)
                group(2 * i, i, 0)
                group(2 * i + 1, i, 1)
            ch.leave(NG // 2 - 2)
            group(NG - 2, NG // 2 - 1, 0)
            group(NG - 1, NG // 2 - 1, 1, last=True)

            ve.wait_ge(group_done, NG)
            ch.need(ch.base + ch.n)
            mlast, dlast = mrun[:, 1, :, GR], den[:, 1, :, GR]
            ch.link(ve.tensor_copy(mB[:], over(mlast, P)))
            ve.sem_inc(aux_ready, 1)
            ve.wait_ge(aux_done, 3)
            ch.mark(ve.tensor_copy(upT[:].rearrange("p c f -> p (c f)"), misc_ps[0][:].bitcast(BF16)[:, 0:C * F]))
            ch.mark(ve.tensor_copy(dnT[:], misc_ps[1][:].bitcast(BF16)[0:F, 0:D]))
            ve.wait_ge(aux_done, 4)
            for k in range(2):
                v = mB[:, 4 * k:4 * k + 4, :]
                ch.link(ve.tensor_tensor(v, proj_ps[k][:].rearrange("p (h q) -> p h q", h=4),
                                         egate[:].unsqueeze(1).to_broadcast([P, 4, P]), ALU.add))
                ch.link(ve.tensor_reduce(gm[:, 4 * k:4 * k + 4], v, AX.X, ALU.max))
            ve.tensor_tensor(wq_in[:], mlast, gm[:], ALU.subtract).then_inc(cross_in, 1)
            ve.wait_ge(cross_exp, 1)
            ch.mark(ve.tensor_tensor(heads(tailrow[:, 0:D]), heads(row[:, 1, GR - 1, 0:D]), over(wq[:], DH), ALU.mult))
            ch.link(ve.tensor_tensor(tailrow[:, D:D + H], dlast, wq[:], ALU.mult))
            ve.sem_inc(aux_ready, 1)
            ve.wait_ge(aux_done, 5)
            ve.wait_ge(fix_got, 16)
            gmax = sc_ps[0][:, H:2 * H]
            ch.link(ve.tensor_tensor(mtot[:], fixrow[:, D + H:RW], gmax, ALU.max))
            ch.mark(ve.tensor_tensor(ab_in[:, 0, :], fixrow[:, D + H:RW], mtot[:], ALU.subtract))
            ve.tensor_tensor(ab_in[:, 1, :], gmax, mtot[:], ALU.subtract).then_inc(cross_in, 1)
            ve.wait_ge(cross_exp, 2)
            fa = heads(fixrow[:, 0:D])
            ch.mark(ve.tensor_tensor(fa, fa, over(ab[:, 0, :], DH), ALU.mult))
            ch.mark(ve.tensor_tensor(heads(vbuf[:, 0, :]), heads(xt_ps[0][:]), over(ab[:, 1, :], DH), ALU.mult))
            ch.mark(ve.tensor_tensor(fixrow[:, D:D + H], fixrow[:, D:D + H], ab[:, 0, :], ALU.mult))
            ch.link(ve.tensor_tensor(cden[:], sc_ps[0][:, 0:H], ab[:, 1, :], ALU.mult))
            ch.mark(ve.tensor_tensor(fixrow[:, D:D + H], fixrow[:, D:D + H], cden[:], ALU.add))
            ch.link(ve.tensor_tensor(fixrow[:, 0:D], fixrow[:, 0:D], vbuf[:, 0, :], ALU.add))
            ve.sem_inc(fix_ready, 1)

            def step(s, m, turn):
                def on(q):
                    return not isinstance(q, int) or 0 <= q < NQ

                def val(a, k):
                    return qv[:, a, k, :]

                fin, hidden, scale, quant, resid, first = on(s - 5), on(s - 4), on(s - 3), on(s - 2), on(s - 1), on(s)
                a5, a4, a3, a2, a1, a0 = ((m - lag) % QS for lag in (5, 4, 3, 2, 1, 0))
                mk = {}

                h1 = hid2[:, a4 % 2, :, :]

                def resid_tile(k):
                    return ch.mark(ve.scalar_tensor_tensor(y_pair(a1)[:, k, :], x_in[:, a1, k, :], 1.0, rg_pair(a1)[:, k, 0:D],
                                                           ALU.mult, ALU.add, accum_out=ysum[:, a1, k:k + 1]))

                def amax(k):
                    ve.wait_ge(yc_ready, 2 * (s - 2) + 1 + k)
                    return ch.mark(ve.tensor_reduce(qv[:, a2, AMAX, k:k + 1], yc_tile(a2 % 2, k), AX.X, ALU.max,
                                                    apply_absolute_value=True))

                if first:
                    ve.wait_ge(rg_got[a0], 32 * turn(0) + 32)
                    mk["den"] = ch.mark(ve.tensor_scalar(rden[:, a0, :, :], rg_pair(a0)[:, :, D:D + H], 0.5, None, ALU.max))
                if hidden:
                    ve.wait_ge(relu_ready, s - 3)
                    mk["h1"] = ch.mark(ve.tensor_scalar(h1, hid[:, a4 % 2, :, :], QMAX, MAGIC, ALU.min, ALU.add))
                if scale:
                    ve.wait_ge(qs_ready, s - 2)
                    ve.tensor_scalar(qm_tile(a3 % 2, 1), yc_tile(a3 % 2, 1), qv[:, a3, QSC, 1:2], MAGIC,
                                     ALU.mult, ALU.add).then_inc(qm_ready[1], 1)
                if fin:
                    ve.wait_ge(dn_done, s - 4)
                    wait(ve, o_out[a5 % 2], 16 * ((s - 5) // 2) if isinstance(s, int) else 32 * turn.i + 16 * ((m - 5) // 2))
                    ve.scalar_tensor_tensor(o_tile(a5 % 2, 0), proj_ps[0][:], qv[:, a5, SDN, 0:1], y_pair(a5)[:, 0, :],
                                            ALU.mult, ALU.add).then_inc(o_ready[0], 1)
                if first:
                    ch.need(mk["den"])
                    ve.reciprocal(rden[:, a0, :, :], rden[:, a0, :, :]).then_inc(rden_ready, 1)
                if hidden:
                    ch.need(mk["h1"])
                    mk["a3"] = ch.mark(ve.tensor_reduce(val(a4, A3), h1, AX.X, ALU.max))
                if hidden:
                    ch.need(mk["a3"])
                    mk["a3"] = ch.mark(ve.tensor_scalar(val(a4, A3), val(a4, A3), MAGIC, Q_EPS, ALU.subtract, ALU.max))
                    mk["h2"] = ch.mark(ve.tensor_scalar(h1, h1, MAGIC, None, ALU.subtract))
                if quant:
                    amax(0)
                if hidden:
                    ch.need(mk["h2"])
                    mk["ia3"] = ch.mark(ve.reciprocal(val(a4, X2), val(a4, A3)))
                    ch.mark(ve.tensor_scalar(val(a4, SDN), val(a4, A3), qsc[:, 1:2], None, ALU.mult))
                if quant:
                    mk["amax"] = amax(1)
                if hidden:
                    ch.need(mk["ia3"])
                    mk["x2"] = ch.link(ve.tensor_scalar(val(a4, X2), val(a4, X2), QMAX, None, ALU.mult))
                    wait(ve, ht_ready, s - 5)
                    for k in range(2):
                        ins = ve.tensor_scalar(hq[:, a4 % 2, k, 0:F], h1[:, k, :], qv[:, a4, X2, k:k + 1], MAGIC, ALU.mult, ALU.add)
                    ins.then_inc(h_ready, 1)
                if resid:
                    ve.wait_ge(agg_ready, s)
                    ve.wait_ge(x_got4[a1], 16 * turn(1) + 16)
                    resid_tile(0)
                    wait(ve, o_ready[1], s - 4)
                    mk["ysum"] = resid_tile(1)
                if quant:
                    ve.wait_ge(std_ready, s - 1)
                    ch.mark(ve.reciprocal(val(a2, RSTD), std[:, a2, :]))
                    ch.need(mk["amax"])
                    mk["a2"] = ch.mark(ve.scalar_tensor_tensor(val(a2, AMAX), std[:, a2, :], Q_EPS, val(a2, AMAX), ALU.mult, ALU.max))
                if resid:
                    ch.need(mk["ysum"])
                    ve.tensor_scalar(negm[:, a1, :], ysum[:, a1, :], -1.0 / D, None, ALU.mult).then_inc(y_ready, 1)
                if quant:
                    ch.need(mk["a2"])
                    mk["ia2"] = ch.mark(ve.reciprocal(val(a2, IA2), val(a2, AMAX)))
                    ch.mark(ve.scalar_tensor_tensor(val(a2, SUP), val(a2, AMAX), qsc[:, 0:1], val(a2, RSTD), ALU.mult, ALU.mult))
                    ch.need(mk["ia2"])
                    ve.tensor_scalar(val(a2, QSC), val(a2, IA2), QMAX, None, ALU.mult).then_inc(qs_ready, 1)

            class Static:
                def __init__(self, s):
                    self.s = s

                def __call__(self, k):
                    return (self.s - k) // QS

            class Turn:
                def __init__(self, i, m):
                    self.i, self.m = i, m

                def __call__(self, k):
                    return self.i + (self.m - k) // QS

            for s in range(2 * QS):
                step(s, s % QS, Static(s))
            with ve.Fori(2, NQ // QS - 1) as i:
                ch.enter(i - 2, 16 * QS)
                for m in range(QS):
                    step(QS * i + m, m, Turn(i, m))
            ch.leave(NQ // QS - 3)
            for s in range(NQ - QS, NQ + LAGS):
                step(s, s % QS, Static(s))


_INS = ["x", "src", "dst", "L0_gnn_Ws", "L0_gnn_Wb", "L0_gnn_a_w", "L0_gnn_a_b", "L0_ffn_w_up", "L0_ffn_w_down"]


def kernel(**inputs):
    import numpy as np
    import concourse.bacc as bacc
    from concourse.bass_utils import run_bass_kernel_spmd

    nc = bacc.Bacc("TRN2", target_bir_lowering=False, num_devices=1)
    arrays, args = {}, []
    for name in _INS:
        a = np.ascontiguousarray(inputs[name])
        arrays[f"in_{name}"] = a
        args.append(nc.dram_tensor(f"in_{name}", a.shape, mybir.dt.from_np(a.dtype), kind="ExternalInput").ap())
    out = nc.dram_tensor("out", arrays["in_x"].shape, F32, kind="ExternalOutput").ap()
    build(nc, *args, out)
    return run_bass_kernel_spmd(nc, [arrays], core_ids=[0]).results[0]["out"]
```

```python
from contextlib import ExitStack

import concourse.bass as bass
from concourse import mybir

ALU = mybir.AluOpType
ACT = mybir.ActivationFunctionType
AX = mybir.AxisListType
F32 = mybir.dt.float32
F32R = mybir.dt.float32r
BF16 = mybir.dt.bfloat16
I32 = mybir.dt.int32

P = 128
BIG = 1.0e30
FAR = 20000
MAGIC = 1.5 * 2.0 ** 23
LN_EPS = 1e-5
Q_EPS = 1e-5
QMAX = 127.0


def wait(eng, sem, value):
    if isinstance(value, int) and value <= 0:
        return
    eng.wait_ge(sem, value)


class Chain:

    def __init__(self, eng, sem):
        self.eng, self.sem, self.base, self.n = eng, sem, 0, 0

    def mark(self, ins):
        ins.then_inc(self.sem, 1)
        self.n += 1
        return self.base + self.n

    def need(self, mark):
        self.eng.wait_ge(self.sem, mark)

    def link(self, ins):
        self.need(self.mark(ins))

    def enter(self, turn, per):
        self.start, self.per = self.base + self.n, per
        self.base, self.n = turn * per + self.start, 0

    def leave(self, turns):
        assert self.n == self.per, f"a turn of the loop marks {self.n} results, not {self.per}"
        self.base, self.n = self.start + turns * self.per, 0


def build(nc, x, src, dst, Ws, Wb, a_w, a_b, w_up, w_down, out):
    N, D = x.shape
    H, _, DH = Ws.shape
    F = w_up.shape[0]
    E = src.shape[0]
    C = D // P
    ET = 80
    EP = E // ET
    GR = 4
    NG = ET // GR
    FULL = N // P
    TAIL0 = N - P
    TN = N - FULL * P
    NT = 80
    RW = D + 2 * H
    SW = H + 2
    NQ = NT // 2
    QS = 4
    NG1 = NT // GR
    assert EP * ET == E and H * DH == D and C * P == D and FULL == NT - 2

    rows = nc.dram_tensor("edge_rows", (P * ET + P, RW), F32, kind="Internal").ap()
    dst_table = nc.dram_tensor("dst_table", (N, H), F32, kind="Internal").ap()
    src_table = nc.dram_tensor("src_table", (N, SW), F32, kind="Internal").ap()
    last_edge = nc.dram_tensor("last_edge", (N, 1), I32, kind="Internal").ap()

    with ExitStack() as ctx:
        def sb(name, shape, dt=F32):
            return ctx.enter_context(nc.sbuf_tensor(name, shape, dt))

        def sem(name):
            return ctx.enter_context(nc.semaphore(name))

        bank = [ctx.enter_context(nc.psum_tensor(f"bank{i}", [P, 512], F32)) for i in range(8)]
        xt_ps = bank[0:4]
        proj_ps = bank[2:4]
        sc_ps = bank[4:6]
        misc_ps = bank[6:8]

        identF = sb("identF", [P, P])
        identB = sb("identB", [P, P], BF16)
        shift = sb("shift", [P, P])
        before = sb("before", [P, P])
        inv_d = sb("inv_d", [P, P])
        epsT = sb("epsT", [P, 1])
        warm = sb("warm", [P, 2])
        magicN = sb("magicN", [P, 1])
        onesB = sb("onesB", [P, P], BF16)

        Wsb = sb("Wsb", [P, C, H, DH])
        awb = sb("awb", [P, H, 2 * DH])
        wbb = sb("wbb", [P, D])
        abb = sb("abb", [P, H])
        prod = sb("prod", [P, C, H, DH])
        Whi = sb("Whi", [P, C, D], F32R)
        Wlo = sb("Wlo", [P, C, D], F32R)
        wts = sb("wts", [P, C, 2 * H])
        wparts = sb("wparts", [P, C, 4 * H], F32R)
        fold2 = sb("fold2", [4 * H, 2 * H])
        s_sb = sb("s_sb", [4 * H, 2, GR * P])
        zrow = sb("zrow", [P, RW])
        const_s = sb("const_s", [P, H])
        bpart = sb("bpart", [1, 3, D], BF16)
        brest = sb("brest", [1, D])
        brow = sb("brow", [3, D], BF16)

        dst_i = sb("dst_i", [P, ET], I32)
        nxt_i = sb("nxt_i", [P, ET], I32)
        prv_i = sb("prv_i", [P, 1], I32)
        src_i = sb("src_i", [P, ET], I32)
        gather_i = sb("gather_i", [P, NG, 2, GR], I32)
        dst_f = sb("dst_f", [P, ET])
        same_next = sb("same_next", [P, ET])
        edge_no = sb("edge_no", [P, ET], I32)
        scat = sb("scat", [P, ET, 2], I32)
        gcol = sb("gcol", [P, ET])
        gates = sb("gates", [P, NG, H, GR + 1])
        headeq = sb("headeq", [P, ET])
        headcnt = sb("headcnt", [P, 1])
        fx = sb("fx", [P, 8])
        fix_idx = sb("fix_idx", [P, 1], I32)
        zero_i = sb("zero_i", [P, FULL], I32)
        scat_ring = sb("scat_ring", [P, 2, GR, 2], I32)
        idx_ring = sb("idx_ring", [P, 2, 2, GR], I32)
        last_sb = sb("last_sb", [P, NT], I32)
        last_ring = sb("last_ring", [P, QS, 2], I32)

        x_in = sb("x_in", [P, QS, 2, D])
        xThi = sb("xThi", [P, 2, C, GR * P], F32R)
        xTlo = sb("xTlo", [P, 2, C, GR * P], F32R)
        bn_all = sb("bn_all", [P, NG1, GR - 1, 6])
        xsum = sb("xsum", [P, NG1])
        xneg = sb("xneg", [P, NG1])
        xsq = sb("xsq", [P, NG1])
        junk = sb("junk", [P, 2, D])
        raw_s = sb("raw_s", [P, NT, 2 * H])
        meanT = sb("meanT", [P, NT])
        varT = sb("varT", [P, NT])
        difT = sb("difT", [P, NT])
        stdT = sb("stdT", [P, NT])
        rstdT = sb("rstdT", [P, NT])
        dst_tab = sb("dst_tab", [P, NT, H])
        src_tab = sb("src_tab", [P, NT, SW])

        xg = sb("xg", [P, 2, GR, D])
        sdst = sb("sdst", [P, 2, GR, H])
        ssrc = sb("ssrc", [P, 2, GR, SW])
        xn = sb("xn", [P, 2, D])
        score = sb("score", [P, 2, H, GR + 1])
        mrun = sb("mrun", [P, 2, H, GR + 1])
        expin = sb("expin", [P, 2, 2, H, GR])
        wc = sb("wc", [P, 2, 2, H, GR + 1])
        den = sb("den", [P, 2, H, GR + 1])
        vbuf = sb("vbuf", [P, 2, D])
        carry = sb("carry", [P, 2, D])
        row = sb("row", [P, 2, GR, RW])

        mB = sb("mB", [P, H, P])
        dB = sb("dB", [P, 2, P])
        egate = sb("egate", [P, P])
        cmask = sb("cmask", [P, P])
        gm = sb("gm", [P, H])
        wq_in = sb("wq_in", [P, H])
        wq = sb("wq", [P, H])
        tailrow = sb("tailrow", [P, D + H])
        fixrow = sb("fixrow", [P, RW])
        mtot = sb("mtot", [P, H])
        ab_in = sb("ab_in", [P, 2, H])
        ab = sb("ab", [P, 2, H])
        cden = sb("cden", [P, H])

        up_sb = sb("up_sb", [F, D])
        dn_sb = sb("dn_sb", [P, C, F])
        asum = sb("asum", [P, 2])
        wsc = sb("wsc", [P, 2])
        whalf = sb("whalf", [P, 2, 2])
        qsc = sb("qsc", [P, 2])
        tern = sb("tern", [P, D], BF16)
        up_t = sb("up_t", [F, D], BF16)
        dn_t = sb("dn_t", [P, C, F], BF16)
        upT = sb("upT", [P, C, F], BF16)
        dnT = sb("dnT", [F, D], BF16)

        prod2 = xg[:, 1, :, :].rearrange("p c (h d) -> p c h d", h=H)

        f1 = wbb[:]
        rg = row
        ybuf = xg
        obuf = prod
        rden = sb("rden", [P, QS, 2, H])
        ysum = sb("ysum", [P, QS, 2])
        sqsum = sb("sqsum", [P, QS, 2])
        negm = sb("negm", [P, QS, 2])
        std = sb("std", [P, QS, 2])
        qT = sb("qT", [P, 2, D], BF16)
        qv = sb("qv", [P, QS, 8, 2])
        hid = sb("hid", [P, 2, 2, F])
        hid2 = sb("hid2", [P, 2, 2, F])
        hq = sb("hq", [P, 2, 2, P])
        hqT = sb("hqT", [F, 2, 2 * P], BF16)

        W_in = [sem(f"W_in{c}") for c in range(C)]
        aw_in = sem("aw_in")
        bias_in = sem("bias_in")
        ffw_in = sem("ffw_in")
        idx_in = sem("idx_in")
        pads_set = sem("pads_set")
        consts_set = sem("consts_set")
        fill_out = sem("fill_out")
        x_got1 = [sem(f"x_got1_{i}") for i in range(QS)]
        src_table_out = sem("src_table_out")
        dst_table_out = sem("dst_table_out")
        last_in = sem("last_in")
        dve_chain = sem("dve_chain")
        pool_chain = sem("pool_chain")
        pool_gate = sem("pool_gate")
        scat_done = [sem(f"scat_done{i}") for i in range(2)]
        scat_ready = sem("scat_ready")
        prod2_ready = sem("prod2_ready")
        Whi_ready = sem("Whi_ready")
        Wlo_ready = sem("Wlo_ready")
        bparts_ready = sem("bparts_ready")
        brow_in = sem("brow_in")
        gcol_ready = sem("gcol_ready")
        gates_ready = sem("gates_ready")
        wsum_ready = sem("wsum_ready")
        wmean_ready = sem("wmean_ready")
        wts_ready = sem("wts_ready")
        t1_done = sem("t1_done")
        hi1_done = sem("hi1_done")
        lo1_done = sem("lo1_done")
        s1_done = sem("s1_done")
        s1_copied = sem("s1_copied")
        back_done = sem("back_done")
        kept = sem("kept")
        stats_done = sem("stats_done")
        sum1_done = sem("sum1_done")
        neg1_done = sem("neg1_done")
        sq1_done = sem("sq1_done")
        var_ready = sem("var_ready")
        std1_ready = sem("std1_ready")
        tables_ready = sem("tables_ready")
        x_got2 = [[sem(f"x_got2_{i}_{r}") for r in range(GR)] for i in range(2)]
        src_got = [sem(f"src_got{i}") for i in range(2)]
        dst_got = [sem(f"dst_got{i}") for i in range(2)]
        normed = sem("normed")
        scored = sem("scored")
        exped = sem("exped")
        t2_done = sem("t2_done")
        hi2_done = sem("hi2_done")
        lo2_done = sem("lo2_done")
        mm_done = sem("mm_done")
        v_done = sem("v_done")
        group_done = sem("group_done")
        rows_out = [sem(f"rows_out{i}") for i in range(2)]
        aux_ready = sem("aux_ready")
        aux_done = sem("aux_done")
        most_done = sem("most_done")
        mB_ready = sem("mB_ready")
        tern_ready = sem("tern_ready")
        cross_in = sem("cross_in")
        cross_exp = sem("cross_exp")
        fix_got = sem("fix_got")
        fix_ready = sem("fix_ready")
        fix_out = sem("fix_out")
        x_got4 = [sem(f"x_got4_{i}") for i in range(QS)]
        rg_got = [sem(f"rg_got{i}") for i in range(QS)]
        rden_ready = sem("rden_ready")
        agg_ready = sem("agg_ready")
        y_ready = sem("y_ready")
        yc_ready = sem("yc_ready")
        sq_done = sem("sq_done")
        std_ready = sem("std_ready")
        qs_ready = sem("qs_ready")
        qm_ready = [sem(f"qm_ready{k}") for k in range(2)]
        qt_ready = sem("qt_ready")
        qt_copied = sem("qt_copied")
        up_done = sem("up_done")
        relu_ready = sem("relu_ready")
        h1_ready = sem("h1_ready")
        h2_ready = sem("h2_ready")
        h_ready = sem("h_ready")
        ht_ready = sem("ht_ready")
        ht_copied = sem("ht_copied")
        dn_done = sem("dn_done")
        f1_ready = sem("f1_ready")
        o_ready = [sem(f"o_ready{k}") for k in range(2)]
        o_out = [sem(f"o_out{i}") for i in range(2)]
        tail_out = sem("tail_out")

        x_main = x[0:FULL * P, :].rearrange("(p j) d -> p j d", j=FULL)
        out_main = out[0:FULL * P, :].rearrange("(p j) d -> p j d", j=FULL)
        rows_v = rows[0:P * ET, :].rearrange("(p t) w -> p t w", t=ET)
        block = ctx.enter_context(nc.Block())

        AMAX, RSTD, IA2, QSC, SUP, A3, X2, SDN = range(8)
        LAGS = 5

        def o_tile(b, k):
            return obuf[:, 2 * b + k, :, :].rearrange("p h d -> p (h d)")

        def o_pair(b):
            return obuf[:, 2 * b:2 * b + 2, :, :].rearrange("p k h d -> p k (h d)")

        def rg_pair(a):
            return rg[:, a // 2, 2 * (a % 2):2 * (a % 2) + 2, :]

        def y_pair(a):
            return ybuf[:, a // 2, 2 * (a % 2):2 * (a % 2) + 2, :]

        def yc_tile(b, k):
            return Wsb[:, 2 * b + k, :, :].rearrange("p h d -> p (h d)")

        def qm_tile(b, k):
            return (vbuf, carry)[b][:, k, :]

        def sq_tile(k):
            return xn[:, k, :]

        def heads(ap):
            return ap.rearrange("p (h d) -> p h d", h=H)

        def over(ap, n):
            return ap.unsqueeze(2).to_broadcast([P, H, n])

        @block.sync
        def _(sp):
            def load(tile, slot, got):
                if isinstance(tile, int) and tile == NT - 2:
                    sp.dma_start(x_in[:, slot, 0, :], x[TAIL0:N, :]).then_inc(got[slot], 16)
                else:
                    sp.dma_start(x_in[:, slot, :, :], x_main[:, bass.ds(tile, 2), :]).then_inc(got[slot], 16)

            def refill1(q, slot):
                sp.wait_ge(lo1_done, 2 * q - 2 * QS + 2)
                if slot % 2 == 1:
                    sp.wait_ge(sq1_done, 2 * q - 2 * QS + 2)
                load(2 * q, slot, x_got1)

            for q in range(2):
                load(2 * q, q, x_got1)
            sp.wait_ge(pads_set, 6)
            dst2 = dst.rearrange("(p t) -> p t", t=ET)
            sp.dma_start(dst_i[0:EP, :], dst2).then_inc(idx_in, 16)
            sp.dma_start(src_i[0:EP, :], src.rearrange("(p t) -> p t", t=ET)).then_inc(idx_in, 16)
            sp.dma_start(nxt_i[0:EP - 1, :], dst[1:1 + (EP - 1) * ET].rearrange("(p t) -> p t", t=ET)).then_inc(idx_in, 16)
            sp.dma_start(nxt_i[EP - 1:EP, 0:ET - 1], dst[1 + (EP - 1) * ET:E].rearrange("(p t) -> p t", p=1)).then_inc(idx_in, 16)
            sp.dma_start(prv_i[1:EP, :], dst2[0:EP - 1, ET - 1:ET], allow_slow_non_contiguous=True).then_inc(idx_in, 16)
            sp.dma_start(awb[:].rearrange("p h d -> p (h d)"), a_w.rearrange("h d -> (h d)").partition_broadcast(P)).then_inc(aw_in, 16)
            for c in range(C):
                sp.dma_start(Wsb[:, c, :, :], Ws[:, c * P:(c + 1) * P, :].rearrange("h k d -> k h d")).then_inc(W_in[c], 16)
            sp.dma_start(wbb[:], Wb.rearrange("h d -> (h d)").partition_broadcast(P)).then_inc(bias_in, 16)
            sp.dma_start(abb[:], a_b.partition_broadcast(P)).then_inc(bias_in, 16)
            for q in range(2, QS):
                load(2 * q, q, x_got1)
            sp.dma_start(up_sb[:], w_up).then_inc(ffw_in, 16)
            sp.dma_start(dn_sb[:], w_down.rearrange("(c k) f -> k c f", k=P)).then_inc(ffw_in, 16)
            with sp.Fori(1, NQ // QS - 1) as i:
                for slot in range(QS):
                    refill1(QS * i + slot, slot)
            for slot in range(QS):
                refill1(NQ - QS + slot, slot)

            sp.wait_ge(bparts_ready, 1)
            for k in range(3):
                sp.dma_start(brow[k:k + 1, :], bpart[:, k, :]).then_inc(brow_in, 16)
            sp.wait_ge(tables_ready, 1)
            for tab, sbt, done in ((src_table, src_tab, src_table_out), (dst_table, dst_tab, dst_table_out)):
                sp.dma_start(tab[0:FULL * P, :].rearrange("(p j) w -> p j w", j=FULL), sbt[:, 0:FULL, :]).then_inc(done, 16)
                sp.dma_start(tab[FULL * P:N, :], sbt[P - TN:P, FULL, :]).then_inc(done, 16)
            def rows_store(G, b):
                sp.wait_ge(group_done, G + 1)
                sp.dma_start(rows_v[:, bass.ds(G * GR, GR), :], row[:, b, :, :]).then_inc(rows_out[b], 16)

            for b in range(2):
                rows_store(b, b)
            for q in range(QS):
                load(2 * q, q, x_got4)
            with sp.Fori(1, NG // 2 - 1) as i:
                for b in range(2):
                    rows_store(2 * i + b, b)
            rows_store(NG - 2, 0)
            sp.wait_ge(most_done, 1)
            sp.dma_start(rows_v[:, ET - GR:ET - 2, :], row[:, 1, 0:GR - 2, :]).then_inc(rows_out[1], 16)
            sp.wait_ge(most_done, 2)
            sp.dma_start(rows_v[:, ET - 2, :], row[:, 1, GR - 2, :]).then_inc(rows_out[1], 16)
            sp.wait_ge(group_done, NG)
            sp.dma_start(rows_v[:, ET - 1, :], row[:, 1, GR - 1, :]).then_inc(rows_out[1], 16)
            for r in range(2):
                sp.wait_ge(scat_done[r], 16 * ET // 2)
            sp.dma_start(last_sb[:, 0:FULL], last_edge[0:FULL * P, :].rearrange("(p j) o -> p (j o)", j=FULL)).then_inc(last_in, 16)
            sp.dma_start(last_sb[:, FULL:FULL + 1], last_edge[TAIL0:N, :]).then_inc(last_in, 16)

            def store(q, b):
                sp.wait_ge(o_ready[0], q + 1)
                sp.wait_ge(o_ready[1], q + 1)
                sp.dma_start(out_main[:, bass.ds(2 * q, 2), :], o_pair(b)).then_inc(o_out[b], 16)

            def refill4(q, slot):
                sp.wait_ge(y_ready, q - QS + 1)
                load(2 * q, slot, x_got4)

            with sp.Fori(1, NQ // QS - 1) as i:
                for slot in range(QS):
                    refill4(QS * i + slot, slot)
                    store(QS * i + slot - QS, slot % 2)
            for slot in range(QS):
                refill4(NQ - QS + slot, slot)
                store(NQ - 2 * QS + slot, slot % 2)
            for q in range(NQ - QS, NQ - 1):
                store(q, q % 2)
            sp.wait_ge(o_ready[0], NQ)
            sp.dma_start(out[FULL * P:N, :], o_tile((NQ - 1) % 2, 0)[P - TN:P, :]).then_inc(tail_out, 16)
            sp.wait_ge(o_out[0], 16 * (NQ // 2))
            sp.wait_ge(o_out[1], 16 * (NQ // 2 - 1))
            sp.wait_ge(tail_out, 16)

        @block.gpsimd
        def _(gp):
            ch = Chain(gp, pool_chain)
            lim_nodes = gp.to_reg(N - 1)
            lim_rows = gp.to_reg(P * ET + P - 1)
            gp.memset(dst_i[:], FAR).then_inc(pads_set, 1)
            gp.memset(nxt_i[:], FAR + 1).then_inc(pads_set, 1)
            gp.memset(prv_i[:], -1).then_inc(pads_set, 1)
            gp.memset(src_i[:], 0).then_inc(pads_set, 1)
            gp.iota(zero_i[:], [[0, FULL]], base=P * ET, channel_multiplier=1).then_inc(pads_set, 1)
            gp.memset(zrow[:], 0.0).then_inc(pads_set, 1)
            gp.iota(edge_no[:], [[1, ET]], base=0, channel_multiplier=ET).then_inc(consts_set, 1)
            ch.mark(gp.memset(identF[:], 0.0))
            ch.mark(gp.memset(shift[:], 0.0))
            ch.link(gp.memset(before[:], 1.0))
            gp.affine_select(out=identF[:], in_=identF[:], compare_op=ALU.not_equal, fill=1.0, base=0,
                             pattern=[[-1, P]], channel_multiplier=1).then_inc(consts_set, 1)
            gp.affine_select(out=shift[:], in_=shift[:], compare_op=ALU.not_equal, fill=1.0, base=-1,
                             pattern=[[1, P]], channel_multiplier=-1).then_inc(consts_set, 1)
            gp.affine_select(out=before[:], in_=before[:], compare_op=ALU.is_gt, fill=0.0, base=0,
                             pattern=[[1, P]], channel_multiplier=-1).then_inc(consts_set, 1)

            gp.wait_ge(pads_set, 6)
            gp.dma_start(last_edge[0:FULL * P, :].rearrange("(p j) o -> p (j o)", j=FULL), zero_i[:]).then_inc(fill_out, 16)
            gp.dma_start(last_edge[FULL * P:N, :], zero_i[0:TN, 0:1]).then_inc(fill_out, 16)
            gp.dma_start(rows[P * ET:P * ET + P, :], zrow[:]).then_inc(fill_out, 16)

            gp.wait_ge(aw_in, 16)
            for c in range(C):
                gp.wait_ge(W_in[c], 16)
                gp.tensor_tensor(prod2[:, c, :, :], Wsb[:, c, :, :], awb[:, :, DH:2 * DH], ALU.mult).then_inc(prod2_ready, 1)

            gp.wait_ge(scat_ready, 1)
            gp.wait_ge(fill_out, 48)

            LATE = 2

            def scatter_turn(i):
                for r in range(2):
                    if isinstance(i, int):
                        col = slice(i * 2 * GR + r * GR, i * 2 * GR + r * GR + GR)
                    else:
                        col = bass.ds(gp.snap(i * 2 * GR + r * GR), GR)
                    wait(gp, scat_done[r], i * (16 * GR))
                    ch.link(gp.tensor_copy(scat_ring[:, r, :, :], scat[:, col, :]))
                    gp.sem_inc(pool_gate, 1)
                    for k in range(GR):
                        gp.indirect_dma_start(last_edge, bass.IndirectOffsetOnAxis(ap=scat_ring[:, r, k, 0:1], axis=0),
                                              scat_ring[:, r, k, 1:2], None,
                                              bounds_check=lim_nodes, oob_is_err=False).then_inc(scat_done[r], 16)

            scatter_turn(0)
            with gp.Fori(1, ET // (2 * GR) - LATE) as i:
                ch.enter(i - 1, 2)
                scatter_turn(i)
            ch.leave(ET // (2 * GR) - LATE - 1)

            def take_indices(G, b):
                one = slice(G, G + 1) if isinstance(G, int) else bass.ds(gp.snap(G), 1)
                ch.link(gp.tensor_copy(idx_ring[:, b, :, :], gather_i[:, one, :, :].rearrange("p o w s -> p (o w) s")))
                gp.sem_inc(pool_gate, 1)

            def gather_x(b):
                for r in range(GR):
                    gp.indirect_dma_start(xg[:, b, r, :], None, x, bass.IndirectOffsetOnAxis(ap=idx_ring[:, b, 1, r:r + 1], axis=0),
                                          bounds_check=lim_nodes, oob_is_err=False).then_inc(x_got2[b][r], 16)

            def gather_src(b):
                for r in range(GR):
                    gp.indirect_dma_start(ssrc[:, b, r, :], None, src_table, bass.IndirectOffsetOnAxis(ap=idx_ring[:, b, 1, r:r + 1], axis=0),
                                          bounds_check=lim_nodes, oob_is_err=False).then_inc(src_got[b], 16)

            def gather_dst(b):
                for r in range(GR):
                    gp.indirect_dma_start(sdst[:, b, r, :], None, dst_table, bass.IndirectOffsetOnAxis(ap=idx_ring[:, b, 0, r:r + 1], axis=0),
                                          bounds_check=lim_nodes, oob_is_err=False).then_inc(dst_got[b], 16)

            gp.wait_ge(wsum_ready, 1)
            for b in range(2):
                take_indices(b, b)
                gather_x(b)
            gp.wait_ge(Whi_ready, 1)
            gp.tensor_tensor(Wlo[:], Wsb[:].rearrange("p c h d -> p c (h d)"), Whi[:].bitcast(F32), ALU.subtract).then_inc(Wlo_ready, 1)
            gp.wait_ge(bias_in, 32)
            gp.sem_inc(pool_gate, 1)
            ch.link(gp.tensor_copy(bpart[:, 0, :], wbb[0:1, :]))
            ch.link(gp.tensor_tensor(brest[:], wbb[0:1, :], bpart[:, 0, :], ALU.subtract))
            ch.link(gp.tensor_copy(bpart[:, 1, :], brest[:]))
            ch.link(gp.tensor_tensor(brest[:], brest[:], bpart[:, 1, :], ALU.subtract))
            gp.tensor_copy(bpart[:, 2, :], brest[:]).then_inc(bparts_ready, 1)
            gp.wait_ge(gcol_ready, 1)
            ch.link(gp.memset(gates[:], -BIG))
            gp.tensor_copy(gates[:, :, :, 1:GR + 1],
                           gcol[:].rearrange("p (g s) -> p g s", s=GR).unsqueeze(2).to_broadcast([P, NG, H, GR])).then_inc(gates_ready, 1)
            for b in range(2):
                if b == 0:
                    gp.wait_ge(src_table_out, 32)
                    gp.sem_inc(pool_gate, 1)
                gather_src(b)
                if b == 0:
                    gp.wait_ge(dst_table_out, 32)
                    gp.sem_inc(pool_gate, 1)
                gather_dst(b)
            with gp.Fori(1, NG // 2) as i:
                ch.enter(i - 1, 2)
                for b in range(2):
                    G = 2 * i + b
                    gp.wait_ge(scored, G - 1)
                    gp.wait_ge(normed, (G - 1) * GR)
                    take_indices(G, b)
                    gather_src(b)
                    gather_dst(b)
                    gather_x(b)
            ch.leave(NG // 2 - 1)

            for i in range(ET // (2 * GR) - LATE, ET // (2 * GR)):
                scatter_turn(i)
            ch.link(gp.memset(fixrow[:], 0.0))
            gp.wait_ge(rows_out[0], 16 * (NG // 2))
            gp.wait_ge(rows_out[1], 16 * (NG // 2 - 1) + 16 * 3)
            gp.sem_inc(pool_gate, 1)
            gp.indirect_dma_start(fixrow[:], None, rows, bass.IndirectOffsetOnAxis(ap=fix_idx[:], axis=0),
                                  bounds_check=lim_rows, oob_is_err=False).then_inc(fix_got, 16)
            gp.wait_ge(fix_ready, 1)
            gp.sem_inc(pool_gate, 1)
            gp.indirect_dma_start(rows, bass.IndirectOffsetOnAxis(ap=fix_idx[:], axis=0), fixrow[:], None,
                                  bounds_check=lim_rows, oob_is_err=False).then_inc(fix_out, 16)
            gp.wait_ge(last_in, 32)
            gp.wait_ge(fix_out, 16)

            def fetch(q, a):
                col = slice(2 * q, 2 * q + 2) if isinstance(q, int) else bass.ds(gp.snap(2 * q), 2)
                wait(gp, y_ready, q - QS + 1)
                ch.link(gp.tensor_copy(last_ring[:, a, :], last_sb[:, col]))
                gp.sem_inc(pool_gate, 1)
                for k in range(2):
                    gp.indirect_dma_start(rg_pair(a)[:, k, :], None, rows, bass.IndirectOffsetOnAxis(ap=last_ring[:, a, k:k + 1], axis=0),
                                          bounds_check=lim_rows, oob_is_err=False).then_inc(rg_got[a], 16)

            def divide(q, a):
                wait(gp, rden_ready, q + 1)
                v = rg_pair(a)[:, :, 0:D].rearrange("p k (h d) -> p k h d", h=H)
                gp.tensor_tensor(v, v, rden[:, a, :, :].unsqueeze(3).to_broadcast([P, 2, H, DH]), ALU.mult).then_inc(agg_ready, 1)

            def output(q, a, stores):
                gp.wait_ge(f1_ready, q + 1)
                b = a % 2
                wait(gp, o_out[b], stores)
                gp.tensor_tensor(o_tile(b, 1), f1, y_pair(a)[:, 1, :], ALU.add).then_inc(o_ready[1], 1)

            AHEAD = 2

            def step(s, m, i=None):
                first = isinstance(s, int) and s == 0
                if first:
                    divide(s, m)
                if not isinstance(s, int) or s + AHEAD < NQ:
                    fetch(s + AHEAD, (m + AHEAD) % QS)
                if not isinstance(s, int) or 5 <= s:
                    output(s - 5, (m - 5) % QS, 16 * ((s - 5) // 2) if i is None else 32 * i + 16 * ((m - 5) // 2))
                if not isinstance(s, int) or 0 < s < NQ:
                    divide(s, m)

            for q in range(AHEAD):
                fetch(q, q)
            for s in range(2 * QS):
                step(s, s % QS)
            with gp.Fori(2, NQ // QS - 1) as i:
                ch.enter(i - 2, QS)
                for m in range(QS):
                    step(QS * i + m, m, i)
            ch.leave(NQ // QS - 3)
            for s in range(NQ - QS, NQ + LAGS):
                step(s, s % QS)

        @block.scalar
        def _(act):
            def high1(t, b, r):
                act.wait_ge(t1_done, t + 1)
                act.activation(xThi[:, b, :, r * P:(r + 1) * P], xt_ps[r][:].rearrange("p (c n) -> p c n", c=C),
                               ACT.Copy).then_inc(hi1_done, 1)

            def scores1(g, b):
                act.wait_ge(s1_done, g + 1)
                wait(act, back_done, g - 1)
                act.activation(s_sb[:, b, :], sc_ps[b][0:4 * H, :], ACT.Copy).then_inc(s1_copied, 1)

            def group1(g, b):
                more, last = not isinstance(g, int) or g + 1 < NG1, x_in[:, 2 * (1 - b) + 1, 1, :]

                def col(tab):
                    return tab[:, bass.ds(g + 1, 1)]

                if more:
                    for r in range(GR):
                        wait(act, s1_done, g)
                        high1(GR * (g + 1) + r, 1 - b, r)
                        if r == GR - 2:
                            act.activation(junk[:, 0, :], last, ACT.Identity, accum_out=col(xsum)).then_inc(sum1_done, 1)
                    act.wait_ge(sum1_done, g + 2)
                    act.activation(col(xneg), col(xsum), ACT.Copy, scale=-1.0 / D).then_inc(neg1_done, 1)
                if not isinstance(g, int) or g >= 0:
                    scores1(g, b)
                if more:
                    act.wait_ge(neg1_done, g + 2)
                    act.activation(junk[:, 1, :], last, ACT.Square, bias=col(xneg), accum_out=col(xsq)).then_inc(sq1_done, GR)

            group1(-1, 1)
            for c in range(C):
                act.wait_ge(W_in[c], 16)
            act.activation(Whi[:], Wsb[:].rearrange("p c h d -> p c (h d)"), ACT.Copy).then_inc(Whi_ready, 1)
            group1(0, 0)
            group1(1, 1)
            with act.Fori(1, NG1 // 2 - 1) as i:
                group1(2 * i, 0)
                group1(2 * i + 1, 1)
            group1(NG1 - 2, 0)
            act.wait_ge(var_ready, 1)
            act.activation(stdT[:], varT[:], ACT.Sqrt, bias=epsT[:]).then_inc(std1_ready, 1)
            group1(NG1 - 1, 1)
            act.activation(warm[:, 0:1], epsT[:], ACT.Exp)

            def norm_tile(t, turn, b, r):
                act.wait_ge(x_got2[b][r], 16 * turn + 16)
                act.wait_ge(src_got[b], 16 * GR * turn + 16 * GR)
                wait(act, t2_done, t - 1)
                act.activation(xn[:, r % 2, :], xg[:, b, r, :], ACT.Identity, bias=ssrc[:, b, r, H:H + 1],
                               scale=ssrc[:, b, r, H + 1:H + 2]).then_inc(normed, 1)

            def high2(t, r):
                act.wait_ge(t2_done, t + 1)
                wait(act, mm_done, t - 1)
                act.activation(xThi[:, r % 2, :, 0:P], xt_ps[r % 2][:].rearrange("p (c n) -> p c n", c=C),
                               ACT.Copy).then_inc(hi2_done, 1)

            def exps(G, b):
                act.wait_ge(scored, G + 1)
                act.activation(wc[:, b, :, :, 1:GR + 1], expin[:, b, :, :, :], ACT.Exp).then_inc(exped, 1)

            norm_tile(0, 0, 0, 0)

            def group(G, turn, b, last=False):
                for r in range(GR):
                    t = G * GR + r
                    high2(t, r)
                    if r < GR - 1:
                        norm_tile(t + 1, turn, b, r + 1)
                    elif not last:
                        norm_tile(t + 1, turn + b, 1 - b, 0)
                    if r == 0 and isinstance(G, int) and G == 0:
                        exps(0, 0)
                    if r == GR - 1 and not last:
                        exps(G + 1, 1 - b)

            group(0, 0, 0)
            group(1, 0, 1)
            with act.Fori(1, NG // 2 - 1) as i:
                group(2 * i, i, 0)
                group(2 * i + 1, i, 1)
            group(NG - 2, NG // 2 - 1, 0)
            act.wait_ge(scored, NG)
            act.activation(mB[:], over(mrun[:, 1, :, GR], P), ACT.Copy).then_inc(mB_ready, 1)
            group(NG - 1, NG // 2 - 1, 1, last=True)

            act.wait_ge(aux_done, 3)
            act.activation(upT[:].rearrange("p c f -> p (c f)"), misc_ps[0][:].bitcast(BF16)[:, 0:C * F], ACT.Copy).then_inc(tern_ready, 1)
            act.activation(dnT[:], misc_ps[1][:].bitcast(BF16)[0:F, 0:D], ACT.Copy).then_inc(tern_ready, 1)
            act.wait_ge(cross_in, 1)
            act.activation(wq[:], wq_in[:], ACT.Exp).then_inc(cross_exp, 1)
            act.wait_ge(cross_in, 2)
            act.activation(ab[:], ab_in[:], ACT.Exp).then_inc(cross_exp, 1)
            act.activation(warm[:, 1:2], epsT[:], ACT.Sqrt)

            def step(s, m):
                def on(q):
                    return not isinstance(q, int) or 0 <= q < NQ

                q3, a3, q2, a2, q4, a4 = s - 3, (m - 3) % QS, s - 2, (m - 2) % QS, s - 4, (m - 4) % QS

                def square(k):
                    ins = act.activation(sq_tile(k), y_pair(a2)[:, k, :], ACT.Square,
                                         bias=negm[:, a2, k:k + 1], accum_out=sqsum[:, a2, k:k + 1])
                    if k == 1:
                        ins.then_inc(sq_done, 1)

                if on(q2):
                    act.wait_ge(y_ready, q2 + 1)
                    for k in range(2):
                        act.activation(yc_tile(a2 % 2, k), y_pair(a2)[:, k, :], ACT.Identity,
                                       bias=negm[:, a2, k:k + 1]).then_inc(yc_ready, 1)
                if on(q4):
                    act.wait_ge(h1_ready, q4 + 1)
                    act.activation(hid[:, a4 % 2, :, :], hid2[:, a4 % 2, :, :], ACT.Identity, bias=magicN[:]).then_inc(h2_ready, 1)
                q5, a5 = s - 5, (m - 5) % QS
                if on(q5):
                    act.wait_ge(dn_done, q5 + 1)
                    wait(act, o_ready[1], q5)
                    act.activation(f1, proj_ps[1][:], ACT.Copy, scale=qv[:, a5, SDN, 1:2]).then_inc(f1_ready, 1)
                if on(q3):
                    for k in range(2):
                        act.wait_ge(qt_ready, 2 * q3 + 1 + k)
                        wait(act, up_done, q3)
                        act.activation(qT[:, k, :], xt_ps[k][:], ACT.Identity, bias=magicN[:]).then_inc(qt_copied, 1)
                if on(q2):
                    square(0)
                    square(1)
                    act.wait_ge(sq_done, q2 + 1)
                    act.activation(std[:, a2, :], sqsum[:, a2, :], ACT.Sqrt, bias=epsT[:], scale=1.0 / D).then_inc(std_ready, 1)
                if on(q4):
                    act.wait_ge(ht_ready, q4 + 1)
                    wait(act, dn_done, q4 - 1)
                    act.activation(hqT[:, a4 % 2, :], misc_ps[a4 % 2][0:F, 0:2 * P], ACT.Identity,
                                   bias=magicN[0:F, :]).then_inc(ht_copied, 1)
                if on(q3):
                    act.wait_ge(up_done, q3 + 1)
                    wait(act, h_ready, q3 - 1)
                    for k in range(2):
                        ins = act.activation(hid[:, a3 % 2, k, :], sc_ps[a3 % 2][:, k * F:(k + 1) * F], ACT.Relu,
                                             scale=qv[:, a3, SUP, k:k + 1])
                    ins.then_inc(relu_ready, 1)

            for s in range(2 * QS):
                step(s, s % QS)
            with act.Fori(2, NQ // QS - 1) as i:
                for m in range(QS):
                    step(QS * i + m, m)
            for s in range(NQ - QS, NQ + LAGS):
                step(s, s % QS)

        @block.tensor
        def _(pe):
            pe.wait_ge(consts_set, 4)

            def turn1(t, r, slot, loads):
                if r % 2 == 0:
                    pe.wait_ge(x_got1[slot], loads)
                wait(pe, lo1_done, t - GR + 1)
                for c in range(C):
                    mm = pe.transpose(xt_ps[r][:, c * P:(c + 1) * P], x_in[:, slot, r % 2, c * P:(c + 1) * P], identF[:])
                mm.then_inc(t1_done, 1)

            def group1(g, b, loads):
                for r in range(GR):
                    if not isinstance(g, int) or g + 1 < NG1:
                        turn1(GR * (g + 1) + r, r, 2 * (1 - b) + r // 2, loads)
                back = not isinstance(g, int) or 0 < g
                if back:
                    pe.wait_ge(s1_copied, g)
                    wait(pe, kept, g - 2)
                if not isinstance(g, int) or 0 <= g < NG1:
                    pe.wait_ge(hi1_done, GR * (g + 1))
                    pe.wait_ge(lo1_done, GR * (g + 1))
                    wait(pe, s1_copied, g - 1)
                    for k, part in enumerate((xThi, xTlo)):
                        for c in range(C):
                            mm = pe.matmul(sc_ps[b][0:4 * H, :], wparts[:, c, :], part[:, b, c, :],
                                           start=(k == 0 and c == 0), stop=(k == 1 and c == C - 1))
                    mm.then_inc(s1_done, 1)
                if back:
                    for r in range(GR):
                        mm = pe.matmul(misc_ps[1 - b][:, r * 2 * H:(r + 1) * 2 * H], s_sb[:, 1 - b, r * P:(r + 1) * P],
                                       fold2[:], start=True, stop=True)
                    mm.then_inc(back_done, 1)

            group1(-1, 1, 16)
            pe.wait_ge(wsum_ready, 1)
            for c in range(C):
                mm = pe.matmul(misc_ps[0][:, 0:2 * H], inv_d[:], wts[:, c, :], start=(c == 0), stop=(c == C - 1))
            mm.then_inc(wmean_ready, 1)
            pe.wait_ge(wts_ready, 1)
            group1(0, 0, 16)
            group1(1, 1, 32)
            with pe.Fori(1, NG1 // 2 - 1) as i:
                group1(2 * i, 0, 16 * i + 16)
                group1(2 * i + 1, 1, 16 * i + 32)
            group1(NG1 - 2, 0, 16 * (NG1 // 2))
            group1(NG1 - 1, 1, None)
            group1(NG1, 0, None)

            pe.wait_ge(aux_ready, 1)
            for k in range(2):
                mm = pe.matmul(misc_ps[0][:, k * P:(k + 1) * P], dB[:, k, :], identF[:], start=True, stop=True)
            mm.then_inc(aux_done, 1)
            pe.matmul(misc_ps[1][:, 0:1], inv_d[0:F, :], asum[0:F, 0:1], start=True, stop=True)
            pe.matmul(misc_ps[1][:, 1:2], inv_d[:], asum[:, 1:2], start=True, stop=True).then_inc(aux_done, 1)

            def turn2(t, r):
                pe.wait_ge(normed, t + 1)
                wait(pe, lo2_done, t - 1)
                for c in range(C):
                    mm = pe.transpose(xt_ps[r % 2][:, c * P:(c + 1) * P], xn[:, r % 2, c * P:(c + 1) * P], identF[:])
                mm.then_inc(t2_done, 1)

            def project(t, r):
                pe.wait_ge(hi2_done, t + 1)
                wait(pe, v_done, t - 1)
                ps = proj_ps[r % 2]
                for c in range(C):
                    hi = xThi[:, r % 2, c, 0:P]
                    pe.matmul(ps[:], hi, Whi[:, c, :], start=(c == 0), stop=False)
                    pe.matmul(ps[:], hi, Wlo[:, c, :], start=False, stop=False)
                pe.wait_ge(lo2_done, t + 1)
                for c in range(C):
                    pe.matmul(ps[:], xTlo[:, r % 2, c, 0:P], Whi[:, c, :], start=False, stop=False)
                pe.matmul(ps[:], onesB[0:3, :], brow[:], start=False, stop=True).then_inc(mm_done, 1)

            pe.wait_ge(aux_ready, 2)
            for c in range(C):
                pe.transpose(misc_ps[0][:].bitcast(BF16)[:, c * F:(c + 1) * F], up_t[:, c * P:(c + 1) * P], identB[0:F, 0:F])
            for c in range(C):
                mm = pe.transpose(misc_ps[1][:].bitcast(BF16)[0:F, c * P:(c + 1) * P], dn_t[:, c, :], identB[:])
            mm.then_inc(aux_done, 1)
            pe.wait_ge(brow_in, 48)
            pe.wait_ge(Wlo_ready, 1)
            turn2(0, 0)
            for t in range(GR):
                turn2(t + 1, (t + 1) % GR)
                project(t, t)
            with pe.Fori(1, NG - 1) as i:
                for r in range(GR):
                    t = GR * i + r
                    turn2(t + 1, (r + 1) % GR)
                    project(t, r)
            def early_cross():
                pe.wait_ge(mB_ready, 1)
                for h in range(H):
                    mm = pe.transpose(sc_ps[h // 4][:, (h % 4) * P:(h % 4 + 1) * P], mB[:, h, :], identF[:])
                mm.then_inc(aux_done, 1)

            for t in range(GR * (NG - 1), ET):
                if t + 1 < ET:
                    turn2(t + 1, (t + 1) % GR)
                project(t, t % GR)
                if t == GR * (NG - 1):
                    early_cross()

            pe.wait_ge(aux_ready, 3)
            pe.matmul(xt_ps[0][:], cmask[:], tailrow[:, 0:D], start=True, stop=True)
            pe.matmul(sc_ps[0][:, 0:H], cmask[:], tailrow[:, D:D + H], start=True, stop=True)
            pe.matmul(sc_ps[0][:, H:2 * H], shift[:], gm[:], start=True, stop=True).then_inc(aux_done, 1)
            pe.wait_ge(fix_ready, 1)
            pe.wait_ge(tern_ready, 2)

            def step(s, m):
                def on(q):
                    return not isinstance(q, int) or 0 <= q < NQ

                q, a = s - 3, (m - 3) % QS
                if on(q):
                    for k in range(2):
                        pe.wait_ge(qm_ready[k], q + 1)
                        wait(pe, qt_copied, 2 * q - 1 + k)
                        for c in range(C):
                            mm = pe.transpose(xt_ps[k][:, c * P:(c + 1) * P], qm_tile(a % 2, k)[:, c * P:(c + 1) * P], identF[:])
                        mm.then_inc(qt_ready, 1)
                    wait(pe, relu_ready, q - 1)
                    for k in range(2):
                        pe.wait_ge(qt_copied, 2 * q + 1 + k)
                        for c in range(C):
                            mm = pe.matmul(sc_ps[a % 2][:, k * F:(k + 1) * F], qT[:, k, c * P:(c + 1) * P], upT[:, c, :],
                                           start=(c == 0), stop=(c == C - 1))
                    mm.then_inc(up_done, 1)
                q, a = s - 4, (m - 4) % QS
                if on(q):
                    pe.wait_ge(h_ready, q + 1)
                    wait(pe, ht_copied, q - 1)
                    for k in range(2):
                        mm = pe.transpose(misc_ps[a % 2][:, k * P:(k + 1) * P], hq[:, a % 2, k, :], identF[:])
                    mm.then_inc(ht_ready, 1)
                    pe.wait_ge(ht_copied, q + 1)
                    wait(pe, o_ready[0], q)
                    wait(pe, f1_ready, q)
                    for k in range(2):
                        mm = pe.matmul(proj_ps[k][:], hqT[:, a % 2, k * P:(k + 1) * P], dnT[:], start=True, stop=True)
                    mm.then_inc(dn_done, 1)

            for s in range(2 * QS):
                step(s, s % QS)
            with pe.Fori(2, NQ // QS - 1) as i:
                for m in range(QS):
                    step(QS * i + m, m)
            for s in range(NQ - QS, NQ + LAGS):
                step(s, s % QS)

        @block.vector
        def _(ve):
            ch = Chain(ve, dve_chain)
            ve.memset(inv_d[:], 1.0 / D)
            ve.memset(onesB[:], 1.0)
            ve.memset(epsT[:], LN_EPS)
            ve.memset(magicN[:], -MAGIC)
            ve.memset(mrun[:], 0.0)
            ve.memset(den[:], 0.0)
            ve.memset(wc[:], 0.0)
            ve.memset(hq[:], 0.0)
            ch.mark(ve.memset(row[:, 1, GR - 1, :], 0.0))

            def tile1(g, t, b, r, slot, loads):
                if r % 2 == 0:
                    ve.wait_ge(x_got1[slot], loads)
                if r < GR - 1:
                    ve.bn_stats(bn_all[:, bass.ds(g, 1), r, :].rearrange("p o s -> p (o s)"), x_in[:, slot, r % 2, :]).then_inc(stats_done, 1)
                ve.wait_ge(hi1_done, t + 1)
                view = (slice(None), b, slice(None), slice(r * P, (r + 1) * P))
                ve.tensor_tensor(xTlo[view], xt_ps[r][:].rearrange("p (c n) -> p c n", c=C), xThi[view].bitcast(F32),
                                 ALU.subtract).then_inc(lo1_done, 1)

            def keep1(g, b):
                ve.wait_ge(back_done, g + 1)
                ve.tensor_copy(raw_s[:, bass.ds(GR * g, GR), :].rearrange("p t s -> p (t s)"),
                               misc_ps[b][:, 0:GR * 2 * H]).then_inc(kept, 1)

            def group1(g, b, loads):
                for r in range(GR):
                    if not isinstance(g, int) or g + 1 < NG1:
                        wait(ve, s1_done, g)
                        tile1(g + 1, GR * (g + 1) + r, 1 - b, r, 2 * (1 - b) + r // 2, loads)
                if not isinstance(g, int) or 0 < g:
                    keep1(g - 1, 1 - b)

            group1(-1, 1, 16)
            ve.wait_ge(idx_in, 16 * 5)
            ve.wait_ge(consts_set, 4)
            ch.mark(ve.tensor_copy(dst_f[:], dst_i[:]))
            by_group = (tab[:].rearrange("p (g s) -> p g s", s=GR) for tab in (dst_i, src_i))
            ch.mark(ve.tensor_scalar(gather_i[:, :, 0, :], next(by_group), float(N - 1), None, ALU.min))
            ch.mark(ve.tensor_copy(gather_i[:, :, 1, :], next(by_group)))
            ch.link(ve.tensor_tensor(same_next[:], dst_i[:], nxt_i[:], ALU.is_equal))
            ch.mark(ve.scalar_tensor_tensor(scat[:, :, 0], same_next[:], float(FAR), dst_f[:], ALU.mult, ALU.add))
            ve.tensor_copy(scat[:, :, 1], edge_no[:]).then_inc(scat_ready, 1)
            ch.mark(ve.memset(gcol[:, 0:1], -BIG))
            ch.link(ve.tensor_tensor(gcol[:, 1:ET], dst_f[:, 1:ET], dst_f[:, 0:ET - 1], ALU.is_equal))
            ve.tensor_scalar(gcol[:, 1:ET], gcol[:, 1:ET], 1.0, BIG, ALU.subtract, ALU.mult).then_inc(gcol_ready, 1)
            ch.mark(ve.tensor_copy(identB[:], identF[:]))
            ch.mark(ve.tensor_tensor(fold2[:], identF[0:4 * H, 0:2 * H], identF[0:4 * H, 2 * H:4 * H], ALU.add))
            ch.mark(ve.memset(last_sb[:, NT - 1:NT], P * ET))

            ve.wait_ge(aw_in, 16)
            for c in range(C):
                ve.wait_ge(W_in[c], 16)
                mark = ch.mark(ve.tensor_tensor(prod[:, c, :, :], Wsb[:, c, :, :], awb[:, :, 0:DH], ALU.mult))
                if c > 0:
                    ve.wait_ge(prod2_ready, c)
                    ch.mark(ve.tensor_reduce(wts[:, c - 1, H:2 * H], prod2[:, c - 1, :, :], AX.X, ALU.add))
                ch.need(mark)
                ch.mark(ve.tensor_reduce(wts[:, c, 0:H], prod[:, c, :, :], AX.X, ALU.add))
            ve.wait_ge(prod2_ready, C)
            ch.link(ve.tensor_reduce(wts[:, C - 1, H:2 * H], prod2[:, C - 1, :, :], AX.X, ALU.add))
            ve.sem_inc(wsum_ready, 1)
            ve.wait_ge(bias_in, 32)
            p0 = prod[:, 0, :, :]
            ch.link(ve.tensor_tensor(p0, awb[:, :, 0:DH], awb[:, :, DH:2 * DH], ALU.add))
            ch.link(ve.tensor_tensor(p0, p0, heads(wbb[:]), ALU.mult))
            ch.link(ve.tensor_reduce(const_s[:], p0, AX.X, ALU.add))
            ch.mark(ve.tensor_tensor(const_s[:], const_s[:], abb[:], ALU.add))
            ve.wait_ge(wmean_ready, 1)
            ch.link(ve.tensor_tensor(wts[:], wts[:], misc_ps[0][:, 0:2 * H].unsqueeze(1).to_broadcast([P, C, 2 * H]),
                                     ALU.subtract))
            ch.link(ve.tensor_copy(wparts[:, :, 0:2 * H], wts[:]))
            ve.tensor_tensor(wparts[:, :, 2 * H:4 * H], wts[:], wparts[:, :, 0:2 * H].bitcast(F32),
                             ALU.subtract).then_inc(wts_ready, 1)

            group1(0, 0, 16)
            group1(1, 1, 32)
            with ve.Fori(1, NG1 // 2 - 1) as i:
                group1(2 * i, 0, 16 * i + 16)
                group1(2 * i + 1, 1, 16 * i + 32)
            group1(NG1 - 2, 0, 16 * (NG1 // 2))
            ve.wait_ge(stats_done, (GR - 1) * NG1)
            ve.wait_ge(sq1_done, NT)
            by_dve = (slice(None), slice(None), slice(0, GR - 1))
            m_all, v_all, d_all = (tab[:].rearrange("p (g r) -> p g r", r=GR) for tab in (meanT, varT, difT))
            half_a, half_b = (bn_all[:, :, :, 3 * k + 1] for k in range(2))
            ch.mark(ve.tensor_tensor(m_all[by_dve], half_a, half_b, ALU.add))
            ch.mark(ve.tensor_tensor(d_all[by_dve], half_a, half_b, ALU.subtract))
            ch.link(ve.tensor_tensor(v_all[by_dve], bn_all[:, :, :, 2], bn_all[:, :, :, 5], ALU.add))
            ch.mark(ve.tensor_scalar(m_all[:, :, GR - 1], xsum[:], 2.0 / D, None, ALU.mult))
            ch.mark(ve.tensor_scalar(v_all[:, :, GR - 1], xsq[:], 1.0 / D, None, ALU.mult))
            ch.link(ve.scalar_tensor_tensor(d_all[by_dve], d_all[by_dve], 0.25, d_all[by_dve], ALU.mult, ALU.mult))
            ve.scalar_tensor_tensor(v_all[by_dve], v_all[by_dve], 1.0 / D, d_all[by_dve], ALU.mult, ALU.add).then_inc(var_ready, 1)
            ve.wait_ge(std1_ready, 1)
            ch.link(ve.reciprocal(rstdT[:], stdT[:]))
            ch.link(ve.tensor_tensor(stdT[:], rstdT[:], rstdT[:], ALU.mult))
            ch.link(ve.scalar_tensor_tensor(stdT[:], varT[:], LN_EPS, stdT[:], ALU.add, ALU.mult))
            ch.link(ve.tensor_scalar(stdT[:], stdT[:], -0.5, 1.5, ALU.mult, ALU.add))
            ch.link(ve.tensor_tensor(rstdT[:], rstdT[:], stdT[:], ALU.mult))

            def tables(lo, hi):
                tiles = (slice(None), slice(lo, hi))
                rb = rstdT[tiles].unsqueeze(2).to_broadcast([P, hi - lo, H])
                ch.mark(ve.scalar_tensor_tensor(src_tab[:, lo:hi, H], meanT[tiles], -0.5, rstdT[tiles], ALU.mult, ALU.mult))
                ch.mark(ve.tensor_copy(src_tab[:, lo:hi, H + 1], rstdT[tiles]))
                ch.link(ve.tensor_tensor(dst_tab[tiles], raw_s[:, lo:hi, 0:H], rb, ALU.mult))
                ch.mark(ve.tensor_tensor(dst_tab[tiles], dst_tab[tiles], const_s[:].unsqueeze(1).to_broadcast([P, hi - lo, H]), ALU.add))
                return ve.tensor_tensor(src_tab[:, lo:hi, 0:H], raw_s[:, lo:hi, H:2 * H], rb, ALU.mult)

            ve.wait_ge(kept, NG1 - 2)
            ch.mark(tables(0, NT - 2 * GR))
            group1(NG1 - 1, 1, None)
            group1(NG1, 0, None)
            ve.wait_ge(kept, NG1)
            tables(NT - 2 * GR, NT).then_inc(tables_ready, 1)

            first, last = dst_f[:, 0:1], dst_f[:, ET - 1:ET]
            ch.link(ve.tensor_scalar(headeq[:], dst_f[:], first, 0.0, ALU.is_equal, ALU.add, accum_out=headcnt[:]))
            ch.mark(ve.tensor_copy(fx[:, 0:1], edge_no[:, 0:1]))
            ch.mark(ve.tensor_tensor(fx[:, 1:2], prv_i[:], dst_i[:, 0:1], ALU.is_equal))
            ch.mark(ve.tensor_tensor(fx[:, 2:3], nxt_i[:, ET - 1:ET], dst_i[:, 0:1], ALU.not_equal))
            ch.link(ve.tensor_scalar(fx[:, 3:4], headcnt[:], ET - 0.5, None, ALU.is_lt))
            ch.link(ve.tensor_tensor(fx[:, 4:5], fx[:, 2:3], fx[:, 3:4], ALU.max))
            ch.link(ve.tensor_tensor(fx[:, 5:6], fx[:, 4:5], fx[:, 1:2], ALU.mult))
            ch.link(ve.tensor_scalar(fx[:, 5:6], fx[:, 5:6], 1.0, -float(FAR), ALU.subtract, ALU.mult))
            ch.link(ve.tensor_tensor(fx[:, 6:7], fx[:, 0:1], headcnt[:], ALU.add))
            ch.link(ve.scalar_tensor_tensor(fix_idx[:], fx[:, 6:7], 1.0, fx[:, 5:6], ALU.subtract, ALU.add))
            ch.mark(ve.tensor_copy(dB[:, 0, :], last.to_broadcast([P, P])))
            ch.mark(ve.tensor_copy(dB[:, 1, :], first.to_broadcast([P, P])))
            ve.wait_ge(ffw_in, 32)
            ch.mark(ve.tensor_reduce(asum[0:F, 0:1], up_sb[:], AX.X, ALU.add, apply_absolute_value=True))
            ch.link(ve.tensor_reduce(asum[:, 1:2], dn_sb[:].rearrange("p c f -> p (c f)"), AX.X, ALU.add, apply_absolute_value=True))
            ve.sem_inc(aux_ready, 1)
            ve.wait_ge(aux_done, 1)
            ch.link(ve.tensor_scalar(egate[:], misc_ps[0][:, 0:P], last, 1.0, ALU.is_equal, ALU.subtract))
            ch.mark(ve.tensor_scalar(egate[:], egate[:], BIG, None, ALU.mult))
            ch.mark(ve.scalar_tensor_tensor(cmask[:], misc_ps[0][:, P:2 * P], last, before[:], ALU.is_equal, ALU.mult))
            ve.wait_ge(aux_done, 2)
            ch.link(ve.tensor_scalar(wsc[:], misc_ps[1][:, 0:2], 1.0 / F, Q_EPS, ALU.mult, ALU.max))
            ch.mark(ve.tensor_scalar(whalf[:, 0, :], wsc[:], 0.5, None, ALU.mult))
            ch.mark(ve.tensor_scalar(qsc[:], wsc[:], 1.0 / QMAX, None, ALU.mult))
            ch.link(ve.tensor_scalar(whalf[:, 1, :], wsc[:], -0.5, None, ALU.mult))
            ch.link(ve.tensor_scalar(tern[0:F, :], up_sb[:], whalf[0:F, 1, 0:1], None, ALU.is_lt))
            ch.link(ve.scalar_tensor_tensor(up_t[:], up_sb[:], whalf[0:F, 0, 0:1], tern[0:F, :], ALU.is_gt, ALU.subtract))
            dn2, dt2 = dn_sb[:].rearrange("p c f -> p (c f)"), dn_t[:].rearrange("p c f -> p (c f)")
            ch.link(ve.tensor_scalar(tern[:, 0:C * F], dn2, whalf[:, 1, 1:2], None, ALU.is_lt))
            ch.link(ve.scalar_tensor_tensor(dt2, dn2, whalf[:, 0, 1:2], tern[:, 0:C * F], ALU.is_gt, ALU.subtract))
            ve.sem_inc(aux_ready, 1)

            def low2(t, r):
                ve.wait_ge(hi2_done, t + 1)
                wait(ve, mm_done, t - 1)
                view = (slice(None), r % 2, slice(None), slice(0, P))
                ve.tensor_tensor(xTlo[view], xt_ps[r % 2][:].rearrange("p (c n) -> p c n", c=C), xThi[view].bitcast(F32),
                                 ALU.subtract).then_inc(lo2_done, 1)

            def scores(G, turn, b):
                gate = gates[:, bass.ds(G, 1), :, :].rearrange("p o h s -> p (o h) s")
                s = score[:, b, :, 1:GR + 1]
                m = mrun[:, b, :, :]
                ve.wait_ge(src_got[b], 16 * GR * turn + 16 * GR)
                ve.wait_ge(dst_got[b], 16 * GR * turn + 16 * GR)
                ch.mark(ve.tensor_copy(score[:, b, :, 0], mrun[:, 1 - b, :, GR]))
                mark = ch.mark(ve.tensor_tensor(s, sdst[:, b, :, :].rearrange("p s h -> p h s"),
                                                ssrc[:, b, :, 0:H].rearrange("p s h -> p h s"), ALU.add))
                yield
                ch.need(mark)
                mark = ch.mark(ve.scalar_tensor_tensor(s, s, 0.2, s, ALU.mult, ALU.max))
                yield
                ch.need(mark)
                mark = ch.mark(ve.tensor_tensor_scan(m.rearrange("p h s -> p (h s)"), gate.rearrange("p h s -> p (h s)"),
                                                     score[:, b, :, :].rearrange("p h s -> p (h s)"), 0.0, ALU.add, ALU.max))
                yield
                ch.need(mark)
                ch.mark(ve.tensor_tensor(expin[:, b, 0, :, :], s, m[:, :, 1:GR + 1], ALU.subtract))
                mark = ch.mark(ve.tensor_tensor(expin[:, b, 1, :, :], m[:, :, 0:GR], gate[:, :, 1:GR + 1], ALU.add))
                yield
                ch.need(mark)
                ve.tensor_tensor(expin[:, b, 1, :, :], expin[:, b, 1, :, :], m[:, :, 1:GR + 1], ALU.subtract).then_inc(scored, 1)
                yield

            def weights(G, turn, b):
                w, c = wc[:, b, 0, :, :], wc[:, b, 1, :, :]
                ve.wait_ge(exped, G + 1)
                mark = ch.mark(ve.tensor_copy(w[:, :, 0], den[:, 1 - b, :, GR]))
                yield
                ch.need(mark)
                mark = ch.mark(ve.tensor_tensor_scan(den[:, b, :, :].rearrange("p h s -> p (h s)"), c.rearrange("p h s -> p (h s)"),
                                                     w.rearrange("p h s -> p (h s)"), 0.0, ALU.mult, ALU.add))
                yield
                wait(ve, rows_out[b], 16 * turn)
                ch.mark(ve.tensor_copy(row[:, b, :, D + H:RW].rearrange("p s h -> p h s"), mrun[:, b, :, 1:GR + 1]))
                ch.need(mark)
                ch.mark(ve.tensor_copy(row[:, b, :, D:D + H].rearrange("p s h -> p h s"), den[:, b, :, 1:GR + 1]))
                yield

            def fold(t, b, r, small, last):
                prev = row[:, b, r - 1, 0:D] if r > 0 else row[:, 1 - b, GR - 1, 0:D]
                if r >= GR - 2 and last:
                    ve.wait_ge(most_done, r - GR + 3)
                elif r > 0:
                    ch.need(fold.mark)
                ch.mark(ve.tensor_tensor(heads(carry[:, r % 2, :]), heads(prev), over(wc[:, b, 1, :, r + 1], DH), ALU.mult))
                next(small, None)
                ve.wait_ge(mm_done, t + 1)
                ve.tensor_tensor(heads(vbuf[:, r % 2, :]), heads(proj_ps[r % 2][:]), over(wc[:, b, 0, :, r + 1], DH), ALU.mult).then_inc(v_done, 1)
                if not last or r < GR - 2:
                    low2(t + 2, r)
                else:
                    next(small, None)
                next(small, None)
                ve.wait_ge(v_done, t + 1)
                ins = ve.tensor_tensor(row[:, b, r, 0:D], carry[:, r % 2, :], vbuf[:, r % 2, :], ALU.add)
                if r == GR - 1:
                    ins.then_inc(group_done, 1)
                elif r >= GR - 3 and last:
                    ins.then_inc(most_done, 1)
                else:
                    fold.mark = ch.mark(ins)
                    next(small, None)

            mlast, dlast = mrun[:, 1, :, GR], den[:, 1, :, GR]

            def early_cross():
                yield
                ve.wait_ge(aux_done, 4)
                for k in range(2):
                    v = mB[:, 4 * k:4 * k + 4, :]
                    mark = ch.mark(ve.tensor_tensor(v, sc_ps[k][:].rearrange("p (h q) -> p h q", h=4),
                                                    egate[:].unsqueeze(1).to_broadcast([P, 4, P]), ALU.add))
                    yield
                    ch.need(mark)
                    mark = ch.mark(ve.tensor_reduce(gm[:, 4 * k:4 * k + 4], v, AX.X, ALU.max))
                    yield
                ch.need(mark)
                ve.tensor_tensor(wq_in[:], mlast, gm[:], ALU.subtract).then_inc(cross_in, 1)
                yield

            def group(G, turn, b, last=False):
                small = early_cross() if last else scores(G + 1, turn + b, 1 - b)
                for r in range(GR):
                    if r == 2 and not last:
                        for _ in small:
                            pass
                        small = weights(G + 1, turn + b, 1 - b)
                    if r == 0 and (not isinstance(G, int) or G > 0):
                        ve.wait_ge(group_done, G)
                    plain = (r == 2 and not last) or (r == 0 and isinstance(G, int) and G == 0)
                    fold(G * GR + r, b, r, iter(()) if plain else small, last)
                for _ in small:
                    pass

            low2(0, 0)
            ve.wait_ge(gates_ready, 1)
            for part in (scores(0, 0, 0), weights(0, 0, 0)):
                for _ in part:
                    pass
            ch.need(ch.base + ch.n)
            low2(1, 1)
            group(0, 0, 0)
            group(1, 0, 1)
            with ve.Fori(1, NG // 2 - 1) as i:
                ch.enter(i - 1, 34)
                group(2 * i, i, 0)
                group(2 * i + 1, i, 1)
            ch.leave(NG // 2 - 2)
            group(NG - 2, NG // 2 - 1, 0)
            group(NG - 1, NG // 2 - 1, 1, last=True)

            ve.wait_ge(group_done, NG)
            ch.need(ch.base + ch.n)
            ve.wait_ge(cross_exp, 1)
            ch.mark(ve.tensor_tensor(heads(tailrow[:, 0:D]), heads(row[:, 1, GR - 1, 0:D]), over(wq[:], DH), ALU.mult))
            ch.link(ve.tensor_tensor(tailrow[:, D:D + H], dlast, wq[:], ALU.mult))
            ve.sem_inc(aux_ready, 1)
            ve.wait_ge(aux_done, 5)
            ve.wait_ge(fix_got, 16)
            gmax = sc_ps[0][:, H:2 * H]
            ch.link(ve.tensor_tensor(mtot[:], fixrow[:, D + H:RW], gmax, ALU.max))
            ch.mark(ve.tensor_tensor(ab_in[:, 0, :], fixrow[:, D + H:RW], mtot[:], ALU.subtract))
            ve.tensor_tensor(ab_in[:, 1, :], gmax, mtot[:], ALU.subtract).then_inc(cross_in, 1)
            ve.wait_ge(cross_exp, 2)
            fa = heads(fixrow[:, 0:D])
            ch.mark(ve.tensor_tensor(fa, fa, over(ab[:, 0, :], DH), ALU.mult))
            ch.mark(ve.tensor_tensor(heads(vbuf[:, 0, :]), heads(xt_ps[0][:]), over(ab[:, 1, :], DH), ALU.mult))
            ch.mark(ve.tensor_tensor(fixrow[:, D:D + H], fixrow[:, D:D + H], ab[:, 0, :], ALU.mult))
            ch.link(ve.tensor_tensor(cden[:], sc_ps[0][:, 0:H], ab[:, 1, :], ALU.mult))
            ch.mark(ve.tensor_tensor(fixrow[:, D:D + H], fixrow[:, D:D + H], cden[:], ALU.add))
            ch.link(ve.tensor_tensor(fixrow[:, 0:D], fixrow[:, 0:D], vbuf[:, 0, :], ALU.add))
            ve.sem_inc(fix_ready, 1)

            def step(s, m, turn):
                def on(q):
                    return not isinstance(q, int) or 0 <= q < NQ

                def val(a, k):
                    return qv[:, a, k, :]

                fin, hidden, scale, quant, resid, first = on(s - 5), on(s - 4), on(s - 3), on(s - 2), on(s - 1), on(s)
                a5, a4, a3, a2, a1, a0 = ((m - lag) % QS for lag in (5, 4, 3, 2, 1, 0))
                mk = {}

                h1 = hid2[:, a4 % 2, :, :]

                def resid_tile(k):
                    return ch.mark(ve.scalar_tensor_tensor(y_pair(a1)[:, k, :], x_in[:, a1, k, :], 1.0, rg_pair(a1)[:, k, 0:D],
                                                           ALU.mult, ALU.add, accum_out=ysum[:, a1, k:k + 1]))

                def amax(k):
                    ve.wait_ge(yc_ready, 2 * (s - 2) + 1 + k)
                    return ch.mark(ve.tensor_reduce(qv[:, a2, AMAX, k:k + 1], yc_tile(a2 % 2, k), AX.X, ALU.max,
                                                    apply_absolute_value=True))

                if first:
                    ve.wait_ge(rg_got[a0], 32 * turn(0) + 32)
                    mk["den"] = ch.mark(ve.tensor_scalar(rden[:, a0, :, :], rg_pair(a0)[:, :, D:D + H], 0.5, None, ALU.max))
                if hidden:
                    ve.wait_ge(relu_ready, s - 3)
                    ve.tensor_scalar(h1, hid[:, a4 % 2, :, :], QMAX, MAGIC, ALU.min, ALU.add).then_inc(h1_ready, 1)
                if scale:
                    ve.wait_ge(qs_ready, s - 2)
                    for k in range(2):
                        ve.tensor_scalar(qm_tile(a3 % 2, k), yc_tile(a3 % 2, k), qv[:, a3, QSC, k:k + 1], MAGIC,
                                         ALU.mult, ALU.add).then_inc(qm_ready[k], 1)
                if fin:
                    ve.wait_ge(dn_done, s - 4)
                    wait(ve, o_out[a5 % 2], 16 * ((s - 5) // 2) if isinstance(s, int) else 32 * turn.i + 16 * ((m - 5) // 2))
                    ve.scalar_tensor_tensor(o_tile(a5 % 2, 0), proj_ps[0][:], qv[:, a5, SDN, 0:1], y_pair(a5)[:, 0, :],
                                            ALU.mult, ALU.add).then_inc(o_ready[0], 1)
                if first:
                    ch.need(mk["den"])
                    ve.reciprocal(rden[:, a0, :, :], rden[:, a0, :, :]).then_inc(rden_ready, 1)
                if hidden:
                    ve.wait_ge(h1_ready, s - 3)
                    mk["a3"] = ch.mark(ve.tensor_reduce(val(a4, A3), h1, AX.X, ALU.max))
                if hidden:
                    ch.need(mk["a3"])
                    mk["a3"] = ch.mark(ve.tensor_scalar(val(a4, A3), val(a4, A3), MAGIC, Q_EPS, ALU.subtract, ALU.max))
                if quant:
                    amax(0)
                if hidden:
                    ch.need(mk["a3"])
                    mk["ia3"] = ch.mark(ve.reciprocal(val(a4, X2), val(a4, A3)))
                    ch.mark(ve.tensor_scalar(val(a4, SDN), val(a4, A3), qsc[:, 1:2], None, ALU.mult))
                    ch.need(mk["ia3"])
                    mk["x2"] = ch.mark(ve.tensor_scalar(val(a4, X2), val(a4, X2), QMAX, None, ALU.mult))
                if quant:
                    mk["amax"] = amax(1)
                if hidden:
                    ch.need(mk["x2"])
                    ve.wait_ge(h2_ready, s - 3)
                    wait(ve, ht_ready, s - 5)
                    for k in range(2):
                        ins = ve.tensor_scalar(hq[:, a4 % 2, k, 0:F], hid[:, a4 % 2, k, :], qv[:, a4, X2, k:k + 1], MAGIC, ALU.mult, ALU.add)
                    ins.then_inc(h_ready, 1)
                if resid:
                    ve.wait_ge(agg_ready, s)
                    ve.wait_ge(x_got4[a1], 16 * turn(1) + 16)
                    resid_tile(0)
                    wait(ve, o_ready[1], s - 4)
                    mk["ysum"] = resid_tile(1)
                if quant:
                    ve.wait_ge(std_ready, s - 1)
                    ch.mark(ve.reciprocal(val(a2, RSTD), std[:, a2, :]))
                    ch.need(mk["amax"])
                    mk["a2"] = ch.mark(ve.scalar_tensor_tensor(val(a2, AMAX), std[:, a2, :], Q_EPS, val(a2, AMAX), ALU.mult, ALU.max))
                if resid:
                    ch.need(mk["ysum"])
                    ve.tensor_scalar(negm[:, a1, :], ysum[:, a1, :], -1.0 / D, None, ALU.mult).then_inc(y_ready, 1)
                if quant:
                    ch.need(mk["a2"])
                    mk["ia2"] = ch.mark(ve.reciprocal(val(a2, IA2), val(a2, AMAX)))
                    ch.mark(ve.scalar_tensor_tensor(val(a2, SUP), val(a2, AMAX), qsc[:, 0:1], val(a2, RSTD), ALU.mult, ALU.mult))
                    ch.need(mk["ia2"])
                    ve.tensor_scalar(val(a2, QSC), val(a2, IA2), QMAX, None, ALU.mult).then_inc(qs_ready, 1)

            class Static:
                def __init__(self, s):
                    self.s = s

                def __call__(self, k):
                    return (self.s - k) // QS

            class Turn:
                def __init__(self, i, m):
                    self.i, self.m = i, m

                def __call__(self, k):
                    return self.i + (self.m - k) // QS

            for s in range(2 * QS):
                step(s, s % QS, Static(s))
            with ve.Fori(2, NQ // QS - 1) as i:
                ch.enter(i - 2, 14 * QS)
                for m in range(QS):
                    step(QS * i + m, m, Turn(i, m))
            ch.leave(NQ // QS - 3)
            for s in range(NQ - QS, NQ + LAGS):
                step(s, s % QS, Static(s))


_INS = ["x", "src", "dst", "L0_gnn_Ws", "L0_gnn_Wb", "L0_gnn_a_w", "L0_gnn_a_b", "L0_ffn_w_up", "L0_ffn_w_down"]


def kernel(**inputs):
    import numpy as np
    import concourse.bacc as bacc
    from concourse.bass_utils import run_bass_kernel_spmd

    nc = bacc.Bacc("TRN2", target_bir_lowering=False, num_devices=1)
    arrays, args = {}, []
    for name in _INS:
        a = np.ascontiguousarray(inputs[name])
        arrays[f"in_{name}"] = a
        args.append(nc.dram_tensor(f"in_{name}", a.shape, mybir.dt.from_np(a.dtype), kind="ExternalInput").ap())
    out = nc.dram_tensor("out", arrays["in_x"].shape, F32, kind="ExternalOutput").ap()
    build(nc, *args, out)
    return run_bass_kernel_spmd(nc, [arrays], core_ids=[0]).results[0]["out"]
```
